# Optimizing a Trainium2 kernel written in Bass

```python
import numpy as np
import jax
import jax.numpy as jnp

def _softmax(x, axis=-1):
    return jax.nn.softmax(x, axis=axis)

def _gelu(x):
    return jax.nn.gelu(x, approximate=True)

def _silu(x):
    return jax.nn.silu(x)

def _sigmoid(x):
    return jax.nn.sigmoid(x)

def _layernorm(x, axis=-1, eps=1e-05):
    m = jnp.mean(x, axis=axis, keepdims=True)
    v = jnp.var(x, axis=axis, keepdims=True)
    return (x - m) / jnp.sqrt(v + eps)

def _scatter_add(tgt, idx, src, axis=0):
    return tgt.at[idx].add(src)

def _segment_sum(src, seg, n):
    return jax.ops.segment_sum(src, seg, n)
kernel_name = 'mk_adj_resnorm_d4_adj_r2_f758de'

def setup_inputs(seed: int=0):
    np.random.seed(seed)
    _w = jnp.asarray

    def _rec_inputs():
        import jax
        import jax.numpy as jnp
        _gk = jax.random.key(seed)
        x = -0.0002928 + 1 * jax.random.normal(jax.random.fold_in(_gk, 1), (4096, 256), jnp.float32)
        _a = jax.random.bernoulli(jax.random.fold_in(_gk, 2), 0.000976562, (4096, 4096))
        _a = jnp.logical_or(_a, jnp.swapaxes(_a, -1, -2))
        _a = jnp.logical_or(_a, jnp.eye(4096, dtype=bool))
        _af = _a.astype(jnp.float32)
        _af = _af * jax.random.uniform(jax.random.fold_in(_gk, 3), (4096, 4096), jnp.float32, 0.05, 5.41998)
        adj = _af
        return (x, adj)
    x, adj = _rec_inputs()

    def _L0_gnn_setup():
        import jax, jax.numpy as jnp
        import numpy as np
        N = 4096
        D = 256
        EPS = 1e-12
        key = jax.random.key(seed)
        k1, k2 = jax.random.split(key)
        cur = jax.random.normal(k1, (N, D), dtype=jnp.float32)
        incidence_m = jax.random.normal(k2, (N, N), dtype=jnp.float32)
        return {'cur': cur, 'incidence_m': incidence_m}
    _L0_gnn_all = _L0_gnn_setup()
    _L0_gnn_in = {k: v for k, v in _L0_gnn_all.items() if k in ()}
    del _L0_gnn_all

    def _L1_gnn_setup():
        import jax, jax.numpy as jnp
        import numpy as np
        N = 4096
        D_IN = 256
        HEADS = 8
        DPH = 256 // HEADS
        EDGE_P = 0.01
        key = jax.random.key(seed)
        k1, k2, k3 = jax.random.split(key, 3)
        H = jax.random.normal(k1, (N, D_IN), dtype=jnp.float32)
        adj = (jax.random.uniform(k2, (N, N)) < EDGE_P).astype(jnp.float32)
        limit = float(np.sqrt(6.0 / (D_IN + DPH)))
        W = jax.random.uniform(k3, (HEADS, D_IN, DPH), jnp.float32, -limit, limit)
        b = jnp.zeros((HEADS, DPH), jnp.float32)
        return {'H': H, 'adj': adj, 'W': W, 'b': b}
    _L1_gnn_all = _L1_gnn_setup()
    _L1_gnn_in = {k: v for k, v in _L1_gnn_all.items() if k in ('W', 'b')}
    del _L1_gnn_all

    def _L2_gnn_setup():
        import jax, jax.numpy as jnp
        import numpy as np
        N, F, H = (1536, 256, 4)
        D = F // H
        ALPHA = 0.5
        EPS = 1e-06

        def _batchnorm(x, gamma, beta):
            m = jnp.mean(x, axis=0)
            v = jnp.var(x, axis=0)
            return (x - m) * jax.lax.rsqrt(v + EPS) * gamma + beta

        def _masked_softmax(scores, mask):
            s = jnp.where(mask, scores, -jnp.inf)
            att = jax.nn.softmax(s, axis=-1)
            return jnp.where(mask, att, 0.0)

        def _mlp_block(x, Wm, bm, g, b):
            h = jax.nn.elu(x @ Wm.T + bm) + x
            return _batchnorm(h, g, b)
        key = jax.random.key(seed)
        ks = jax.random.split(key, 12)
        X = jax.random.normal(ks[0], (N, F), dtype=jnp.float32)
        eye = jnp.eye(N, dtype=jnp.float32)
        local = (jax.random.uniform(ks[1], (N, N)) < 32.0 / N).astype(jnp.float32)
        local = jnp.clip(local + eye, 0.0, 1.0)
        longr = (jax.random.uniform(ks[2], (N, N)) < 16.0 / N).astype(jnp.float32)
        longr = jnp.clip(longr + eye, 0.0, 1.0)
        W = jax.random.normal(ks[3], (H, D, D), dtype=jnp.float32) * 0.1
        V = jax.random.normal(ks[4], (H, 2, D, 1), dtype=jnp.float32) * 0.1
        return {'X': X, 'local_pattern': local, 'long_range_pattern': longr, 'W': W, 'V': V, 'enc_bn_gamma': jnp.ones((F,), jnp.float32), 'enc_bn_beta': jnp.zeros((F,), jnp.float32), 'enc_mlp_W': jax.random.normal(ks[5], (F, F), dtype=jnp.float32) * 0.02, 'enc_mlp_b': jnp.zeros((F,), jnp.float32), 'enc_mlp_bn_gamma': jnp.ones((F,), jnp.float32), 'enc_mlp_bn_beta': jnp.zeros((F,), jnp.float32), 'dec_mlp_W': jax.random.normal(ks[6], (F, F), dtype=jnp.float32) * 0.02, 'dec_mlp_b': jnp.zeros((F,), jnp.float32), 'dec_mlp_bn_gamma': jnp.ones((F,), jnp.float32), 'dec_mlp_bn_beta': jnp.zeros((F,), jnp.float32)}
    _L2_gnn_all = _L2_gnn_setup()
    _L2_gnn_in = {k: v for k, v in _L2_gnn_all.items() if k in ('W', 'V', 'enc_bn_gamma', 'enc_bn_beta', 'enc_mlp_W', 'enc_mlp_b', 'enc_mlp_bn_gamma', 'enc_mlp_bn_beta', 'dec_mlp_W', 'dec_mlp_b', 'dec_mlp_bn_gamma', 'dec_mlp_bn_beta')}
    del _L2_gnn_all

    def _L3_gnn_setup():
        import jax, jax.numpy as jnp
        import numpy as np
        N = 2048
        DIM_IN = 256
        DIM_Q = 256
        DIM_K = 256
        N_GRAPHS = 32
        key = jax.random.key(seed)
        ks = jax.random.split(key, 9)
        x = jax.random.normal(ks[0], (N, DIM_IN), dtype=jnp.float32)
        b = jax.random.normal(ks[1], (N, N), dtype=jnp.float32)
        edge_encoding = jax.random.normal(ks[2], (N, N), dtype=jnp.float32)
        ptr = jnp.arange(N_GRAPHS + 1, dtype=jnp.int64) * (N // N_GRAPHS)
        s_in = 1.0 / np.sqrt(DIM_IN)
        Wq = jax.random.normal(ks[3], (DIM_Q, DIM_IN), dtype=jnp.float32) * s_in
        bq = jnp.zeros((DIM_Q,), dtype=jnp.float32)
        Wk = jax.random.normal(ks[4], (DIM_K, DIM_IN), dtype=jnp.float32) * s_in
        bk = jnp.zeros((DIM_K,), dtype=jnp.float32)
        Wv = jax.random.normal(ks[5], (DIM_K, DIM_IN), dtype=jnp.float32) * s_in
        bv = jnp.zeros((DIM_K,), dtype=jnp.float32)
        return {'x': x, 'b': b, 'edge_encoding': edge_encoding, 'ptr': ptr, 'Wq': Wq, 'bq': bq, 'Wk': Wk, 'bk': bk, 'Wv': Wv, 'bv': bv}
    _L3_gnn_all = _L3_gnn_setup()
    _L3_gnn_in = {k: v for k, v in _L3_gnn_all.items() if k in ('ptr', 'Wq', 'bq', 'Wk', 'bk', 'Wv', 'bv')}
    del _L3_gnn_all
    return {'x': x, 'adj': adj, 'L1_gnn_W': _L1_gnn_in['W'], 'L1_gnn_b': _L1_gnn_in['b'], 'L2_gnn_W': _L2_gnn_in['W'], 'L2_gnn_V': _L2_gnn_in['V'], 'L2_gnn_enc_bn_gamma': _L2_gnn_in['enc_bn_gamma'], 'L2_gnn_enc_bn_beta': _L2_gnn_in['enc_bn_beta'], 'L2_gnn_enc_mlp_W': _L2_gnn_in['enc_mlp_W'], 'L2_gnn_enc_mlp_b': _L2_gnn_in['enc_mlp_b'], 'L2_gnn_enc_mlp_bn_gamma': _L2_gnn_in['enc_mlp_bn_gamma'], 'L2_gnn_enc_mlp_bn_beta': _L2_gnn_in['enc_mlp_bn_beta'], 'L2_gnn_dec_mlp_W': _L2_gnn_in['dec_mlp_W'], 'L2_gnn_dec_mlp_b': _L2_gnn_in['dec_mlp_b'], 'L2_gnn_dec_mlp_bn_gamma': _L2_gnn_in['dec_mlp_bn_gamma'], 'L2_gnn_dec_mlp_bn_beta': _L2_gnn_in['dec_mlp_bn_beta'], 'L3_gnn_ptr': _L3_gnn_in['ptr'], 'L3_gnn_Wq': _L3_gnn_in['Wq'], 'L3_gnn_bq': _L3_gnn_in['bq'], 'L3_gnn_Wk': _L3_gnn_in['Wk'], 'L3_gnn_bk': _L3_gnn_in['bk'], 'L3_gnn_Wv': _L3_gnn_in['Wv'], 'L3_gnn_bv': _L3_gnn_in['bv']}

def reference(x, adj, L1_gnn_W, L1_gnn_b, L2_gnn_W, L2_gnn_V, L2_gnn_enc_bn_gamma, L2_gnn_enc_bn_beta, L2_gnn_enc_mlp_W, L2_gnn_enc_mlp_b, L2_gnn_enc_mlp_bn_gamma, L2_gnn_enc_mlp_bn_beta, L2_gnn_dec_mlp_W, L2_gnn_dec_mlp_b, L2_gnn_dec_mlp_bn_gamma, L2_gnn_dec_mlp_bn_beta, L3_gnn_ptr, L3_gnn_Wq, L3_gnn_bq, L3_gnn_Wk, L3_gnn_bk, L3_gnn_Wv, L3_gnn_bv):
    import jax
    import jax.numpy as jnp

    def _L0_gnn_ref(cur, incidence_m):
        import jax, jax.numpy as jnp
        import numpy as np
        N = 4096
        D = 256
        EPS = 1e-12
        mask = incidence_m > 0
        head = jax.lax.stop_gradient(mask.astype(incidence_m.dtype))
        head = head / jnp.maximum(jnp.sqrt(jnp.sum(head * head, axis=-1, keepdims=True)), EPS)
        inc = incidence_m + head
        edge_fea = inc @ cur
        edge_degree = jnp.sum(inc, axis=-1, keepdims=True)
        return edge_fea / edge_degree

    def _L1_gnn_ref(H, adj, W, b):
        import jax, jax.numpy as jnp
        import numpy as np
        N = 4096
        D_IN = 256
        HEADS = 8
        DPH = 256 // HEADS
        EDGE_P = 0.01
        H_ = jnp.einsum('nd,hde->hne', H, W)
        out = jnp.einsum('nm,hme->hne', adj, H_) + b[:, None, :]
        return jnp.transpose(out, (1, 0, 2)).reshape(H.shape[0], HEADS * DPH)

    def _L2_gnn_ref(X, local_pattern, long_range_pattern, W, V, enc_bn_gamma, enc_bn_beta, enc_mlp_W, enc_mlp_b, enc_mlp_bn_gamma, enc_mlp_bn_beta, dec_mlp_W, dec_mlp_b, dec_mlp_bn_gamma, dec_mlp_bn_beta):
        import jax, jax.numpy as jnp
        import numpy as np
        N, F, H = (1536, 256, 4)
        D = F // H
        ALPHA = 0.5
        EPS = 1e-06

        def _batchnorm(x, gamma, beta):
            m = jnp.mean(x, axis=0)
            v = jnp.var(x, axis=0)
            return (x - m) * jax.lax.rsqrt(v + EPS) * gamma + beta

        def _masked_softmax(scores, mask):
            s = jnp.where(mask, scores, -jnp.inf)
            att = jax.nn.softmax(s, axis=-1)
            return jnp.where(mask, att, 0.0)

        def _mlp_block(x, Wm, bm, g, b):
            h = jax.nn.elu(x @ Wm.T + bm) + x
            return _batchnorm(h, g, b)
        n = X.shape[0]
        Xh = X.reshape(n, H, D).transpose(1, 0, 2)
        Xw = jnp.einsum('hnd,hde->hne', Xh, W)
        f1 = jnp.einsum('hnd,hd->hn', Xw, V[:, 0, :, 0])
        f2 = jnp.einsum('hnd,hd->hn', Xw, V[:, 1, :, 0])
        sig = jax.nn.sigmoid(f1[:, :, None] + f2[:, None, :])
        lmask = (local_pattern != 0)[None]
        gmask = (long_range_pattern != 0)[None]
        local_att = _masked_softmax(local_pattern[None] * sig, lmask)
        long_att = _masked_softmax(long_range_pattern[None] * sig, gmask)
        att = ALPHA * long_att + (1.0 - ALPHA) * local_att
        Xa = jnp.einsum('hij,hjd->hid', att, Xw)
        Xc = Xa.transpose(1, 0, 2).reshape(n, F)
        Xn = _batchnorm(Xc, enc_bn_gamma, enc_bn_beta)
        emb = _mlp_block(Xn, enc_mlp_W, enc_mlp_b, enc_mlp_bn_gamma, enc_mlp_bn_beta)
        Yh = emb.reshape(n, H, D).transpose(1, 0, 2)
        Y = jnp.einsum('hij,hjd->hid', att, Yh)
        Y = jnp.einsum('hnd,hed->hne', Y, W)
        Yc = Y.transpose(1, 0, 2).reshape(n, F)
        Yc = jax.nn.elu(Yc)
        out = _mlp_block(Yc, dec_mlp_W, dec_mlp_b, dec_mlp_bn_gamma, dec_mlp_bn_beta)
        return out

    def _L3_gnn_ref(x, b, edge_encoding, ptr, Wq, bq, Wk, bk, Wv, bv):
        import jax, jax.numpy as jnp
        import numpy as np
        N = 2048
        DIM_IN = 256
        DIM_Q = 256
        DIM_K = 256
        N_GRAPHS = 32
        n = x.shape[0]
        graph_id = jnp.searchsorted(ptr, jnp.arange(n), side='right') - 1
        mask = graph_id[:, None] == graph_id[None, :]
        query = x @ Wq.T + bq
        key = x @ Wk.T + bk
        value = x @ Wv.T + bv
        scale = 1.0 / jnp.sqrt(jnp.float32(query.shape[-1]))
        a = jnp.where(mask, query @ key.T * scale, 0.0)
        scores = (a + b + edge_encoding) * jnp.where(mask, 1.0, -1000000.0)
        softmax = jax.nn.softmax(scores, axis=-1) * mask
        return softmax @ value
    x = _layernorm(x + _L0_gnn_ref(x, adj), axis=-1)
    x = _layernorm(x + _L1_gnn_ref(x, adj, L1_gnn_W, L1_gnn_b), axis=-1)
    x = _layernorm(x + _L2_gnn_ref(x, adj, adj, L2_gnn_W, L2_gnn_V, L2_gnn_enc_bn_gamma, L2_gnn_enc_bn_beta, L2_gnn_enc_mlp_W, L2_gnn_enc_mlp_b, L2_gnn_enc_mlp_bn_gamma, L2_gnn_enc_mlp_bn_beta, L2_gnn_dec_mlp_W, L2_gnn_dec_mlp_b, L2_gnn_dec_mlp_bn_gamma, L2_gnn_dec_mlp_bn_beta), axis=-1)
    x = _layernorm(x + _L3_gnn_ref(x, adj, adj, L3_gnn_ptr, L3_gnn_Wq, L3_gnn_bq, L3_gnn_Wk, L3_gnn_bk, L3_gnn_Wv, L3_gnn_bv), axis=-1)
    return x

_drawn_inputs = setup_inputs


def setup_inputs(seed=0):
    import zlib

    import numpy as np

    out = dict(_drawn_inputs(seed))
    spreads = {'L1_gnn_b': (0.0, 0.8),
     'L2_gnn_enc_bn_gamma': (1.0, 0.2),
     'L2_gnn_enc_bn_beta': (0.0, 2.0),
     'L2_gnn_enc_mlp_b': (0.0, 0.8),
     'L2_gnn_enc_mlp_bn_gamma': (1.0, 0.2),
     'L2_gnn_enc_mlp_bn_beta': (0.0, 0.549),
     'L2_gnn_dec_mlp_b': (0.0, 0.8),
     'L2_gnn_dec_mlp_bn_gamma': (1.0, 0.2),
     'L2_gnn_dec_mlp_bn_beta': (0.0, 0.1),
     'L3_gnn_bq': (0.0, 0.566),
     'L3_gnn_bk': (0.0, 0.8),
     'L3_gnn_bv': (0.0, 0.1)}
    factors = {}
    for name, (base, spread) in spreads.items():
        noise = np.random.default_rng([zlib.crc32(name.encode()), seed]).standard_normal(out[name].shape)
        drawn = base * np.exp(spread * noise) if base else spread * noise
        out[name] = jnp.asarray(drawn.astype(out[name].dtype))
    for name, factor in factors.items():
        out[name] = (out[name] * factor).astype(out[name].dtype)
    return out
```

```python
from contextlib import ExitStack

import concourse.bass as bass
from concourse import mybir

F32 = mybir.dt.float32
BF16 = mybir.dt.bfloat16
I32 = mybir.dt.int32
ALU = mybir.AluOpType
ACT = mybir.ActivationFunctionType
AX_X = mybir.AxisListType.X

P = 128
N = 4096
T = N // P
D = 256
KC = D // P
HEADS = 4
DH = D // HEADS
NPTR = 33
LN_EPS = 1e-5
BN_EPS = 1e-6
NORM_EPS = 1e-12
MASKED = -1.0e38
TANH_ONE = 1.0 + 2.0 ** -23
OFF_GRAPH = -1000000.0
BANK = 512
GROUP = 8
NG = T // GROUP
GW = GROUP * P
CH = N // BANK


class Steps:

    def __init__(self, eng, sem, per):
        self.eng, self.sem, self.per, self.k = eng, sem, per, per

    def tile(self, t):
        assert self.k == self.per, (self.k, self.per)
        self.base, self.k = t * self.per, 0

    def __call__(self, ins):
        self.k += 1
        ins.then_inc(self.sem, 1)
        self.eng.wait_ge(self.sem, self.base + self.k)


def early(t, n):
    return isinstance(t, int) and t < n


def late(t, n):
    return isinstance(t, int) and t >= T - n


def pairs(eng, tile):
    for q in (0,):
        tile(2 * q, 0, q)
        tile(2 * q + 1, 1, q)
    with eng.Fori(1, T // 2 - 1) as q:
        tile(2 * q, 0, q)
        tile(2 * q + 1, 1, q)
    for q in (T // 2 - 1,):
        tile(2 * q, 0, q)
        tile(2 * q + 1, 1, q)


def singles(eng, tile):
    tile(0)
    with eng.Fori(1, T - 1) as t:
        tile(t)
    tile(T - 1)


class Memory:

    def __init__(self, nc, ctx):
        self.nc, self.taken = nc, []
        sb = lambda name, shape, dt=F32: ctx.enter_context(nc.sbuf_tensor(name, shape, dt))
        self.arena = sb("arena", [P, 51328])
        self.ident = sb("ident", [P, P])
        self.ones_bf = sb("ones_bf", [P, P], BF16)
        self.eps = sb("eps", [P, 2])
        self.weights = sb("weights", [P, 1040])
        self.small = sb("small", [P, 384])
        self.params = sb("params", [P, 2 * 10])
        self.banks = ctx.enter_context(nc.psum_tensor("banks", [P, 8, BANK], F32))

    def at(self, start, *shape):
        n = 1
        for s in shape:
            n *= s
        v = self.arena[:, start:start + n]
        if len(shape) == 2:
            v = v.rearrange("p (a b) -> p a b", a=shape[0])
        if len(shape) == 3:
            v = v.rearrange("p (a b c) -> p a b c", a=shape[0], b=shape[1])
        return v

    def sem(self, name):
        self.taken.append(self.nc.alloc_semaphore(name))
        return self.taken[-1]

    def clear_semaphores(self):
        self.nc.clear_and_free_semaphores(self.taken)
        self.nc.all_engine_barrier()
        self.taken = []

    def sems(self, name, n):
        return [self.sem(f"{name}{i}") for i in range(n)]


def constants(nc, m, params):
    s_loaded = m.sem("c_loaded")
    s_ones = m.sem("c_ones")
    s_built = m.built = m.sem("c_built")
    with nc.Block() as block:
        @block.sync
        def _(sp):
            sp.dma_start(m.params[:], params).then_inc(s_loaded, 16)
            sp.wait_ge(s_loaded, 16)

        @block.vector
        def _(dve):
            nc.vector.memset(m.ident[:], 1.0).then_inc(s_ones, 1)
            nc.vector.memset(m.ones_bf[:], 1.0).then_inc(s_ones, 1)
            nc.vector.memset(m.eps[:, 0:1], LN_EPS).then_inc(s_ones, 1)
            nc.vector.memset(m.eps[:, 1:2], BN_EPS).then_inc(s_ones, 1)
            dve.wait_ge(s_ones, 4)

        @block.gpsimd
        def _(pool):
            pool.wait_ge(s_ones, 1)
            nc.gpsimd.affine_select(out=m.ident[:], in_=m.ident[:], compare_op=ALU.is_equal, fill=0.0,
                                    base=0, pattern=[[-1, P]], channel_multiplier=1).then_inc(s_built, 1)
            pool.wait_ge(s_built, 1)


class Post:

    def __init__(self, m, at, bank, name):
        self.m = m
        self.pre = m.at(at, D)
        self.xn = m.at(at + 256, D)
        self.xnT = m.at(at + 512, KC, P)
        self.stats = m.at(at + 768, 6)
        self.mv = m.at(at + 776, 2)
        self.sd = m.at(at + 780, 1)
        self.rs = m.at(at + 784, 1)
        self.spare = m.at(at + 788, 1)
        self.turned_bank = bank.rearrange("p (c n) -> p c n", c=KC)
        self.var_built = m.sem(name + "_var_built")
        self.sd_built = m.sem(name + "_sd_built")
        self.normalised = m.sem(name + "_normalised")
        self.turned = m.sem(name + "_turned")
        self.copied = m.sem(name + "_turned_copied")

    def normalise(self, nc, dve, steps, t, out=None, used=None):
        steps(nc.vector.bn_stats(self.stats, self.pre))
        nc.vector.memset(self.spare, 0.0)
        nc.vector.bn_aggr(self.mv, self.stats).then_inc(self.var_built, 1)
        dve.wait_ge(self.var_built, t + 1)
        dve.wait_ge(self.sd_built, t + 1)
        steps(nc.vector.reciprocal(self.rs, self.sd))
        if used is None and not early(t, 1):
            dve.wait_ge(self.turned, t)
        nc.vector.tensor_scalar(self.xn, self.pre, self.mv[:, 0:1], self.rs, ALU.subtract,
                                ALU.mult).then_inc(self.normalised, 1)

    def deviation(self, nc, act, t, eps):
        act.wait_ge(self.var_built, t + 1)
        nc.scalar.activation(self.sd, self.mv[:, 1:2], ACT.Sqrt, bias=eps).then_inc(self.sd_built, 1)

    def turn(self, nc, pe, t):
        pe.wait_ge(self.normalised, t + 1)
        if not early(t, 1):
            pe.wait_ge(self.copied, t)
        for c in range(KC):
            mm = nc.tensor.transpose(self.turned_bank[:, c, :], self.xn[:, c * P:(c + 1) * P], self.m.ident[:])
        mm.then_inc(self.turned, 1)

    def copy_turned(self, nc, act, t, used):
        act.wait_ge(self.turned, t + 1)
        if not early(t, 1):
            act.wait_ge(used, t)
        nc.scalar.copy(self.xnT, self.turned_bank).then_inc(self.copied, 1)


def layer0(nc, m, x, adjT_blocks, w1):
    x_in = m.at(0, T, D + 1)
    adj_in = [m.at(24704 + 4096 * b, T, P) for b in range(2)]
    inc = [m.at(32896 + 4096 * b, T, P) for b in range(2)]
    mask = m.arena[:, 41088:43136].bitcast(BF16).rearrange("p (t i) -> p t i", t=T)
    rnorm = m.at(43136, P)
    w = m.weights[:, 0:KC * D].rearrange("p (c n) -> p c n", c=KC)
    counts = m.banks[:, 0, 0:P]
    agg = [m.banks[:, 1 + b, 0:D + 1] for b in range(2)]
    proj = m.banks[:, 4, 0:D]
    post = Post(m, 43264, m.banks[:, 3, 0:D], "l0")
    rdeg = m.at(43264 + 1024, 1)

    adj_loaded = m.sems("l0_adj_loaded", 2)
    x_loaded = m.sem("l0_x_loaded")
    w_loaded = m.sem("l0_w_loaded")
    ones_set = m.sem("l0_ones_set")
    mask_built = m.sem("l0_mask_built")
    counted = m.sem("l0_counted")
    norm_built = m.sem("l0_norm_built")
    inc_built = m.sem("l0_inc_built")
    agg_done = m.sem("l0_agg_done")
    x1_kept = m.sem("l0_x1_kept")
    proj_done = m.sem("l0_proj_done")
    proj_copied = m.sem("l0_proj_copied")
    inc_step = m.sem("l0_inc_step")
    post_step = m.sem("l0_post_step")

    with nc.Block() as block:
        @block.sync
        def _(sp):
            def tile(t, b, q):
                if not early(t, 2):
                    sp.wait_ge(inc_built, t - 1)
                sp.dma_start(adj_in[b], adjT_blocks[t].rearrange("p (j i) -> p j i", j=T)).then_inc(
                    adj_loaded[b], 16)
                if early(t, 1):
                    sp.dma_start(x_in[:, :, 0:D], x.rearrange("(t p) d -> p t d", p=P)).then_inc(x_loaded, 16)
                    sp.dma_start(w, w1.rearrange("(c p) n -> p c n", p=P)).then_inc(w_loaded, 16)
            pairs(sp, tile)

        @block.vector
        def _(dve):
            inc_steps = Steps(dve, inc_step, 3)
            post_steps = Steps(dve, post_step, 4)

            def build_mask(t, b, q):
                dve.wait_ge(adj_loaded[b], 16 * (q + 1))
                if not early(t, 1):
                    dve.wait_ge(counted, t)
                nc.vector.tensor_scalar(mask, adj_in[b], 0.0, None, ALU.is_gt).then_inc(mask_built, 1)

            def build_inc(t, b):
                inc_steps.tile(t)
                dve.wait_ge(norm_built, t + 1)
                inc_steps(nc.vector.tensor_scalar(rnorm, rnorm, NORM_EPS, None, ALU.max))
                inc_steps(nc.vector.reciprocal(rnorm, rnorm))
                if not early(t, 2):
                    dve.wait_ge(agg_done, t - 1)
                rnorm_all = rnorm.unsqueeze(1).to_broadcast([P, T, P])
                inc_steps(nc.vector.scalar_tensor_tensor(inc[b], adj_in[b], 0.0, rnorm_all,
                                                         ALU.is_gt, ALU.mult))
                nc.vector.tensor_tensor(inc[b], inc[b], adj_in[b], ALU.add).then_inc(inc_built, 1)

            def finish(t, b):
                post_steps.tile(t)
                dve.wait_ge(agg_done, t + 1)
                post_steps(nc.vector.reciprocal(rdeg, agg[b][:, D:D + 1]))
                post_steps(nc.vector.scalar_tensor_tensor(post.pre, agg[b][:, 0:D], rdeg, x_in[:, t, 0:D],
                                                          ALU.mult, ALU.add))
                if not early(t, 1):
                    dve.wait_ge(x1_kept, t)
                post.normalise(nc, dve, post_steps, t)

            nc.vector.memset(x_in[:, :, D:D + 1], 1.0).then_inc(ones_set, 1)
            dve.wait_ge(x_loaded, 16)
            build_mask(0, 0, 0)
            build_inc(0, 0)
            build_mask(1, 1, 0)

            def tile(t, b, q):
                if not late(t, 1):
                    build_inc(t + 1, 1 - b)
                if not late(t, 2):
                    build_mask(t + 2, b, q + 1)
                if not early(t, 1):
                    finish(t - 1, 1 - b)
            pairs(dve, tile)
            finish(T - 1, 1)

        @block.scalar
        def _(act):
            def norm(t):
                act.wait_ge(counted, t + 1)
                if not early(t, 1):
                    act.wait_ge(inc_built, t)
                nc.scalar.activation(rnorm, counts, ACT.Sqrt).then_inc(norm_built, 1)

            def finish(t):
                post.deviation(nc, act, t, m.eps[:, 0:1])
                post.copy_turned(nc, act, t, proj_done)
                act.wait_ge(proj_done, t + 1)
                nc.scalar.copy(m.h[:, t, :], proj).then_inc(proj_copied, 1)

            norm(0)

            def tile(t, b, q):
                if not late(t, 1):
                    norm(t + 1)
                if not early(t, 1):
                    finish(t - 1)
            pairs(act, tile)
            finish(T - 1)
            act.wait_ge(proj_copied, T)

        @block.gpsimd
        def _(pool):
            def tile(t, b, q):
                pool.wait_ge(post.normalised, t + 1)
                nc.gpsimd.tensor_copy(m.x1[:, t, :], post.xn).then_inc(x1_kept, 1)
            pairs(pool, tile)
            pool.wait_ge(x1_kept, T)

        @block.tensor
        def _(pe):
            def count(t):
                pe.wait_ge(mask_built, t + 1)
                if not early(t, 1):
                    pe.wait_ge(norm_built, t)
                for j in range(T):
                    mm = nc.tensor.matmul(counts, m.ones_bf[:], mask[:, j, :], start=(j == 0), stop=(j == T - 1))
                mm.then_inc(counted, 1)

            def aggregate(t, b):
                pe.wait_ge(inc_built, t + 1)
                if not early(t, 2):
                    pe.wait_ge(post.normalised, t - 1)
                for j in range(T):
                    mm = nc.tensor.matmul(agg[b], inc[b][:, j, :], x_in[:, j, :],
                                          start=(j == 0), stop=(j == T - 1))
                mm.then_inc(agg_done, 1)

            def project(t):
                post.turn(nc, pe, t)
                if not early(t, 1):
                    pe.wait_ge(proj_copied, t)
                pe.wait_ge(post.copied, t + 1)
                for c in range(KC):
                    mm = nc.tensor.matmul(proj, post.xnT[:, c, :], w[:, c, :], start=(c == 0), stop=(c == KC - 1))
                mm.then_inc(proj_done, 1)

            pe.wait_ge(ones_set, 1)
            pe.wait_ge(x_loaded, 16)
            pe.wait_ge(w_loaded, 16)
            count(0)

            def tile(t, b, q):
                if not late(t, 1):
                    count(t + 1)
                aggregate(t, b)
                if not early(t, 1):
                    project(t - 1)
            pairs(pe, tile)
            project(T - 1)


def layer2_weights(nc, m, wbd, wbdT, vbd):
    wT = m.at(43264, KC, P)
    v = m.at(43520, KC, 4)
    prod = m.banks[:, 0, 0:KC * 4].rearrange("p (c k) -> p c k", c=KC)
    loaded = m.sem("lw_loaded")
    multiplied = m.sem("lw_multiplied")
    spread = m.sem("lw_spread")
    with nc.Block() as block:
        @block.sync
        def _(sp):
            sp.dma_start(m.wext[:, :, 0:P], wbd.rearrange("c p n -> p c n")).then_inc(loaded, 16)
            sp.dma_start(wT, wbdT.rearrange("c p n -> p c n")).then_inc(loaded, 16)
            sp.dma_start(v, vbd.rearrange("c p n -> p c n")).then_inc(loaded, 16)
            sp.wait_ge(loaded, 48)

        @block.tensor
        def _(pe):
            pe.wait_ge(loaded, 48)
            for c in range(KC):
                mm = nc.tensor.matmul(prod[:, c, :], wT[:, c, :], v[:, c, :], start=True, stop=True)
            mm.then_inc(multiplied, 1)

        @block.vector
        def _(dve):
            dve.wait_ge(multiplied, 1)
            dve.wait_ge(loaded, 48)
            nc.vector.tensor_copy(m.wext[:, :, P:P + 4], prod).then_inc(spread, 1)
            for h in range(HEADS):
                col = prod[:, h // 2, 2 + h % 2:3 + h % 2]
                nc.vector.tensor_copy(m.wv_rows[:, h, :], col.to_broadcast([P, P])).then_inc(spread, 1)
            dve.wait_ge(spread, 1 + HEADS)


def layer1(nc, m, adjT_blocks, b1, x2_dram):
    adj_in = [m.at(24704 + 4096 * b, T, P) for b in range(2)]
    bias = m.at(50400, D)
    agg = [m.banks[:, 1 + b, 0:D] for b in range(2)]
    proj = m.banks[:, 4, 0:KC * (P + 4)].rearrange("p (c k) -> p c k", c=KC)
    f2_rows = m.banks[:, 5, :].rearrange("p (h n) -> p h n", h=HEADS)
    post = Post(m, 49280, m.banks[:, 3, 0:D], "l1")

    adj_loaded = m.sems("l1_adj_loaded", 2)
    bias_loaded = m.sem("l1_bias_loaded")
    agg_done = m.sem("l1_agg_done")
    x2_stored = m.sem("l1_x2_stored")
    proj_done = m.sem("l1_proj_done")
    proj_copied = m.sem("l1_proj_copied")
    post_step = m.sem("l1_post_step")

    with nc.Block() as block:
        @block.sync
        def _(sp):
            sp.dma_start(bias, b1.partition_broadcast(P)).then_inc(bias_loaded, 16)

            def tile(t, b, q):
                if not early(t, 2):
                    sp.wait_ge(agg_done, t - 1)
                sp.dma_start(adj_in[b], adjT_blocks[t].rearrange("p (j i) -> p j i", j=T)).then_inc(
                    adj_loaded[b], 16)
            pairs(sp, tile)

        @block.vector
        def _(dve):
            post_steps = Steps(dve, post_step, 4)
            dve.wait_ge(bias_loaded, 16)

            def tile(t, b, q):
                post_steps.tile(t)
                dve.wait_ge(agg_done, t + 1)
                if not early(t, 1):
                    dve.wait_ge(post.normalised, t)
                post_steps(nc.vector.tensor_tensor(post.pre, agg[b], bias, ALU.add))
                post_steps(nc.vector.tensor_tensor(post.pre, post.pre, m.x1[:, t, :], ALU.add))
                if not early(t, 1):
                    dve.wait_ge(x2_stored, 16 * t)
                post.normalise(nc, dve, post_steps, t)
            pairs(dve, tile)

        @block.scalar
        def _(act):
            def tile(t, b, q):
                post.deviation(nc, act, t, m.eps[:, 0:1])
                act.wait_ge(post.normalised, t + 1)
                act.dma_start(x2_dram[t], post.xn).then_inc(x2_stored, 16)
                post.copy_turned(nc, act, t, proj_done)
                act.wait_ge(proj_done, t + 1)
                nc.scalar.copy(m.feats[:, t, :].rearrange("p (c n) -> p c n", c=KC), proj[:, :, 0:P])
                nc.scalar.mul(m.f1[:, t, :].rearrange("p (c n) -> p c n", c=KC), proj[:, :, P:P + 2], 0.5)
                nc.scalar.copy(m.f2.rearrange("p h (t n) -> p h t n", t=T)[:, :, t, :], f2_rows).then_inc(
                    proj_copied, 1)
            pairs(act, tile)
            act.wait_ge(proj_copied, T)
            act.wait_ge(x2_stored, 16 * T)

        @block.tensor
        def _(pe):
            def aggregate(t, b, q):
                pe.wait_ge(adj_loaded[b], 16 * (q + 1))
                if not early(t, 2):
                    pe.wait_ge(post.normalised, t - 1)
                for j in range(T):
                    mm = nc.tensor.matmul(agg[b], adj_in[b][:, j, :], m.h[:, j, :],
                                          start=(j == 0), stop=(j == T - 1))
                mm.then_inc(agg_done, 1)

            def project(t):
                post.turn(nc, pe, t)
                if not early(t, 1):
                    pe.wait_ge(proj_copied, t)
                pe.wait_ge(post.copied, t + 1)
                for c in range(KC):
                    nc.tensor.matmul(proj[:, c, :], post.xnT[:, c, :], m.wext[:, c, :], start=True, stop=True)
                for h in range(HEADS):
                    mm = nc.tensor.matmul(f2_rows[:, h, :], m.wv_rows[:, h, :], post.xnT[:, h // 2, :],
                                          start=True, stop=True)
                mm.then_inc(proj_done, 1)

            def tile(t, b, q):
                aggregate(t, b, q)
                if not early(t, 1):
                    project(t - 1)
            pairs(pe, tile)
            project(T - 1)


def attention(nc, m, adj, out_dram, name, first):
    e = [m.at(8320 + 4096 * h, N) for h in range(HEADS)]
    adj_raw = m.at(24704, N)
    adj_masked = m.at(28800, N)
    eT = [m.at(49280 + GW * i, GROUP, P) for i in range(2)]
    turned = [m.banks[:, 0:2, :], m.banks[:, 2:4, :], m.banks[:, 4:6, :], m.banks[:, 2:4, :]]
    turned = [x.rearrange("p a (b i) -> p (a b) i", i=P) for x in turned]
    on_vector = (0,) if first else (0, 2)
    agg = [m.banks[:, 6 + h % 2, DH * (h // 2):DH * (h // 2) + DH] for h in range(HEADS)]
    xc = m.weights[:, 0:D]
    den = m.weights[:, D:D + 1]
    top = m.weights[:, D + 2:D + 3]

    raw_loaded = m.sem(name + "_raw_loaded")
    masked = m.sem(name + "_masked")
    tanh_done = m.sem(name + "_tanh_done")
    scored = m.sem(name + "_scored")
    exp_done = m.sem(name + "_exp_done")
    turn_done = m.sems(name + "_turn_done", NG)
    copied = m.sems(name + "_copied", NG)
    used = m.sems(name + "_used", NG)
    agg_read = m.sem(name + "_agg_read")
    stored = m.sem(name + "_stored")
    mask_step = m.sem(name + "_mask_step")
    top_found = m.sem(name + "_top_found")
    max_step = m.sem(name + "_max_step")
    finish_step = m.sem(name + "_finish_step")

    def unit(t, h):
        return t + h // HEADS, h % HEADS

    def exists(t, h):
        return not (isinstance(t, int) and (t < 0 or t >= T))

    def copy_out(nc, eng, copy, t, h, g):
        eng.wait_ge(turn_done[g], HEADS * t + h + 1)
        if g < 2:
            if not (early(t, 1) and h == 0):
                eng.wait_ge(used[g + 2], HEADS * t + h)
        else:
            eng.wait_ge(used[g - 2], HEADS * t + h + 1)
        copy(eT[g % 2], turned[g]).then_inc(copied[g], 1)

    with nc.Block() as block:
        @block.sync
        def _(sp):
            sp.dma_start(adj_raw, adj[0]).then_inc(raw_loaded, 16)

            def tile(t):
                if not late(t, 1):
                    sp.wait_ge(masked, t + 1)
                    sp.dma_start(adj_raw, adj[t + 1]).then_inc(raw_loaded, 16)
                if not early(t, 1):
                    sp.wait_ge(agg_read, HEADS * t)
                    sp.dma_start(out_dram[t - 1], xc).then_inc(stored, 16)
            singles(sp, tile)
            sp.wait_ge(agg_read, HEADS * T)
            sp.dma_start(out_dram[T - 1], xc).then_inc(stored, 16)
            sp.wait_ge(stored, 16 * T)

        @block.vector
        def _(dve):
            mask_steps = Steps(dve, mask_step, 1)
            max_steps = Steps(dve, max_step, 1)
            finish_steps = Steps(dve, finish_step, 2)

            def mask(t):
                mask_steps.tile(t)
                dve.wait_ge(raw_loaded, 16 * (t + 1))
                if not early(t, 1):
                    dve.wait_ge(scored, HEADS * t)
                mask_steps(nc.vector.tensor_scalar(adj_masked, adj_raw, 0.0, MASKED, ALU.is_equal, ALU.mult))
                nc.vector.tensor_tensor(adj_masked, adj_masked, adj_raw, ALU.add).then_inc(masked, 1)
                dve.wait_ge(masked, t + 1)

            def score(t, h):
                if first:
                    max_steps.tile(HEADS * t + h)
                dve.wait_ge(tanh_done, HEADS * t + h + 1)
                op = nc.vector.scalar_tensor_tensor(e[h], e[h], TANH_ONE, adj_masked, ALU.add, ALU.mult)
                if first:
                    if not (early(t, 1) and h == 0):
                        dve.wait_ge(scored, HEADS * t + h)
                    max_steps(op)
                    nc.vector.tensor_reduce(top, e[h], AX_X, ALU.max).then_inc(top_found, 1)
                    dve.wait_ge(top_found, HEADS * t + h + 1)
                    op = nc.vector.tensor_scalar(m.neg_top[:, t, h:h + 1], top, -0.5, -MASKED * 1e-8,
                                                 ALU.mult, ALU.min)
                op.then_inc(scored, 1)

            def finish(t, h):
                finish_steps.tile(HEADS * t + h)
                dve.wait_ge(exp_done, HEADS * t + h + 1)
                if not (early(t, 1) and h == 0):
                    dve.wait_ge(agg_read, HEADS * t + h)
                finish_steps(nc.vector.tensor_scalar(den, m.row_sum[:, t, h:h + 1], 1e-30, None, ALU.max))
                finish_steps(nc.vector.reciprocal(den, den))
                dve.wait_ge(used[NG - 1], HEADS * t + h + 1)
                if h == 0 and not early(t, 1):
                    dve.wait_ge(stored, 16 * t)
                nc.vector.tensor_scalar(xc[:, DH * h:DH * h + DH], agg[h], den, None,
                                        ALU.mult).then_inc(agg_read, 1)

            def copy(g, t, h):
                if g in on_vector and exists(t, h):
                    copy_out(nc, dve, nc.vector.tensor_copy, t, h, g)

            mask(0)
            score(0, 0)

            def tile(t):
                for h in range(HEADS):
                    before, two_before, ahead = unit(t, h - 1), unit(t, h - 2), unit(t, h + 1)
                    if exists(*two_before):
                        finish(*two_before)
                    copy(0, *before)
                    if exists(*ahead):
                        if ahead[1] == 0:
                            mask(ahead[0])
                        score(*ahead)
                    copy(2, *before)
            singles(dve, tile)
            finish(T - 1, 2)
            copy(0, T - 1, 3)
            copy(2, T - 1, 3)
            finish(T - 1, 3)

        @block.scalar
        def _(act):
            def tanh(t, h):
                if not early(t, 1):
                    act.wait_ge(turn_done[NG - 1], HEADS * (t - 1) + h + 1)
                nc.scalar.activation(e[h], m.f2[:, h, :], ACT.Tanh, bias=m.f1[:, t, h:h + 1],
                                     scale=0.5).then_inc(tanh_done, 1)

            def exp(t, h):
                act.wait_ge(scored, HEADS * t + h + 1)
                nc.scalar.activation(e[h], e[h], ACT.Exp, bias=m.neg_top[:, t, h:h + 1], scale=0.5,
                                     accum_out=m.row_sum[:, t, h:h + 1]).then_inc(exp_done, 1)

            def copy(g, t, h):
                if g not in on_vector and exists(t, h):
                    copy_out(nc, act, nc.scalar.copy, t, h, g)

            tanh(0, 0)
            tanh(0, 1)

            def tile(t):
                for h in range(HEADS):
                    before, ahead = unit(t, h - 1), unit(t, h + 2)
                    copy(1, *before)
                    copy(2, *before)
                    if exists(*ahead):
                        tanh(*ahead)
                    copy(3, *before)
                    exp(t, h)
            singles(act, tile)
            for g in range(NG):
                copy(g, T - 1, 3)

        @block.tensor
        def _(pe):
            def turn(t, h, g):
                if g == 0:
                    pe.wait_ge(exp_done, HEADS * t + h + 1)
                if g == 3:
                    pe.wait_ge(copied[1], HEADS * t + h + 1)
                elif not (early(t, 1) and h == 0):
                    pe.wait_ge(copied[3 if g == 1 else g], HEADS * t + h)
                for k in range(GROUP):
                    j = GROUP * g + k
                    mm = nc.tensor.transpose(turned[g][:, k, :], e[h][:, P * j:P * j + P], m.ident[:])
                mm.then_inc(turn_done[g], 1)

            def aggregate(t, h, g):
                if g == 0 and not (early(t, 1) and h < 2):
                    pe.wait_ge(agg_read, HEADS * t + h - 1)
                pe.wait_ge(copied[g], HEADS * t + h + 1)
                for k in range(GROUP):
                    j = GROUP * g + k
                    mm = nc.tensor.matmul(agg[h], eT[g % 2][:, k, :], m.feats[:, j, DH * h:DH * h + DH],
                                          start=(j == 0), stop=(j == T - 1))
                mm.then_inc(used[g], 1)

            def tile(t):
                for h in range(HEADS):
                    turn(t, h, 0)
                    turn(t, h, 1)
                    turn(t, h, 2)
                    aggregate(t, h, 0)
                    turn(t, h, 3)
                    aggregate(t, h, 1)
                    aggregate(t, h, 2)
                    aggregate(t, h, 3)
            singles(pe, tile)


def turn_nodes(nc, m, name, src, dst, to_rows, load=None, extra=None):
    PER = BANK // P
    STEPS = KC * T // PER
    bank = [m.banks[:, i, :].rearrange("p (k i) -> p k i", k=PER) for i in range(8)]
    loaded = m.sems(name + "_loaded", 4)
    extra_loaded = m.sem(name + "_extra_loaded")
    turned = m.sem(name + "_turned")
    copied = m.sems(name + "_copied", 2)
    QT = T // 4

    def blocks(k):
        if to_rows:
            t = k * PER // KC
            return [(t + i // KC, i % KC) for i in range(PER)], dst[:, t:t + PER // KC, :].rearrange(
                "p t (c i) -> p (t c) i", c=KC)
        t, c = PER * (k // KC), k % KC
        return [(t + i, c) for i in range(PER)], dst[:, c, P * t:P * (t + PER)].rearrange(
            "p (k i) -> p k i", k=PER)

    with nc.Block() as block:
        @block.sync
        def _(sp):
            if load is not None:
                for i in range(4):
                    sp.dma_start(load[1][:, QT * i:QT * (i + 1), :],
                                 load[0][QT * i:QT * (i + 1)].rearrange("t p d -> p t d")).then_inc(loaded[i], 16)
            if extra is not None:
                sp.dma_start(extra[1], extra[0].rearrange("t p d -> p t d")).then_inc(extra_loaded, 16)
                sp.wait_ge(extra_loaded, 16)

        @block.tensor
        def _(pe):
            for k in range(STEPS):
                where, _ = blocks(k)
                if load is not None and k % (STEPS // 4) == 0:
                    pe.wait_ge(loaded[k // (STEPS // 4)], 16)
                if k >= 8:
                    pe.wait_ge(copied[k % 2], (k - 8) // 2 + 1)
                for i, (t, c) in enumerate(where):
                    block_in = src[:, c, P * t:P * t + P] if to_rows else src[:, t, P * c:P * c + P]
                    mm = nc.tensor.transpose(bank[k % 8][:, i, :], block_in, m.ident[:])
                mm.then_inc(turned, 1)

        @block.vector
        def _(dve):
            for k in range(0, STEPS, 2):
                dve.wait_ge(turned, k + 1)
                nc.vector.tensor_copy(blocks(k)[1], bank[k % 8]).then_inc(copied[0], 1)
            dve.wait_ge(copied[0], STEPS // 2)

        @block.scalar
        def _(act):
            for k in range(1, STEPS, 2):
                act.wait_ge(turned, k + 1)
                nc.scalar.copy(blocks(k)[1], bank[k % 8]).then_inc(copied[1], 1)
            act.wait_ge(copied[1], STEPS // 2)


def batch_norm(nc, m, name, data, gamma, beta):
    stats = m.weights[:, 0:KC * CH * 6].rearrange("p (c n k) -> p c n k", c=KC, n=CH)
    mv = m.weights[:, 100:100 + 2 * KC].rearrange("p (c k) -> p c k", c=KC)
    sd = m.weights[:, 110:110 + KC]
    scale = m.weights[:, 112:112 + KC]
    shift = m.weights[:, 114:114 + KC]
    measured = m.sem(name + "_measured")
    var_built = m.sem(name + "_var_built")
    sd_built = m.sem(name + "_sd_built")
    affine = m.sem(name + "_affine")
    applied = m.sem(name + "_applied")
    with nc.Block() as block:
        @block.vector
        def _(dve):
            for c in range(KC):
                for n in range(CH):
                    nc.vector.bn_stats(stats[:, c, n, :], data[:, c, BANK * n:BANK * (n + 1)]).then_inc(measured, 1)
            dve.wait_ge(measured, KC * CH)
            for c in range(KC):
                nc.vector.bn_aggr(mv[:, c, :], stats[:, c, :, :].rearrange("p n k -> p (n k)")).then_inc(
                    var_built, 1)
            dve.wait_ge(sd_built, 1)
            nc.vector.reciprocal(sd, sd).then_inc(affine, 1)
            dve.wait_ge(affine, 1)
            nc.vector.tensor_tensor(scale, sd, gamma, ALU.mult).then_inc(affine, 1)
            dve.wait_ge(affine, 2)
            dve.wait_ge(var_built, KC)
            nc.vector.tensor_tensor(shift, mv[:, :, 0], scale, ALU.mult).then_inc(affine, 1)
            dve.wait_ge(affine, 3)
            nc.vector.tensor_tensor(shift, beta, shift, ALU.subtract).then_inc(affine, 1)
            dve.wait_ge(affine, 4)
            nc.vector.tensor_scalar(data[:, 0, :], data[:, 0, :], scale[:, 0:1], shift[:, 0:1], ALU.mult,
                                    ALU.add).then_inc(applied, 1)

        @block.scalar
        def _(act):
            act.wait_ge(var_built, KC)
            nc.scalar.activation(sd, mv[:, :, 1], ACT.Sqrt, bias=m.eps[:, 1:2]).then_inc(sd_built, 1)
            act.wait_ge(affine, 4)
            nc.scalar.activation(data[:, 1, :], data[:, 1, :], ACT.Identity, bias=shift[:, 1:2],
                                 scale=scale[:, 1:2]).then_inc(applied, 1)
            act.wait_ge(applied, 2)


def dense(nc, m, name, src, dst, w_dram, bias, elu=False, residual=False, block_diagonal=False,
          scale=None, at=41088):
    w = m.weights[:, 0:KC * D].rearrange("p (c n) -> p c n", c=KC)
    low = [m.at(at + BANK * i, BANK) for i in range(2)]
    high = [m.at(at + 1024 + BANK * i, BANK) for i in range(2)]
    loaded = m.sem(name + "_loaded")
    multiplied = m.sem(name + "_multiplied")
    low_built = m.sem(name + "_low_built")
    low_exp = m.sem(name + "_low_exp")
    high_built = m.sem(name + "_high_built")
    joined = m.sem(name + "_joined")
    done = m.sem(name + "_done")
    steps = [(k // CH, slice(BANK * (k % CH), BANK * (k % CH + 1))) for k in range(KC * CH)]

    with nc.Block() as block:
        @block.sync
        def _(sp):
            sp.dma_start(w, w_dram.rearrange("c p n -> p c n")).then_inc(loaded, 16)

        @block.tensor
        def _(pe):
            pe.wait_ge(loaded, 16)
            for k, (o, nodes) in enumerate(steps):
                if k >= 4:
                    pe.wait_ge(high_built if elu else done, k - 3)
                chunks = [o] if block_diagonal else list(range(KC))
                for c in chunks:
                    mm = nc.tensor.matmul(m.banks[:, k % 4, :], w[:, c, P * o:P * o + P], src[:, c, nodes],
                                          start=(c == chunks[0]), stop=(c == chunks[-1]))
                mm.then_inc(multiplied, 1)

        @block.vector
        def _(dve):
            if elu:
                def join(k):
                    o, nodes = steps[k]
                    dve.wait_ge(low_exp, k + 1)
                    dve.wait_ge(high_built, k + 1)
                    to = high[k % 2] if residual else dst[:, o, nodes]
                    nc.vector.scalar_tensor_tensor(to, low[k % 2], -1.0, high[k % 2], ALU.add,
                                                   ALU.add).then_inc(joined, 1)
                    if residual:
                        dve.wait_ge(joined, k + 1)
                        nc.vector.tensor_tensor(dst[:, o, nodes], high[k % 2], src[:, o, nodes],
                                                ALU.add).then_inc(done, 1)

                for k, (o, nodes) in enumerate(steps):
                    dve.wait_ge(multiplied, k + 1)
                    if k >= 2:
                        dve.wait_ge(joined, k - 1)
                    b = 0.0 if bias is None else bias[:, o:o + 1]
                    nc.vector.tensor_scalar(low[k % 2], m.banks[:, k % 4, :], b, 0.0, ALU.add,
                                            ALU.min).then_inc(low_built, 1)
                    if k >= 1:
                        join(k - 1)
                join(len(steps) - 1)
                dve.wait_ge(done if residual else joined, len(steps))
            else:
                for k, (o, nodes) in enumerate(steps):
                    dve.wait_ge(multiplied, k + 1)
                    nc.vector.tensor_scalar(dst[:, o, nodes], m.banks[:, k % 4, :], bias[:, o:o + 1],
                                            1.0 if scale is None else scale, ALU.add, ALU.mult).then_inc(done, 1)
                dve.wait_ge(done, len(steps))

        @block.scalar
        def _(act):
            if elu:
                for k, (o, nodes) in enumerate(steps):
                    act.wait_ge(low_built, k + 1)
                    if k >= 2:
                        act.wait_ge(done if residual else joined, k - 1)
                    b = 0.0 if bias is None else bias[:, o:o + 1]
                    nc.scalar.activation(high[k % 2], m.banks[:, k % 4, :], ACT.Relu, bias=b).then_inc(
                        high_built, 1)
                    nc.scalar.activation(low[k % 2], low[k % 2], ACT.Exp).then_inc(low_exp, 1)
                act.wait_ge(low_exp, len(steps))


def layer_norm_rows(nc, m, rows, residual, x3_dram):
    stats = m.at(0, T, 6)
    mv = m.at(256, T, 2)
    sd = m.at(384, T)
    measured = m.sem("n3_measured")
    added = m.sem("n3_added")
    var_built = m.sem("n3_var_built")
    sd_built = m.sem("n3_sd_built")
    rs_built = m.sem("n3_rs_built")
    normalised = m.sem("n3_normalised")
    stored = m.sem("n3_stored")
    with nc.Block() as block:
        @block.vector
        def _(dve):
            nc.vector.tensor_tensor(rows, rows, residual, ALU.add).then_inc(added, 1)
            dve.wait_ge(added, 1)
            for t in range(T):
                nc.vector.bn_stats(stats[:, t, :], rows[:, t, :]).then_inc(measured, 1)
            dve.wait_ge(measured, T)
            for t in range(T):
                nc.vector.bn_aggr(mv[:, t, :], stats[:, t, :]).then_inc(var_built, 1)
            dve.wait_ge(sd_built, 1)
            nc.vector.reciprocal(sd, sd).then_inc(rs_built, 1)
            dve.wait_ge(rs_built, 1)
            dve.wait_ge(var_built, T)
            for t in range(T):
                nc.vector.tensor_scalar(rows[:, t, :], rows[:, t, :], mv[:, t, 0:1], sd[:, t:t + 1],
                                        ALU.subtract, ALU.mult).then_inc(normalised, 1)

        @block.scalar
        def _(act):
            act.wait_ge(var_built, T)
            nc.scalar.activation(sd, mv[:, :, 1], ACT.Sqrt, bias=m.eps[:, 0:1]).then_inc(sd_built, 1)

        @block.sync
        def _(sp):
            sp.wait_ge(normalised, T)
            sp.dma_start(x3_dram.rearrange("t p d -> p t d"), rows).then_inc(stored, 16)
            sp.wait_ge(stored, 16)


def values(nc, m, xT, w_dram, bv, v_rows):
    w = m.weights[:, 0:KC * D].rearrange("p (c n) -> p c n", c=KC)
    bias = m.at(41088, D)
    loaded = m.sem("v_loaded")
    multiplied = m.sem("v_multiplied")
    done = m.sem("v_done")
    with nc.Block() as block:
        @block.sync
        def _(sp):
            sp.dma_start(w, w_dram.rearrange("c p n -> p c n")).then_inc(loaded, 16)
            sp.dma_start(bias, bv.partition_broadcast(P)).then_inc(loaded, 16)

        @block.tensor
        def _(pe):
            pe.wait_ge(loaded, 32)
            for t in range(T):
                if t >= 8:
                    pe.wait_ge(done, t - 7)
                for c in range(KC):
                    mm = nc.tensor.matmul(m.banks[:, t % 8, 0:D], xT[:, c, P * t:P * t + P], w[:, c, :],
                                          start=(c == 0), stop=(c == KC - 1))
                mm.then_inc(multiplied, 1)

        @block.vector
        def _(dve):
            dve.wait_ge(loaded, 32)
            for t in range(T):
                dve.wait_ge(multiplied, t + 1)
                nc.vector.tensor_tensor(v_rows[:, t, :], m.banks[:, t % 8, 0:D], bias, ALU.add).then_inc(done, 1)
            dve.wait_ge(done, T)


def graph_ids(nc, m, ptr, q, q_dram, g_rows, g_cols):
    ptr_in = m.at(33000, NPTR).bitcast(I32)
    ptr_f = m.at(33100, NPTR)
    node = m.at(33200, T)
    at_most = m.at(33300, T, NPTR)
    spread = m.at(34400, T * P // 2).bitcast(BF16).rearrange("p (t i) -> p t i", t=T)
    loaded = m.sem("g_loaded")
    numbered = m.sem("g_numbered")
    step = m.sem("g_step")
    broadcast = m.sem("g_broadcast")
    copied = m.sem("g_copied")
    stored = m.sem("g_q_stored")
    with nc.Block() as block:
        @block.sync
        def _(sp):
            sp.dma_start(ptr_in, ptr.partition_broadcast(P)).then_inc(loaded, 16)
            for c in range(KC):
                sp.dma_start(q_dram.rearrange("t p c n -> c p t n")[c],
                             q[:, c, :].rearrange("p (t n) -> p t n", t=T)).then_inc(stored, 16)
            sp.wait_ge(stored, 16 * KC)

        @block.gpsimd
        def _(pool):
            nc.gpsimd.iota(node, pattern=[[P, T]], base=0, channel_multiplier=1,
                           allow_small_or_imprecise_dtypes=True).then_inc(numbered, 1)

        @block.vector
        def _(dve):
            dve.wait_ge(loaded, 16)
            nc.vector.tensor_copy(ptr_f, ptr_in).then_inc(step, 1)
            dve.wait_ge(step, 1)
            dve.wait_ge(numbered, 1)
            nc.vector.tensor_tensor(at_most, node.unsqueeze(2).to_broadcast([P, T, NPTR]),
                                    ptr_f.unsqueeze(1).to_broadcast([P, T, NPTR]), ALU.is_ge).then_inc(step, 1)
            dve.wait_ge(step, 2)
            nc.vector.tensor_reduce(g_cols, at_most, AX_X, ALU.add).then_inc(step, 1)
            dve.wait_ge(step, 3)
            nc.vector.tensor_tensor(spread, m.ident[:].unsqueeze(1).to_broadcast([P, T, P]),
                                    g_cols.unsqueeze(2).to_broadcast([P, T, P]), ALU.mult).then_inc(step, 1)
            for n in range(CH):
                dve.wait_ge(broadcast, n + 1)
                nc.vector.tensor_copy(g_rows[:, BANK * n:BANK * (n + 1)], m.banks[:, n, :]).then_inc(copied, 1)
            dve.wait_ge(copied, CH)

        @block.tensor
        def _(pe):
            pe.wait_ge(step, 4)
            for n in range(CH):
                nc.tensor.matmul(m.banks[:, n, :], m.ones_bf[:], spread[:, 4 * n:4 * n + 4, :],
                                 start=True, stop=True).then_inc(broadcast, 1)


def layer3(nc, m, adj, q_dram, x3_dram, kT, v_rows, g_rows, out):
    plain = m.at(12416, N)
    s = [m.at(16512 + N * b, N) for b in range(2)]
    adj_in = [m.at(32896 + N * b, N) for b in range(2)]
    eT = [m.at(41088 + GW * i, GROUP, P) for i in range(2)]
    q_in = [m.at(43136 + D * b, KC, P) for b in range(2)]
    x3_in = [m.at(43648 + D * b, D) for b in range(2)]
    top = m.at(44160, 2)
    row_sum = m.small[:, T:2 * T].rearrange("p (t k) -> p t k", t=T)
    rden = m.at(44168, 1)
    post = Post(m, 44200, m.banks[:, 7, 0:D], "l3")
    qk = [m.banks[:, 2 * i:2 * i + 2, :].rearrange("p a n -> p (a n)") for i in range(2)]
    turned = m.banks[:, 4:6, :].rearrange("p a (b i) -> p (a b) i", i=P)
    agg = [m.banks[:, 6 + b, 0:D] for b in range(2)]

    in_loaded = m.sems("l3_in_loaded", 2)
    x3_loaded = m.sems("l3_x3_loaded", 2)
    qk_done = m.sem("l3_qk_done")
    qk_read = m.sem("l3_qk_read")
    in_graph_built = m.sem("l3_in_graph_built")
    plain_built = m.sem("l3_plain_built")
    top_found = m.sem("l3_top_found")
    neg_top_built = m.sem("l3_neg_top_built")
    exp_done = m.sem("l3_exp_done")
    masked = m.sem("l3_masked")
    turn_done = m.sem("l3_turn_done")
    copied = m.sem("l3_copied")
    used = m.sem("l3_used")
    post_step = m.sem("l3_post_step")
    stored = m.sem("l3_stored")

    with nc.Block() as block:
        @block.sync
        def _(sp):
            def tile(t, b, q):
                if not early(t, 2):
                    sp.wait_ge(qk_done, NG * (t - 1))
                    sp.wait_ge(plain_built, t - 1)
                sp.dma_start(q_in[b], q_dram[t]).then_inc(in_loaded[b], 16)
                sp.dma_start(adj_in[b], adj[t]).then_inc(in_loaded[b], 16)
                if not early(t, 1):
                    load_x3(t - 1, 1 - b)

            def load_x3(t, b):
                if not early(t, 2):
                    sp.wait_ge(post.normalised, t - 1)
                sp.dma_start(x3_in[b], x3_dram[t]).then_inc(x3_loaded[b], 16)
            pairs(sp, tile)
            load_x3(T - 1, 1)

        @block.vector
        def _(dve):
            post_steps = Steps(dve, post_step, 4)

            def build_plain(t, b, q):
                g = m.g_cols.unsqueeze(2)[:, t, :]
                if not early(t, 1):
                    dve.wait_ge(top_found, t)
                nc.vector.tensor_scalar(plain, g_rows, g, 2.0 - 2.0 * OFF_GRAPH, ALU.is_equal,
                                        ALU.mult).then_inc(in_graph_built, 1)
                dve.wait_ge(in_graph_built, t + 1)
                dve.wait_ge(in_loaded[b], 32 * (q + 1))
                nc.vector.scalar_tensor_tensor(plain, plain, 2.0 * OFF_GRAPH, adj_in[b], ALU.add,
                                               ALU.mult).then_inc(plain_built, 1)

            def score(t, b):
                g = m.g_cols.unsqueeze(2)[:, t, :]
                for c in range(NG):
                    dve.wait_ge(qk_done, NG * t + c + 1)
                    if c == 0 and not early(t, 2):
                        dve.wait_ge(turn_done, NG * (t - 1))
                    nodes = slice(GW * c, GW * (c + 1))
                    nc.vector.scalar_tensor_tensor(s[b][:, nodes], g_rows[:, nodes], g, qk[c % 2],
                                                   ALU.is_equal, ALU.mult).then_inc(qk_read, 1)
                dve.wait_ge(qk_read, NG * (t + 1))
                dve.wait_ge(plain_built, t + 1)
                if not early(t, 1):
                    dve.wait_ge(neg_top_built, t)
                nc.vector.memset(post.spare, 0.0)
                nc.vector.tensor_tensor_reduce(s[b], s[b], plain, 1.0, -3.0e38, ALU.add, ALU.max,
                                               top[:, 0:1]).then_inc(top_found, 1)
                dve.wait_ge(top_found, t + 1)
                if not early(t, 1):
                    dve.wait_ge(exp_done, t)
                nc.vector.tensor_scalar(top[:, 1:2], top[:, 0:1], -1.0, None, ALU.mult).then_inc(neg_top_built, 1)

            def mask(t, b):
                g = m.g_cols.unsqueeze(2)[:, t, :]
                dve.wait_ge(exp_done, t + 1)
                nc.vector.scalar_tensor_tensor(s[b], g_rows, g, s[b], ALU.is_equal, ALU.mult).then_inc(masked, 1)

            def finish(t, b, q):
                post_steps.tile(t)
                dve.wait_ge(used, NG * (t + 1))
                dve.wait_ge(x3_loaded[b], 16 * (q + 1))
                if not early(t, 1):
                    dve.wait_ge(post.normalised, t)
                post_steps(nc.vector.reciprocal(rden, row_sum[:, t, :]))
                post_steps(nc.vector.scalar_tensor_tensor(post.pre, agg[b], rden, x3_in[b], ALU.mult, ALU.add))
                if not early(t, 1):
                    dve.wait_ge(stored, 16 * t)
                post.normalise(nc, dve, post_steps, t, used=stored)

            build_plain(0, 0, 0)
            score(0, 0)
            build_plain(1, 1, 0)
            mask(0, 0)

            def tile(t, b, q):
                if not late(t, 1):
                    score(t + 1, 1 - b)
                if not early(t, 1):
                    finish(t - 1, 1 - b, q if b else q - 1)
                if not late(t, 2):
                    build_plain(t + 2, b, q + 1)
                if not late(t, 1):
                    mask(t + 1, 1 - b)
            pairs(dve, tile)
            finish(T - 1, 1, T // 2 - 1)

        @block.scalar
        def _(act):
            def exp(t, b):
                act.wait_ge(neg_top_built, t + 1)
                nc.scalar.activation(s[b], s[b], ACT.Exp, bias=top[:, 1:2], accum_out=row_sum[:, t, :]).then_inc(
                    exp_done, 1)

            def finish(t):
                post.deviation(nc, act, t, m.eps[:, 0:1])
                act.wait_ge(post.normalised, t + 1)
                act.dma_start(out[t], post.xn).then_inc(stored, 16)

            exp(0, 0)

            def tile(t, b, q):
                for g in range(NG):
                    act.wait_ge(turn_done, NG * t + g + 1)
                    if not (early(t, 1) and g < 2):
                        act.wait_ge(used, NG * t + g - 1)
                    nc.scalar.copy(eT[g % 2], turned).then_inc(copied, 1)
                if not late(t, 1):
                    exp(t + 1, 1 - b)
                if not early(t, 1):
                    finish(t - 1)
            pairs(act, tile)
            finish(T - 1)
            act.wait_ge(stored, 16 * T)

        @block.tensor
        def _(pe):
            def scores(t, b, q, c):
                if c == 0:
                    pe.wait_ge(in_loaded[b], 32 * (q + 1))
                if not (early(t, 1) and c < 2):
                    pe.wait_ge(qk_read, NG * t + c - 1)
                for half in range(2):
                    for k in range(KC):
                        n = GW * c + BANK * half
                        mm = nc.tensor.matmul(qk[c % 2][:, BANK * half:BANK * (half + 1)], q_in[b][:, k, :],
                                              kT[:, k, n:n + BANK], start=(k == 0), stop=(k == KC - 1))
                mm.then_inc(qk_done, 1)

            def turn(t, b, g):
                if g == 0:
                    pe.wait_ge(masked, t + 1)
                if not (early(t, 1) and g == 0):
                    pe.wait_ge(copied, NG * t + g)
                for k in range(GROUP):
                    j = GROUP * g + k
                    mm = nc.tensor.transpose(turned[:, k, :], s[b][:, P * j:P * j + P], m.ident[:])
                mm.then_inc(turn_done, 1)

            def aggregate(t, b, g):
                if g == 0 and not early(t, 2):
                    pe.wait_ge(post.normalised, t - 1)
                pe.wait_ge(copied, NG * t + g + 1)
                for k in range(GROUP):
                    j = GROUP * g + k
                    mm = nc.tensor.matmul(agg[b], eT[g % 2][:, k, :], v_rows[:, j, :],
                                          start=(j == 0), stop=(j == T - 1))
                mm.then_inc(used, 1)

            for c in range(NG):
                scores(0, 0, 0, c)

            def tile(t, b, q):
                more = not late(t, 1)
                q_next = q if b == 0 else q + 1
                if more:
                    scores(t + 1, 1 - b, q_next, 0)
                    scores(t + 1, 1 - b, q_next, 1)
                turn(t, b, 0)
                if more:
                    scores(t + 1, 1 - b, q_next, 2)
                turn(t, b, 1)
                if more:
                    scores(t + 1, 1 - b, q_next, 3)
                aggregate(t, b, 0)
                turn(t, b, 2)
                aggregate(t, b, 1)
                turn(t, b, 3)
                aggregate(t, b, 2)
                aggregate(t, b, 3)
            pairs(pe, tile)


PARAMS = ["enc_bn_gamma", "enc_bn_beta", "enc_mlp_b", "enc_mlp_bn_gamma", "enc_mlp_bn_beta",
          "dec_mlp_b", "dec_mlp_bn_gamma", "dec_mlp_bn_beta", "bq", "bk"]


def program(nc, x, adj, adjT_blocks, w1, b1, wbd, wbdT, vbd, params, w_enc, w_dec, wq, wk, wv, wdec_head,
            bv, ptr, out):
    def scratch(name, *shape):
        return nc.dram_tensor(name, shape, F32).ap()
    x2_dram = scratch("x2_scratch", T, P, D)
    xc_dram = scratch("xc_scratch", T, P, D)
    x3_dram = scratch("x3_scratch", T, P, D)
    q_dram = scratch("q_scratch", T, P, KC, P)
    with ExitStack() as ctx:
        m = Memory(nc, ctx)
        m.h = m.at(8320, T, D)
        m.x1 = m.at(16512, T, D)
        m.feats = m.at(0, T, D)
        m.f2 = m.at(32896, HEADS, N)
        m.f1 = m.small[:, 0:P].rearrange("p (t h) -> p t h", t=T)
        m.neg_top = m.small[:, P:2 * P].rearrange("p (t h) -> p t h", t=T)
        m.row_sum = m.small[:, 2 * P:3 * P].rearrange("p (t h) -> p t h", t=T)
        m.g_cols = m.small[:, 0:T]
        m.wext = m.weights[:, 0:KC * (P + 4)].rearrange("p (c n) -> p c n", c=KC)
        m.wv_rows = m.weights[:, KC * (P + 4):KC * (P + 4) + HEADS * P].rearrange("p (h n) -> p h n", h=HEADS)
        param = {k: m.params[:, KC * i:KC * (i + 1)] for i, k in enumerate(PARAMS)}
        rows = lambda start: m.at(start, T, D)
        cols = lambda start: m.at(start, KC, N)
        A, B, C, E = 8320, 16512, 24704, 32896

        constants(nc, m, params)
        layer0(nc, m, x, adjT_blocks, w1)
        layer2_weights(nc, m, wbd, wbdT, vbd)
        layer1(nc, m, adjT_blocks, b1, x2_dram)

        m.clear_semaphores()
        attention(nc, m, adj, xc_dram, "a1", True)
        turn_nodes(nc, m, "t1", rows(A), cols(B), False, load=(xc_dram, rows(A)))
        batch_norm(nc, m, "n1", cols(B), param["enc_bn_gamma"], param["enc_bn_beta"])
        dense(nc, m, "d1", cols(B), cols(C), w_enc, param["enc_mlp_b"], elu=True, residual=True, at=A)
        batch_norm(nc, m, "n2", cols(C), param["enc_mlp_bn_gamma"], param["enc_mlp_bn_beta"])
        turn_nodes(nc, m, "t2", cols(C), m.feats, True)

        m.clear_semaphores()
        attention(nc, m, adj, xc_dram, "a2", False)
        turn_nodes(nc, m, "t3", rows(A), cols(B), False, load=(xc_dram, rows(A)), extra=(x2_dram, rows(E)))
        dense(nc, m, "d2", cols(B), cols(C), wdec_head, None, elu=True, block_diagonal=True)
        dense(nc, m, "d3", cols(C), cols(B), w_dec, param["dec_mlp_b"], elu=True, residual=True)
        batch_norm(nc, m, "n4", cols(B), param["dec_mlp_bn_gamma"], param["dec_mlp_bn_beta"])
        turn_nodes(nc, m, "t4", cols(B), rows(A), True)
        layer_norm_rows(nc, m, rows(A), rows(E), x3_dram)

        turn_nodes(nc, m, "t5", rows(A), cols(B), False)
        values(nc, m, cols(B), wv, bv, m.feats)
        dense(nc, m, "d4", cols(B), cols(C), wk, param["bk"])
        dense(nc, m, "d5", cols(B), cols(A), wq, param["bq"], scale=1.0 / 16)
        g_rows = m.at(45400, N)
        graph_ids(nc, m, ptr, cols(A), q_dram, g_rows, m.g_cols)
        m.clear_semaphores()
        layer3(nc, m, adj, q_dram, x3_dram, cols(C), m.feats, g_rows, out)


def kernel(**inputs):
    import numpy as np
    import concourse.bacc as bacc
    from concourse import mybir as mb
    from concourse.bass_utils import run_bass_kernel_spmd as run

    g = {k: np.asarray(v) for k, v in inputs.items()}
    adj = g["adj"]

    def block_diagonal(a):
        n = a.shape[2]
        o = np.zeros((KC, P, 2 * n), a.dtype)
        for h in range(HEADS):
            o[h // 2, DH * (h % 2):DH * (h % 2) + DH, n * (h % 2):n * (h % 2) + n] = a[h]
        return o

    v = block_diagonal(g["L2_gnn_V"][..., 0].transpose(0, 2, 1))
    params = np.stack([g["L3_gnn_" + k if k in ("bq", "bk") else "L2_gnn_" + k] for k in PARAMS])
    head_out = np.zeros((KC, P, D), adj.dtype)
    wT = block_diagonal(g["L2_gnn_W"].transpose(0, 2, 1))
    for c in range(KC):
        head_out[c, :, P * c:P * c + P] = wT[c]
    arrays = {
        "x": g["x"],
        "adj": adj.reshape(T, P, N),
        "adjT_blocks": adj.reshape(T, P, T, P).transpose(0, 3, 2, 1).reshape(T, P, N),
        "w1": g["L1_gnn_W"].transpose(1, 0, 2).reshape(D, D),
        "b1": g["L1_gnn_b"].reshape(D),
        "wbd": block_diagonal(g["L2_gnn_W"]),
        "wbdT": wT,
        "vbd": v[:, :, [0, 2, 1, 3]],
        "params": params.reshape(-1, P).T,
        "w_enc": g["L2_gnn_enc_mlp_W"].T.reshape(KC, P, D),
        "w_dec": g["L2_gnn_dec_mlp_W"].T.reshape(KC, P, D),
        "wq": g["L3_gnn_Wq"].T.reshape(KC, P, D),
        "wk": g["L3_gnn_Wk"].T.reshape(KC, P, D),
        "wv": g["L3_gnn_Wv"].T.reshape(KC, P, D),
        "w_head_out": head_out,
        "bv": g["L3_gnn_bv"],
        "ptr": g["L3_gnn_ptr"],
    }
    nc = bacc.Bacc("TRN2", target_bir_lowering=False, num_devices=1)
    maps, args = {}, []
    for name, a in arrays.items():
        maps[f"in_{name}"] = np.ascontiguousarray(a)
        args.append(nc.dram_tensor(f"in_{name}", a.shape, mb.dt.from_np(a.dtype), kind="ExternalInput").ap())
    args.append(nc.dram_tensor("out_dram", (T, P, D), mb.dt.float32, kind="ExternalOutput").ap())
    program(nc, *args)
    return run(nc, [maps], core_ids=[0]).results[0]["out_dram"].reshape(N, D)
```

```python
from contextlib import ExitStack

import concourse.bass as bass
from concourse import mybir

F32 = mybir.dt.float32
BF16 = mybir.dt.bfloat16
I32 = mybir.dt.int32
ALU = mybir.AluOpType
ACT = mybir.ActivationFunctionType
AX_X = mybir.AxisListType.X

P = 128
N = 4096
T = N // P
D = 256
KC = D // P
HEADS = 4
DH = D // HEADS
NPTR = 33
LN_EPS = 1e-5
BN_EPS = 1e-6
NORM_EPS = 1e-12
MASKED = -1.0e38
TANH_ONE = 1.0 + 2.0 ** -23
OFF_GRAPH = -1000000.0
BANK = 512
GROUP = 8
NG = T // GROUP
GW = GROUP * P
CH = N // BANK


class Steps:

    def __init__(self, eng, sem, per):
        self.eng, self.sem, self.per, self.k = eng, sem, per, per

    def tile(self, t):
        assert self.k == self.per, (self.k, self.per)
        self.base, self.k = t * self.per, 0

    def __call__(self, ins):
        self.k += 1
        ins.then_inc(self.sem, 1)
        self.eng.wait_ge(self.sem, self.base + self.k)


def early(t, n):
    return isinstance(t, int) and t < n


def late(t, n):
    return isinstance(t, int) and t >= T - n


def pairs(eng, tile):
    for q in (0,):
        tile(2 * q, 0, q)
        tile(2 * q + 1, 1, q)
    with eng.Fori(1, T // 2 - 1) as q:
        tile(2 * q, 0, q)
        tile(2 * q + 1, 1, q)
    for q in (T // 2 - 1,):
        tile(2 * q, 0, q)
        tile(2 * q + 1, 1, q)


def singles(eng, tile):
    tile(0)
    with eng.Fori(1, T - 1) as t:
        tile(t)
    tile(T - 1)


class Memory:

    def __init__(self, nc, ctx):
        self.nc, self.taken = nc, []
        sb = lambda name, shape, dt=F32: ctx.enter_context(nc.sbuf_tensor(name, shape, dt))
        self.arena = sb("arena", [P, 51328])
        self.ident = sb("ident", [P, P])
        self.ones_bf = sb("ones_bf", [P, P], BF16)
        self.eps = sb("eps", [P, 2])
        self.weights = sb("weights", [P, 1040])
        self.small = sb("small", [P, 384])
        self.params = sb("params", [P, 2 * 10])
        self.banks = ctx.enter_context(nc.psum_tensor("banks", [P, 8, BANK], F32))

    def at(self, start, *shape):
        n = 1
        for s in shape:
            n *= s
        v = self.arena[:, start:start + n]
        if len(shape) == 2:
            v = v.rearrange("p (a b) -> p a b", a=shape[0])
        if len(shape) == 3:
            v = v.rearrange("p (a b c) -> p a b c", a=shape[0], b=shape[1])
        return v

    def sem(self, name):
        self.taken.append(self.nc.alloc_semaphore(name))
        return self.taken[-1]

    def clear_semaphores(self):
        self.nc.clear_and_free_semaphores(self.taken)
        self.nc.all_engine_barrier()
        self.taken = []

    def sems(self, name, n):
        return [self.sem(f"{name}{i}") for i in range(n)]


def constants(nc, m, params):
    s_loaded = m.sem("c_loaded")
    s_ones = m.sem("c_ones")
    s_built = m.built = m.sem("c_built")
    with nc.Block() as block:
        @block.sync
        def _(sp):
            sp.dma_start(m.params[:], params).then_inc(s_loaded, 16)
            sp.wait_ge(s_loaded, 16)

        @block.vector
        def _(dve):
            nc.vector.memset(m.ident[:], 1.0).then_inc(s_ones, 1)
            nc.vector.memset(m.ones_bf[:], 1.0).then_inc(s_ones, 1)
            nc.vector.memset(m.eps[:, 0:1], LN_EPS).then_inc(s_ones, 1)
            nc.vector.memset(m.eps[:, 1:2], BN_EPS).then_inc(s_ones, 1)
            dve.wait_ge(s_ones, 4)

        @block.gpsimd
        def _(pool):
            pool.wait_ge(s_ones, 1)
            nc.gpsimd.affine_select(out=m.ident[:], in_=m.ident[:], compare_op=ALU.is_equal, fill=0.0,
                                    base=0, pattern=[[-1, P]], channel_multiplier=1).then_inc(s_built, 1)
            pool.wait_ge(s_built, 1)


class Post:

    def __init__(self, m, at, bank, name):
        self.m = m
        self.pre = m.at(at, D)
        self.xn = m.at(at + 256, D)
        self.xnT = m.at(at + 512, KC, P)
        self.stats = m.at(at + 768, 6)
        self.mv = m.at(at + 776, 2)
        self.sd = m.at(at + 780, 1)
        self.rs = m.at(at + 784, 1)
        self.spare = m.at(at + 788, 1)
        self.turned_bank = bank.rearrange("p (c n) -> p c n", c=KC)
        self.var_built = m.sem(name + "_var_built")
        self.sd_built = m.sem(name + "_sd_built")
        self.normalised = m.sem(name + "_normalised")
        self.turned = m.sem(name + "_turned")
        self.copied = m.sem(name + "_turned_copied")

    def normalise(self, nc, dve, steps, t, out=None, used=None):
        steps(nc.vector.bn_stats(self.stats, self.pre))
        nc.vector.memset(self.spare, 0.0)
        nc.vector.bn_aggr(self.mv, self.stats).then_inc(self.var_built, 1)
        dve.wait_ge(self.var_built, t + 1)
        dve.wait_ge(self.sd_built, t + 1)
        steps(nc.vector.reciprocal(self.rs, self.sd))
        if used is None and not early(t, 1):
            dve.wait_ge(self.turned, t)
        nc.vector.tensor_scalar(self.xn, self.pre, self.mv[:, 0:1], self.rs, ALU.subtract,
                                ALU.mult).then_inc(self.normalised, 1)

    def deviation(self, nc, act, t, eps):
        act.wait_ge(self.var_built, t + 1)
        nc.scalar.activation(self.sd, self.mv[:, 1:2], ACT.Sqrt, bias=eps).then_inc(self.sd_built, 1)

    def turn(self, nc, pe, t):
        pe.wait_ge(self.normalised, t + 1)
        if not early(t, 1):
            pe.wait_ge(self.copied, t)
        for c in range(KC):
            mm = nc.tensor.transpose(self.turned_bank[:, c, :], self.xn[:, c * P:(c + 1) * P], self.m.ident[:])
        mm.then_inc(self.turned, 1)

    def copy_turned(self, nc, act, t, used):
        act.wait_ge(self.turned, t + 1)
        if not early(t, 1):
            act.wait_ge(used, t)
        nc.scalar.copy(self.xnT, self.turned_bank).then_inc(self.copied, 1)


def layer0(nc, m, x, adjT_blocks, w1):
    x_in = m.at(0, T, D + 1)
    adj_in = [m.at(24704 + 4096 * b, T, P) for b in range(2)]
    inc = [m.at(32896 + 4096 * b, T, P) for b in range(2)]
    mask = m.arena[:, 41088:43136].bitcast(BF16).rearrange("p (t i) -> p t i", t=T)
    rnorm = m.at(43136, P)
    w = m.weights[:, 0:KC * D].rearrange("p (c n) -> p c n", c=KC)
    counts = m.banks[:, 0, 0:P]
    agg = [m.banks[:, 1 + b, 0:D + 1] for b in range(2)]
    proj = m.banks[:, 4, 0:D]
    post = Post(m, 43264, m.banks[:, 3, 0:D], "l0")
    rdeg = m.at(43264 + 1024, 1)

    adj_loaded = m.sems("l0_adj_loaded", 2)
    x_loaded = m.sem("l0_x_loaded")
    w_loaded = m.sem("l0_w_loaded")
    ones_set = m.sem("l0_ones_set")
    mask_built = m.sem("l0_mask_built")
    counted = m.sem("l0_counted")
    norm_built = m.sem("l0_norm_built")
    inc_built = m.sem("l0_inc_built")
    agg_done = m.sem("l0_agg_done")
    x1_kept = m.sem("l0_x1_kept")
    proj_done = m.sem("l0_proj_done")
    proj_copied = m.sem("l0_proj_copied")
    inc_step = m.sem("l0_inc_step")
    post_step = m.sem("l0_post_step")

    with nc.Block() as block:
        @block.sync
        def _(sp):
            def tile(t, b, q):
                if not early(t, 2):
                    sp.wait_ge(inc_built, t - 1)
                sp.dma_start(adj_in[b], adjT_blocks[t].rearrange("p (j i) -> p j i", j=T)).then_inc(
                    adj_loaded[b], 16)
                if early(t, 1):
                    sp.dma_start(x_in[:, :, 0:D], x.rearrange("(t p) d -> p t d", p=P)).then_inc(x_loaded, 16)
                    sp.dma_start(w, w1.rearrange("(c p) n -> p c n", p=P)).then_inc(w_loaded, 16)
            pairs(sp, tile)

        @block.vector
        def _(dve):
            inc_steps = Steps(dve, inc_step, 3)
            post_steps = Steps(dve, post_step, 4)

            def build_mask(t, b, q):
                dve.wait_ge(adj_loaded[b], 16 * (q + 1))
                if not early(t, 1):
                    dve.wait_ge(counted, t)
                nc.vector.tensor_scalar(mask, adj_in[b], 0.0, None, ALU.is_gt).then_inc(mask_built, 1)

            def build_inc(t, b):
                inc_steps.tile(t)
                dve.wait_ge(norm_built, t + 1)
                inc_steps(nc.vector.tensor_scalar(rnorm, rnorm, NORM_EPS, None, ALU.max))
                inc_steps(nc.vector.reciprocal(rnorm, rnorm))
                if not early(t, 2):
                    dve.wait_ge(agg_done, t - 1)
                rnorm_all = rnorm.unsqueeze(1).to_broadcast([P, T, P])
                inc_steps(nc.vector.scalar_tensor_tensor(inc[b], adj_in[b], 0.0, rnorm_all,
                                                         ALU.is_gt, ALU.mult))
                nc.vector.tensor_tensor(inc[b], inc[b], adj_in[b], ALU.add).then_inc(inc_built, 1)

            def finish(t, b):
                post_steps.tile(t)
                dve.wait_ge(agg_done, t + 1)
                post_steps(nc.vector.reciprocal(rdeg, agg[b][:, D:D + 1]))
                post_steps(nc.vector.scalar_tensor_tensor(post.pre, agg[b][:, 0:D], rdeg, x_in[:, t, 0:D],
                                                          ALU.mult, ALU.add))
                if not early(t, 1):
                    dve.wait_ge(x1_kept, t)
                post.normalise(nc, dve, post_steps, t)

            nc.vector.memset(x_in[:, :, D:D + 1], 1.0).then_inc(ones_set, 1)
            dve.wait_ge(x_loaded, 16)
            build_mask(0, 0, 0)
            build_inc(0, 0)
            build_mask(1, 1, 0)

            def tile(t, b, q):
                if not late(t, 1):
                    build_inc(t + 1, 1 - b)
                if not late(t, 2):
                    build_mask(t + 2, b, q + 1)
                if not early(t, 1):
                    finish(t - 1, 1 - b)
            pairs(dve, tile)
            finish(T - 1, 1)

        @block.scalar
        def _(act):
            def norm(t):
                act.wait_ge(counted, t + 1)
                if not early(t, 1):
                    act.wait_ge(inc_built, t)
                nc.scalar.activation(rnorm, counts, ACT.Sqrt).then_inc(norm_built, 1)

            def finish(t):
                post.deviation(nc, act, t, m.eps[:, 0:1])
                post.copy_turned(nc, act, t, proj_done)
                act.wait_ge(proj_done, t + 1)
                nc.scalar.copy(m.h[:, t, :], proj).then_inc(proj_copied, 1)

            norm(0)

            def tile(t, b, q):
                if not late(t, 1):
                    norm(t + 1)
                if not early(t, 1):
                    finish(t - 1)
            pairs(act, tile)
            finish(T - 1)
            act.wait_ge(proj_copied, T)

        @block.gpsimd
        def _(pool):
            def tile(t, b, q):
                pool.wait_ge(post.normalised, t + 1)
                nc.gpsimd.tensor_copy(m.x1[:, t, :], post.xn).then_inc(x1_kept, 1)
            pairs(pool, tile)
            pool.wait_ge(x1_kept, T)

        @block.tensor
        def _(pe):
            def count(t):
                pe.wait_ge(mask_built, t + 1)
                if not early(t, 1):
                    pe.wait_ge(norm_built, t)
                for j in range(T):
                    mm = nc.tensor.matmul(counts, m.ones_bf[:], mask[:, j, :], start=(j == 0), stop=(j == T - 1))
                mm.then_inc(counted, 1)

            def aggregate(t, b):
                pe.wait_ge(inc_built, t + 1)
                if not early(t, 2):
                    pe.wait_ge(post.normalised, t - 1)
                for j in range(T):
                    mm = nc.tensor.matmul(agg[b], inc[b][:, j, :], x_in[:, j, :],
                                          start=(j == 0), stop=(j == T - 1))
                mm.then_inc(agg_done, 1)

            def project(t):
                post.turn(nc, pe, t)
                if not early(t, 1):
                    pe.wait_ge(proj_copied, t)
                pe.wait_ge(post.copied, t + 1)
                for c in range(KC):
                    mm = nc.tensor.matmul(proj, post.xnT[:, c, :], w[:, c, :], start=(c == 0), stop=(c == KC - 1))
                mm.then_inc(proj_done, 1)

            pe.wait_ge(ones_set, 1)
            pe.wait_ge(x_loaded, 16)
            pe.wait_ge(w_loaded, 16)
            count(0)

            def tile(t, b, q):
                if not late(t, 1):
                    count(t + 1)
                aggregate(t, b)
                if not early(t, 1):
                    project(t - 1)
            pairs(pe, tile)
            project(T - 1)


def layer2_weights(nc, m, wbd, wbdT, vbd):
    wT = m.at(43264, KC, P)
    v = m.at(43520, KC, 4)
    prod = m.banks[:, 0, 0:KC * 4].rearrange("p (c k) -> p c k", c=KC)
    loaded = m.sem("lw_loaded")
    multiplied = m.sem("lw_multiplied")
    spread = m.sem("lw_spread")
    with nc.Block() as block:
        @block.sync
        def _(sp):
            sp.dma_start(m.wext[:, :, 0:P], wbd.rearrange("c p n -> p c n")).then_inc(loaded, 16)
            sp.dma_start(wT, wbdT.rearrange("c p n -> p c n")).then_inc(loaded, 16)
            sp.dma_start(v, vbd.rearrange("c p n -> p c n")).then_inc(loaded, 16)
            sp.wait_ge(loaded, 48)

        @block.tensor
        def _(pe):
            pe.wait_ge(loaded, 48)
            for c in range(KC):
                mm = nc.tensor.matmul(prod[:, c, :], wT[:, c, :], v[:, c, :], start=True, stop=True)
            mm.then_inc(multiplied, 1)

        @block.vector
        def _(dve):
            dve.wait_ge(multiplied, 1)
            dve.wait_ge(loaded, 48)
            nc.vector.tensor_copy(m.wext[:, :, P:P + 4], prod).then_inc(spread, 1)
            for h in range(HEADS):
                col = prod[:, h // 2, 2 + h % 2:3 + h % 2]
                nc.vector.tensor_copy(m.wv_rows[:, h, :], col.to_broadcast([P, P])).then_inc(spread, 1)
            nc.vector.memset(m.feats[:, :, :, DH:DH + 1], 1.0).then_inc(spread, 1)
            dve.wait_ge(spread, 2 + HEADS)


def layer1(nc, m, adjT_blocks, b1, x2_dram):
    adj_in = [m.at(24704 + 4096 * b, T, P) for b in range(2)]
    bias = m.at(50400, D)
    agg = [m.banks[:, 1 + b, 0:D] for b in range(2)]
    proj = m.banks[:, 4, 0:KC * (P + 4)].rearrange("p (c k) -> p c k", c=KC)
    f2_rows = m.banks[:, 5, :].rearrange("p (h n) -> p h n", h=HEADS)
    post = Post(m, 49280, m.banks[:, 3, 0:D], "l1")

    adj_loaded = m.sems("l1_adj_loaded", 2)
    bias_loaded = m.sem("l1_bias_loaded")
    agg_done = m.sem("l1_agg_done")
    x2_stored = m.sem("l1_x2_stored")
    proj_done = m.sem("l1_proj_done")
    proj_copied = m.sem("l1_proj_copied")
    post_step = m.sem("l1_post_step")

    with nc.Block() as block:
        @block.sync
        def _(sp):
            sp.dma_start(bias, b1.partition_broadcast(P)).then_inc(bias_loaded, 16)

            def tile(t, b, q):
                if not early(t, 2):
                    sp.wait_ge(agg_done, t - 1)
                sp.dma_start(adj_in[b], adjT_blocks[t].rearrange("p (j i) -> p j i", j=T)).then_inc(
                    adj_loaded[b], 16)
            pairs(sp, tile)

        @block.vector
        def _(dve):
            post_steps = Steps(dve, post_step, 4)
            dve.wait_ge(bias_loaded, 16)

            def tile(t, b, q):
                post_steps.tile(t)
                dve.wait_ge(agg_done, t + 1)
                if not early(t, 1):
                    dve.wait_ge(post.normalised, t)
                post_steps(nc.vector.tensor_tensor(post.pre, agg[b], bias, ALU.add))
                post_steps(nc.vector.tensor_tensor(post.pre, post.pre, m.x1[:, t, :], ALU.add))
                if not early(t, 1):
                    dve.wait_ge(x2_stored, 16 * t)
                post.normalise(nc, dve, post_steps, t)
            pairs(dve, tile)

        @block.scalar
        def _(act):
            def tile(t, b, q):
                post.deviation(nc, act, t, m.eps[:, 0:1])
                act.wait_ge(post.normalised, t + 1)
                act.dma_start(x2_dram[t], post.xn).then_inc(x2_stored, 16)
                post.copy_turned(nc, act, t, proj_done)
                act.wait_ge(proj_done, t + 1)
                nc.scalar.copy(m.feats[:, t, :, 0:DH].rearrange("p (c k) n -> p c k n", c=KC),
                               proj[:, :, 0:P].rearrange("p c (k n) -> p c k n", k=2))
                nc.scalar.mul(m.f1[:, t, :].rearrange("p (c n) -> p c n", c=KC), proj[:, :, P:P + 2], 0.5)
                nc.scalar.copy(m.f2.rearrange("p h (t n) -> p h t n", t=T)[:, :, t, :], f2_rows).then_inc(
                    proj_copied, 1)
            pairs(act, tile)
            act.wait_ge(proj_copied, T)
            act.wait_ge(x2_stored, 16 * T)

        @block.tensor
        def _(pe):
            def aggregate(t, b, q):
                pe.wait_ge(adj_loaded[b], 16 * (q + 1))
                if not early(t, 2):
                    pe.wait_ge(post.normalised, t - 1)
                for j in range(T):
                    mm = nc.tensor.matmul(agg[b], adj_in[b][:, j, :], m.h[:, j, :],
                                          start=(j == 0), stop=(j == T - 1))
                mm.then_inc(agg_done, 1)

            def project(t):
                post.turn(nc, pe, t)
                if not early(t, 1):
                    pe.wait_ge(proj_copied, t)
                pe.wait_ge(post.copied, t + 1)
                for c in range(KC):
                    nc.tensor.matmul(proj[:, c, :], post.xnT[:, c, :], m.wext[:, c, :], start=True, stop=True)
                for h in range(HEADS):
                    mm = nc.tensor.matmul(f2_rows[:, h, :], m.wv_rows[:, h, :], post.xnT[:, h // 2, :],
                                          start=True, stop=True)
                mm.then_inc(proj_done, 1)

            def tile(t, b, q):
                aggregate(t, b, q)
                if not early(t, 1):
                    project(t - 1)
            pairs(pe, tile)
            project(T - 1)


def attention(nc, m, adj, out_dram, name, first):
    TC = HEADS * NG
    TANH_AHEAD, SCORE_AHEAD, EXP_AHEAD = 15, 10, 6
    PIECE = BANK
    e = [m.at(8320 + 4096 * h, N) for h in range(HEADS)]
    adj_in = [m.at(24704 + 4096 * b, N) for b in range(2)]
    eT = [m.at(49280 + GW * i, GROUP, P) for i in range(2)]
    turned = [m.banks[:, 2 * i:2 * i + 2, :].rearrange("p a (b i) -> p (a b) i", i=P) for i in range(3)]
    agg = [m.banks[:, 6 + h % 2, (DH + 1) * (h // 2):(DH + 1) * (h // 2 + 1)] for h in range(HEADS)]
    xc = m.weights[:, 0:D]
    den = m.weights[:, D:D + 1]
    top = m.weights[:, D + 2:D + 3]
    tops = m.weights[:, D + 4:D + 4 + NG]
    off_edge = m.weights[:, BANK:BANK + PIECE]
    f1_now = [m.small[:, 2 * P + 8 * b:2 * P + 8 * b + HEADS] for b in range(2)]
    neg_top_now = [m.small[:, 2 * P + 8 * b + 4:2 * P + 8 * b + 8] for b in range(2)]
    on_vector = [] if first else [n for n in range(TC) if n % 2 == 0]
    on_scalar = [n for n in range(TC) if n not in on_vector]

    adj_loaded = m.sems(name + "_adj_loaded", 2)
    off_edge_built = m.sem(name + "_off_edge_built")
    masked = m.sem(name + "_masked")
    tanh_done = m.sem(name + "_tanh_done")
    scored = m.sem(name + "_scored")
    top_found = m.sem(name + "_top_found")
    top_joined = m.sem(name + "_top_joined")
    neg_top_built = m.sem(name + "_neg_top_built")
    neg_top_kept = m.sem(name + "_neg_top_kept")
    f1_fetched = m.sem(name + "_f1_fetched")
    exp_done = m.sem(name + "_exp_done")
    turn_done = m.sem(name + "_turn_done")
    copied_by_vector = m.sem(name + "_copied_by_vector")
    copied_by_scalar = m.sem(name + "_copied_by_scalar")
    used = m.sem(name + "_used")
    agg_read = m.sem(name + "_agg_read")
    stored = m.sem(name + "_stored")
    finish_step = m.sem(name + "_finish_step")

    def ahead(t, n, k):
        return t + (n + k) // TC, (n + k) % TC

    def exists(t):
        return not (isinstance(t, int) and (t < 0 or t >= T))

    def wait_copied(eng, t, n):
        if n in on_vector:
            eng.wait_ge(copied_by_vector, len(on_vector) * t + on_vector.index(n) + 1)
        else:
            eng.wait_ge(copied_by_scalar, len(on_scalar) * t + on_scalar.index(n) + 1)

    def columns(n):
        return slice(GW * (n % NG), GW * (n % NG + 1))

    def copy_out(eng, copy, sem, t, n):
        if not exists(t):
            return
        eng.wait_ge(turn_done, TC * t + n + 1)
        if not (early(t, 1) and n < 2):
            eng.wait_ge(used, TC * t + n - 1)
        copy(eT[n % 2], turned[n % 3]).then_inc(sem, 1)

    with nc.Block() as block:
        @block.sync
        def _(sp):
            def store(t):
                sp.wait_ge(agg_read, HEADS * (t + 1))
                sp.dma_start(out_dram[t], xc).then_inc(stored, 16)

            def tile(t, b, q):
                if not early(t, 2):
                    sp.wait_ge(scored, TC * (t - 1))
                sp.dma_start(adj_in[b], adj[t]).then_inc(adj_loaded[b], 16)
                if not early(t, 2):
                    store(t - 2)
            pairs(sp, tile)
            store(T - 2)
            store(T - 1)
            sp.wait_ge(stored, 16 * T)

        @block.vector
        def _(dve):
            finish_steps = Steps(dve, finish_step, 2)

            def find_off_edge(t, b, q, p):
                dve.wait_ge(adj_loaded[b], 16 * (q + 1))
                if not (early(t, 1) and p == 0):
                    dve.wait_ge(masked, CH * t + p)
                nc.vector.tensor_scalar(off_edge, adj_in[b][:, PIECE * p:PIECE * (p + 1)], 0.0, MASKED,
                                        ALU.is_equal, ALU.mult).then_inc(off_edge_built, 1)

            def mask(t, b, p):
                dve.wait_ge(off_edge_built, CH * t + p + 1)
                piece = adj_in[b][:, PIECE * p:PIECE * (p + 1)]
                nc.vector.tensor_tensor(piece, piece, off_edge, ALU.add).then_inc(masked, 1)

            def score(t, b, n):
                dve.wait_ge(tanh_done, TC * t + n + 1)
                dve.wait_ge(masked, CH * t + 2 * (n % NG) + 2)
                c = columns(n)
                nc.vector.scalar_tensor_tensor(e[n // NG][:, c], e[n // NG][:, c], TANH_ONE, adj_in[b][:, c],
                                               ALU.add, ALU.mult).then_inc(scored, 1)

            def find_top(t, n):
                if n % NG == 0 and not (early(t, 1) and n == 0):
                    dve.wait_ge(top_joined, HEADS * t + n // NG)
                dve.wait_ge(scored, TC * t + n + 1)
                nc.vector.tensor_reduce(tops[:, n % NG:n % NG + 1], e[n // NG][:, columns(n)], AX_X,
                                        ALU.max).then_inc(top_found, 1)

            def join_tops(t, b, h):
                dve.wait_ge(top_found, TC * t + NG * (h + 1))
                if not (early(t, 1) and h == 0):
                    dve.wait_ge(neg_top_built, HEADS * t + h)
                nc.vector.tensor_reduce(top, tops, AX_X, ALU.max).then_inc(top_joined, 1)
                dve.wait_ge(top_joined, HEADS * t + h + 1)
                if h == 0 and not early(t, 2):
                    dve.wait_ge(exp_done, TC * (t - 1))
                    dve.wait_ge(neg_top_kept, t - 1)
                nc.vector.tensor_scalar(neg_top_now[b][:, h:h + 1], top, -0.5, -MASKED * 1e-8, ALU.mult,
                                        ALU.min).then_inc(neg_top_built, 1)
                if h == HEADS - 1:
                    dve.wait_ge(neg_top_built, HEADS * (t + 1))
                    nc.vector.tensor_copy(m.neg_top[:, t, :], neg_top_now[b]).then_inc(neg_top_kept, 1)

            def fetch_neg_top(t, b):
                if not early(t, 2):
                    dve.wait_ge(exp_done, TC * (t - 1))
                nc.vector.tensor_copy(neg_top_now[b], m.neg_top[:, t, :]).then_inc(neg_top_built, 1)

            def finish(t, h):
                finish_steps.tile(HEADS * t + h)
                dve.wait_ge(used, TC * t + NG * (h + 1))
                if not (early(t, 1) and h == 0):
                    dve.wait_ge(agg_read, HEADS * t + h)
                finish_steps(nc.vector.tensor_scalar(den, agg[h][:, DH:DH + 1], 1e-30, None, ALU.max))
                finish_steps(nc.vector.reciprocal(den, den))
                if h == 0 and not early(t, 1):
                    dve.wait_ge(stored, 16 * t)
                nc.vector.tensor_scalar(xc[:, DH * h:DH * h + DH], agg[h][:, 0:DH], den, None,
                                        ALU.mult).then_inc(agg_read, 1)

            def find_tops(t, b, n):
                if not first:
                    if n == 0:
                        fetch_neg_top(t, b)
                    return
                if n % NG > 0:
                    find_top(t, n - 1)
                if n % NG == NG - 1:
                    find_top(t, n)
                    join_tops(t, b, n // NG)

            def step(t, b, q, n):
                turn_t, turn_n = ahead(t, n, 2)
                if turn_n in on_vector:
                    copy_out(dve, nc.vector.tensor_copy, copied_by_vector, turn_t, turn_n)
                masks = exists(t + 1) and n < CH
                if masks:
                    find_off_edge(t + 1, 1 - b, q + b, n)
                score_t, score_n = ahead(t, n, SCORE_AHEAD)
                score_b = b if score_n > n else 1 - b
                if exists(score_t):
                    score(score_t, score_b, score_n)
                if masks:
                    mask(t + 1, 1 - b, n)
                if exists(score_t):
                    find_tops(score_t, score_b, score_n)
                if n % NG == 1:
                    done_t, done_n = ahead(t, n, -NG)
                    if exists(done_t):
                        finish(done_t, done_n // NG)

            for p in range(CH):
                find_off_edge(0, 0, 0, p)
                mask(0, 0, p)
            for n in range(SCORE_AHEAD):
                score(0, 0, n)
                find_tops(0, 0, n)
            for n in range(2):
                if n in on_vector:
                    copy_out(dve, nc.vector.tensor_copy, copied_by_vector, 0, n)

            def tile(t, b, q):
                for n in range(TC):
                    step(t, b, q, n)
            pairs(dve, tile)
            finish(T - 1, HEADS - 1)

        @block.scalar
        def _(act):
            def fetch_f1(t, b):
                if not early(t, 2):
                    act.wait_ge(tanh_done, TC * (t - 1))
                nc.scalar.copy(f1_now[b], m.f1[:, t, :]).then_inc(f1_fetched, 1)

            def both(n):
                return slice(GW * (n % NG), GW * (n % NG + 2))

            def tanh(t, b, n):
                if n == 0:
                    act.wait_ge(f1_fetched, t + 1)
                if not early(t, 1):
                    act.wait_ge(turn_done, TC * (t - 1) + n + 2)
                h, c = n // NG, both(n)
                nc.scalar.activation(e[h][:, c], m.f2[:, h, c], ACT.Tanh, bias=f1_now[b][:, h:h + 1],
                                     scale=0.5).then_inc(tanh_done, 2)

            def exp(t, b, n):
                h, c = n // NG, both(n)
                if first:
                    act.wait_ge(neg_top_built, HEADS * t + h + 1)
                elif n == 0:
                    act.wait_ge(neg_top_built, t + 1)
                act.wait_ge(scored, TC * t + n + 2)
                nc.scalar.activation(e[h][:, c], e[h][:, c], ACT.Exp, bias=neg_top_now[b][:, h:h + 1],
                                     scale=0.5).then_inc(exp_done, 2)

            def copy(t, n):
                if n in on_scalar:
                    copy_out(act, nc.scalar.copy, copied_by_scalar, t, n)

            fetch_f1(0, 0)
            for n in range(0, TANH_AHEAD, 2):
                tanh(0, 0, n)
            for n in range(0, EXP_AHEAD, 2):
                exp(0, 0, n)
            copy(0, 0)
            copy(0, 1)

            def tile(t, b, q):
                for n in range(TC):
                    copy(*ahead(t, n, 2))
                    if n == 0 and exists(t + 1):
                        fetch_f1(t + 1, 1 - b)
                    if n % 2 == 0:
                        exp_t, exp_n = ahead(t, n, EXP_AHEAD)
                        if exists(exp_t):
                            exp(exp_t, b if exp_n > n else 1 - b, exp_n)
                    else:
                        tanh_t, tanh_n = ahead(t, n, TANH_AHEAD)
                        if exists(tanh_t):
                            tanh(tanh_t, 1 - b, tanh_n)
            pairs(act, tile)

        @block.tensor
        def _(pe):
            def turn(t, n):
                if not exists(t):
                    return
                pe.wait_ge(exp_done, TC * t + n + 1)
                if n >= 3:
                    wait_copied(pe, t, n - 3)
                elif not early(t, 1):
                    wait_copied(pe, t - 1, TC - 1 if n == 0 else TC - 4 + n)
                for k in range(GROUP):
                    at = GW * (n % NG) + P * k
                    mm = nc.tensor.transpose(turned[n % 3][:, k, :], e[n // NG][:, at:at + P], m.ident[:])
                mm.then_inc(turn_done, 1)

            def aggregate(t, n):
                h = n // NG
                if n % NG == 0 and not (early(t, 1) and h < 2):
                    pe.wait_ge(agg_read, HEADS * t + h - 1)
                wait_copied(pe, t, n)
                for k in range(GROUP):
                    j = GROUP * (n % NG) + k
                    mm = nc.tensor.matmul(agg[h], eT[n % 2][:, k, :], m.feats[:, j, h, :],
                                          start=(j == 0), stop=(j == T - 1))
                mm.then_inc(used, 1)

            turn(0, 0)
            turn(0, 1)

            def tile(t, b, q):
                for n in range(TC):
                    turn(*ahead(t, n, 2))
                    aggregate(t, n)
            pairs(pe, tile)

def turn_nodes(nc, m, name, src, dst, to_rows, load=None, extra=None, by_head=False):
    PER = BANK // P
    STEPS = KC * T // PER
    bank = [m.banks[:, i, :].rearrange("p (k i) -> p k i", k=PER) for i in range(8)]
    loaded = m.sems(name + "_loaded", 4)
    extra_loaded = m.sem(name + "_extra_loaded")
    turned = m.sem(name + "_turned")
    copied = m.sems(name + "_copied", 2)
    QT = T // 4

    def contents(k):
        if by_head:
            return m.banks[:, k % 8, :].rearrange("p (t h n) -> p t h n", h=HEADS, n=DH)
        return bank[k % 8]

    def blocks(k):
        if to_rows:
            t = k * PER // KC
            to = dst[:, t:t + PER // KC]
            to = to[:, :, :, 0:DH] if by_head else to.rearrange("p t (c i) -> p (t c) i", c=KC)
            return [(t + i // KC, i % KC) for i in range(PER)], to
        t, c = PER * (k // KC), k % KC
        return [(t + i, c) for i in range(PER)], dst[:, c, P * t:P * (t + PER)].rearrange(
            "p (k i) -> p k i", k=PER)

    with nc.Block() as block:
        @block.sync
        def _(sp):
            if load is not None:
                for i in range(4):
                    sp.dma_start(load[1][:, QT * i:QT * (i + 1), :],
                                 load[0][QT * i:QT * (i + 1)].rearrange("t p d -> p t d")).then_inc(loaded[i], 16)
            if extra is not None:
                sp.dma_start(extra[1], extra[0].rearrange("t p d -> p t d")).then_inc(extra_loaded, 16)
                sp.wait_ge(extra_loaded, 16)

        @block.tensor
        def _(pe):
            for k in range(STEPS):
                where, _ = blocks(k)
                if load is not None and k % (STEPS // 4) == 0:
                    pe.wait_ge(loaded[k // (STEPS // 4)], 16)
                if k >= 8:
                    pe.wait_ge(copied[k % 2], (k - 8) // 2 + 1)
                for i, (t, c) in enumerate(where):
                    block_in = src[:, c, P * t:P * t + P] if to_rows else src[:, t, P * c:P * c + P]
                    mm = nc.tensor.transpose(bank[k % 8][:, i, :], block_in, m.ident[:])
                mm.then_inc(turned, 1)

        @block.vector
        def _(dve):
            for k in range(0, STEPS, 2):
                dve.wait_ge(turned, k + 1)
                nc.vector.tensor_copy(blocks(k)[1], contents(k)).then_inc(copied[0], 1)
            dve.wait_ge(copied[0], STEPS // 2)

        @block.scalar
        def _(act):
            for k in range(1, STEPS, 2):
                act.wait_ge(turned, k + 1)
                nc.scalar.copy(blocks(k)[1], contents(k)).then_inc(copied[1], 1)
            act.wait_ge(copied[1], STEPS // 2)


def batch_norm(nc, m, name, data, gamma, beta):
    stats = m.weights[:, 0:KC * CH * 6].rearrange("p (c n k) -> p c n k", c=KC, n=CH)
    mv = m.weights[:, 100:100 + 2 * KC].rearrange("p (c k) -> p c k", c=KC)
    sd = m.weights[:, 110:110 + KC]
    scale = m.weights[:, 112:112 + KC]
    shift = m.weights[:, 114:114 + KC]
    measured = m.sem(name + "_measured")
    var_built = m.sem(name + "_var_built")
    sd_built = m.sem(name + "_sd_built")
    affine = m.sem(name + "_affine")
    applied = m.sem(name + "_applied")
    with nc.Block() as block:
        @block.vector
        def _(dve):
            for c in range(KC):
                for n in range(CH):
                    nc.vector.bn_stats(stats[:, c, n, :], data[:, c, BANK * n:BANK * (n + 1)]).then_inc(measured, 1)
            dve.wait_ge(measured, KC * CH)
            for c in range(KC):
                nc.vector.bn_aggr(mv[:, c, :], stats[:, c, :, :].rearrange("p n k -> p (n k)")).then_inc(
                    var_built, 1)
            dve.wait_ge(sd_built, 1)
            nc.vector.reciprocal(sd, sd).then_inc(affine, 1)
            dve.wait_ge(affine, 1)
            nc.vector.tensor_tensor(scale, sd, gamma, ALU.mult).then_inc(affine, 1)
            dve.wait_ge(affine, 2)
            dve.wait_ge(var_built, KC)
            nc.vector.tensor_tensor(shift, mv[:, :, 0], scale, ALU.mult).then_inc(affine, 1)
            dve.wait_ge(affine, 3)
            nc.vector.tensor_tensor(shift, beta, shift, ALU.subtract).then_inc(affine, 1)
            dve.wait_ge(affine, 4)
            nc.vector.tensor_scalar(data[:, 0, :], data[:, 0, :], scale[:, 0:1], shift[:, 0:1], ALU.mult,
                                    ALU.add).then_inc(applied, 1)

        @block.scalar
        def _(act):
            act.wait_ge(var_built, KC)
            nc.scalar.activation(sd, mv[:, :, 1], ACT.Sqrt, bias=m.eps[:, 1:2]).then_inc(sd_built, 1)
            act.wait_ge(affine, 4)
            nc.scalar.activation(data[:, 1, :], data[:, 1, :], ACT.Identity, bias=shift[:, 1:2],
                                 scale=scale[:, 1:2]).then_inc(applied, 1)
            act.wait_ge(applied, 2)


def dense(nc, m, name, src, dst, w_dram, bias, elu=False, residual=False, block_diagonal=False,
          scale=None, at=41088):
    w = m.weights[:, 0:KC * D].rearrange("p (c n) -> p c n", c=KC)
    low = [m.at(at + BANK * i, BANK) for i in range(2)]
    high = [m.at(at + 1024 + BANK * i, BANK) for i in range(2)]
    loaded = m.sem(name + "_loaded")
    multiplied = m.sem(name + "_multiplied")
    low_built = m.sem(name + "_low_built")
    low_exp = m.sem(name + "_low_exp")
    high_built = m.sem(name + "_high_built")
    joined = m.sem(name + "_joined")
    done = m.sem(name + "_done")
    steps = [(k // CH, slice(BANK * (k % CH), BANK * (k % CH + 1))) for k in range(KC * CH)]

    with nc.Block() as block:
        @block.sync
        def _(sp):
            sp.dma_start(w, w_dram.rearrange("c p n -> p c n")).then_inc(loaded, 16)

        @block.tensor
        def _(pe):
            pe.wait_ge(loaded, 16)
            for k, (o, nodes) in enumerate(steps):
                if k >= 4:
                    pe.wait_ge(high_built if elu else done, k - 3)
                chunks = [o] if block_diagonal else list(range(KC))
                for c in chunks:
                    mm = nc.tensor.matmul(m.banks[:, k % 4, :], w[:, c, P * o:P * o + P], src[:, c, nodes],
                                          start=(c == chunks[0]), stop=(c == chunks[-1]))
                mm.then_inc(multiplied, 1)

        @block.vector
        def _(dve):
            if elu:
                def join(k):
                    o, nodes = steps[k]
                    dve.wait_ge(low_exp, k + 1)
                    dve.wait_ge(high_built, k + 1)
                    to = high[k % 2] if residual else dst[:, o, nodes]
                    nc.vector.scalar_tensor_tensor(to, low[k % 2], -1.0, high[k % 2], ALU.add,
                                                   ALU.add).then_inc(joined, 1)
                    if residual:
                        dve.wait_ge(joined, k + 1)
                        nc.vector.tensor_tensor(dst[:, o, nodes], high[k % 2], src[:, o, nodes],
                                                ALU.add).then_inc(done, 1)

                for k, (o, nodes) in enumerate(steps):
                    dve.wait_ge(multiplied, k + 1)
                    if k >= 2:
                        dve.wait_ge(joined, k - 1)
                    b = 0.0 if bias is None else bias[:, o:o + 1]
                    nc.vector.tensor_scalar(low[k % 2], m.banks[:, k % 4, :], b, 0.0, ALU.add,
                                            ALU.min).then_inc(low_built, 1)
                    if k >= 1:
                        join(k - 1)
                join(len(steps) - 1)
                dve.wait_ge(done if residual else joined, len(steps))
            else:
                for k, (o, nodes) in enumerate(steps):
                    dve.wait_ge(multiplied, k + 1)
                    nc.vector.tensor_scalar(dst[:, o, nodes], m.banks[:, k % 4, :], bias[:, o:o + 1],
                                            1.0 if scale is None else scale, ALU.add, ALU.mult).then_inc(done, 1)
                dve.wait_ge(done, len(steps))

        @block.scalar
        def _(act):
            if elu:
                for k, (o, nodes) in enumerate(steps):
                    act.wait_ge(low_built, k + 1)
                    if k >= 2:
                        act.wait_ge(done if residual else joined, k - 1)
                    b = 0.0 if bias is None else bias[:, o:o + 1]
                    nc.scalar.activation(high[k % 2], m.banks[:, k % 4, :], ACT.Relu, bias=b).then_inc(
                        high_built, 1)
                    nc.scalar.activation(low[k % 2], low[k % 2], ACT.Exp).then_inc(low_exp, 1)
                act.wait_ge(low_exp, len(steps))


def layer_norm_rows(nc, m, rows, residual, x3_dram):
    stats = m.at(0, T, 6)
    mv = m.at(256, T, 2)
    sd = m.at(384, T)
    measured = m.sem("n3_measured")
    added = m.sem("n3_added")
    var_built = m.sem("n3_var_built")
    sd_built = m.sem("n3_sd_built")
    rs_built = m.sem("n3_rs_built")
    normalised = m.sem("n3_normalised")
    stored = m.sem("n3_stored")
    with nc.Block() as block:
        @block.vector
        def _(dve):
            nc.vector.tensor_tensor(rows, rows, residual, ALU.add).then_inc(added, 1)
            dve.wait_ge(added, 1)
            for t in range(T):
                nc.vector.bn_stats(stats[:, t, :], rows[:, t, :]).then_inc(measured, 1)
            dve.wait_ge(measured, T)
            for t in range(T):
                nc.vector.bn_aggr(mv[:, t, :], stats[:, t, :]).then_inc(var_built, 1)
            dve.wait_ge(sd_built, 1)
            nc.vector.reciprocal(sd, sd).then_inc(rs_built, 1)
            dve.wait_ge(rs_built, 1)
            dve.wait_ge(var_built, T)
            for t in range(T):
                nc.vector.tensor_scalar(rows[:, t, :], rows[:, t, :], mv[:, t, 0:1], sd[:, t:t + 1],
                                        ALU.subtract, ALU.mult).then_inc(normalised, 1)

        @block.scalar
        def _(act):
            act.wait_ge(var_built, T)
            nc.scalar.activation(sd, mv[:, :, 1], ACT.Sqrt, bias=m.eps[:, 0:1]).then_inc(sd_built, 1)

        @block.sync
        def _(sp):
            sp.wait_ge(normalised, T)
            sp.dma_start(x3_dram.rearrange("t p d -> p t d"), rows).then_inc(stored, 16)
            sp.wait_ge(stored, 16)


def values(nc, m, xT, w_dram, bv, v_rows):
    w = m.weights[:, 0:KC * D].rearrange("p (c n) -> p c n", c=KC)
    bias = m.at(41088, D)
    loaded = m.sem("v_loaded")
    multiplied = m.sem("v_multiplied")
    done = m.sem("v_done")
    with nc.Block() as block:
        @block.sync
        def _(sp):
            sp.dma_start(w, w_dram.rearrange("c p n -> p c n")).then_inc(loaded, 16)
            sp.dma_start(bias, bv.partition_broadcast(P)).then_inc(loaded, 16)

        @block.tensor
        def _(pe):
            pe.wait_ge(loaded, 32)
            for t in range(T):
                if t >= 8:
                    pe.wait_ge(done, t - 7)
                for c in range(KC):
                    mm = nc.tensor.matmul(m.banks[:, t % 8, 0:D], xT[:, c, P * t:P * t + P], w[:, c, :],
                                          start=(c == 0), stop=(c == KC - 1))
                mm.then_inc(multiplied, 1)

        @block.vector
        def _(dve):
            dve.wait_ge(loaded, 32)
            for t in range(T):
                dve.wait_ge(multiplied, t + 1)
                nc.vector.tensor_tensor(v_rows[:, t, :], m.banks[:, t % 8, 0:D], bias, ALU.add).then_inc(done, 1)
            dve.wait_ge(done, T)


def graph_ids(nc, m, ptr, q, q_dram, g_rows, g_cols):
    ptr_in = m.at(33000, NPTR).bitcast(I32)
    ptr_f = m.at(33100, NPTR)
    node = m.at(33200, T)
    at_most = m.at(33300, T, NPTR)
    spread = m.at(34400, T * P // 2).bitcast(BF16).rearrange("p (t i) -> p t i", t=T)
    loaded = m.sem("g_loaded")
    numbered = m.sem("g_numbered")
    step = m.sem("g_step")
    broadcast = m.sem("g_broadcast")
    copied = m.sem("g_copied")
    stored = m.sem("g_q_stored")
    with nc.Block() as block:
        @block.sync
        def _(sp):
            sp.dma_start(ptr_in, ptr.partition_broadcast(P)).then_inc(loaded, 16)
            for c in range(KC):
                sp.dma_start(q_dram.rearrange("t p c n -> c p t n")[c],
                             q[:, c, :].rearrange("p (t n) -> p t n", t=T)).then_inc(stored, 16)
            sp.wait_ge(stored, 16 * KC)

        @block.gpsimd
        def _(pool):
            nc.gpsimd.iota(node, pattern=[[P, T]], base=0, channel_multiplier=1,
                           allow_small_or_imprecise_dtypes=True).then_inc(numbered, 1)

        @block.vector
        def _(dve):
            dve.wait_ge(loaded, 16)
            nc.vector.tensor_copy(ptr_f, ptr_in).then_inc(step, 1)
            dve.wait_ge(step, 1)
            dve.wait_ge(numbered, 1)
            nc.vector.tensor_tensor(at_most, node.unsqueeze(2).to_broadcast([P, T, NPTR]),
                                    ptr_f.unsqueeze(1).to_broadcast([P, T, NPTR]), ALU.is_ge).then_inc(step, 1)
            dve.wait_ge(step, 2)
            nc.vector.tensor_reduce(g_cols, at_most, AX_X, ALU.add).then_inc(step, 1)
            dve.wait_ge(step, 3)
            nc.vector.tensor_tensor(spread, m.ident[:].unsqueeze(1).to_broadcast([P, T, P]),
                                    g_cols.unsqueeze(2).to_broadcast([P, T, P]), ALU.mult).then_inc(step, 1)
            for n in range(CH):
                dve.wait_ge(broadcast, n + 1)
                nc.vector.tensor_copy(g_rows[:, BANK * n:BANK * (n + 1)], m.banks[:, n, :]).then_inc(copied, 1)
            dve.wait_ge(copied, CH)

        @block.tensor
        def _(pe):
            pe.wait_ge(step, 4)
            for n in range(CH):
                nc.tensor.matmul(m.banks[:, n, :], m.ones_bf[:], spread[:, 4 * n:4 * n + 4, :],
                                 start=True, stop=True).then_inc(broadcast, 1)


def layer3(nc, m, adj, q_dram, x3_dram, kT, v_rows, g_rows, out):
    plain = m.at(12416, N)
    s = [m.at(16512 + N * b, N) for b in range(2)]
    adj_in = [m.at(32896 + N * b, N) for b in range(2)]
    eT = [m.at(41088 + GW * i, GROUP, P) for i in range(2)]
    q_in = [m.at(43136 + D * b, KC, P) for b in range(2)]
    x3_in = [m.at(43648 + D * b, D) for b in range(2)]
    top = m.at(44160, 2)
    row_sum = m.small[:, T:2 * T].rearrange("p (t k) -> p t k", t=T)
    rden = m.at(44168, 1)
    post = Post(m, 44200, m.banks[:, 7, 0:D], "l3")
    qk = [m.banks[:, 2 * i:2 * i + 2, :].rearrange("p a n -> p (a n)") for i in range(2)]
    turned = m.banks[:, 4:6, :].rearrange("p a (b i) -> p (a b) i", i=P)
    agg = [m.banks[:, 6 + b, 0:D] for b in range(2)]

    in_loaded = m.sems("l3_in_loaded", 2)
    x3_loaded = m.sems("l3_x3_loaded", 2)
    qk_done = m.sem("l3_qk_done")
    qk_read = m.sem("l3_qk_read")
    in_graph_built = m.sem("l3_in_graph_built")
    plain_built = m.sem("l3_plain_built")
    top_found = m.sem("l3_top_found")
    neg_top_built = m.sem("l3_neg_top_built")
    exp_done = m.sem("l3_exp_done")
    masked = m.sem("l3_masked")
    turn_done = m.sem("l3_turn_done")
    copied = m.sem("l3_copied")
    used = m.sem("l3_used")
    post_step = m.sem("l3_post_step")
    stored = m.sem("l3_stored")

    with nc.Block() as block:
        @block.sync
        def _(sp):
            def tile(t, b, q):
                if not early(t, 2):
                    sp.wait_ge(qk_done, NG * (t - 1))
                    sp.wait_ge(plain_built, t - 1)
                sp.dma_start(q_in[b], q_dram[t]).then_inc(in_loaded[b], 16)
                sp.dma_start(adj_in[b], adj[t]).then_inc(in_loaded[b], 16)
                if not early(t, 1):
                    load_x3(t - 1, 1 - b)

            def load_x3(t, b):
                if not early(t, 2):
                    sp.wait_ge(post.normalised, t - 1)
                sp.dma_start(x3_in[b], x3_dram[t]).then_inc(x3_loaded[b], 16)
            pairs(sp, tile)
            load_x3(T - 1, 1)

        @block.vector
        def _(dve):
            post_steps = Steps(dve, post_step, 4)

            def build_plain(t, b, q):
                g = m.g_cols.unsqueeze(2)[:, t, :]
                if not early(t, 1):
                    dve.wait_ge(top_found, t)
                nc.vector.tensor_scalar(plain, g_rows, g, 2.0 - 2.0 * OFF_GRAPH, ALU.is_equal,
                                        ALU.mult).then_inc(in_graph_built, 1)
                dve.wait_ge(in_graph_built, t + 1)
                dve.wait_ge(in_loaded[b], 32 * (q + 1))
                nc.vector.scalar_tensor_tensor(plain, plain, 2.0 * OFF_GRAPH, adj_in[b], ALU.add,
                                               ALU.mult).then_inc(plain_built, 1)

            def score(t, b):
                g = m.g_cols.unsqueeze(2)[:, t, :]
                for c in range(NG):
                    dve.wait_ge(qk_done, NG * t + c + 1)
                    if c == 0 and not early(t, 2):
                        dve.wait_ge(turn_done, NG * (t - 1))
                    nodes = slice(GW * c, GW * (c + 1))
                    nc.vector.scalar_tensor_tensor(s[b][:, nodes], g_rows[:, nodes], g, qk[c % 2],
                                                   ALU.is_equal, ALU.mult).then_inc(qk_read, 1)
                dve.wait_ge(qk_read, NG * (t + 1))
                dve.wait_ge(plain_built, t + 1)
                if not early(t, 1):
                    dve.wait_ge(neg_top_built, t)
                nc.vector.memset(post.spare, 0.0)
                nc.vector.tensor_tensor_reduce(s[b], s[b], plain, 1.0, -3.0e38, ALU.add, ALU.max,
                                               top[:, 0:1]).then_inc(top_found, 1)
                dve.wait_ge(top_found, t + 1)
                if not early(t, 1):
                    dve.wait_ge(exp_done, t)
                nc.vector.tensor_scalar(top[:, 1:2], top[:, 0:1], -1.0, None, ALU.mult).then_inc(neg_top_built, 1)

            def mask(t, b):
                g = m.g_cols.unsqueeze(2)[:, t, :]
                dve.wait_ge(exp_done, t + 1)
                nc.vector.scalar_tensor_tensor(s[b], g_rows, g, s[b], ALU.is_equal, ALU.mult).then_inc(masked, 1)

            def finish(t, b, q):
                post_steps.tile(t)
                dve.wait_ge(used, NG * (t + 1))
                dve.wait_ge(x3_loaded[b], 16 * (q + 1))
                if not early(t, 1):
                    dve.wait_ge(post.normalised, t)
                post_steps(nc.vector.reciprocal(rden, row_sum[:, t, :]))
                post_steps(nc.vector.scalar_tensor_tensor(post.pre, agg[b], rden, x3_in[b], ALU.mult, ALU.add))
                if not early(t, 1):
                    dve.wait_ge(stored, 16 * t)
                post.normalise(nc, dve, post_steps, t, used=stored)

            build_plain(0, 0, 0)
            score(0, 0)
            build_plain(1, 1, 0)
            mask(0, 0)

            def tile(t, b, q):
                if not late(t, 1):
                    score(t + 1, 1 - b)
                if not early(t, 1):
                    finish(t - 1, 1 - b, q if b else q - 1)
                if not late(t, 2):
                    build_plain(t + 2, b, q + 1)
                if not late(t, 1):
                    mask(t + 1, 1 - b)
            pairs(dve, tile)
            finish(T - 1, 1, T // 2 - 1)

        @block.scalar
        def _(act):
            def exp(t, b):
                act.wait_ge(neg_top_built, t + 1)
                nc.scalar.activation(s[b], s[b], ACT.Exp, bias=top[:, 1:2], accum_out=row_sum[:, t, :]).then_inc(
                    exp_done, 1)

            def finish(t):
                post.deviation(nc, act, t, m.eps[:, 0:1])
                act.wait_ge(post.normalised, t + 1)
                act.dma_start(out[t], post.xn).then_inc(stored, 16)

            exp(0, 0)

            def tile(t, b, q):
                for g in range(NG):
                    act.wait_ge(turn_done, NG * t + g + 1)
                    if not (early(t, 1) and g < 2):
                        act.wait_ge(used, NG * t + g - 1)
                    nc.scalar.copy(eT[g % 2], turned).then_inc(copied, 1)
                if not late(t, 1):
                    exp(t + 1, 1 - b)
                if not early(t, 1):
                    finish(t - 1)
            pairs(act, tile)
            finish(T - 1)
            act.wait_ge(stored, 16 * T)

        @block.tensor
        def _(pe):
            def scores(t, b, q, c):
                if c == 0:
                    pe.wait_ge(in_loaded[b], 32 * (q + 1))
                if not (early(t, 1) and c < 2):
                    pe.wait_ge(qk_read, NG * t + c - 1)
                for half in range(2):
                    for k in range(KC):
                        n = GW * c + BANK * half
                        mm = nc.tensor.matmul(qk[c % 2][:, BANK * half:BANK * (half + 1)], q_in[b][:, k, :],
                                              kT[:, k, n:n + BANK], start=(k == 0), stop=(k == KC - 1))
                mm.then_inc(qk_done, 1)

            def turn(t, b, g):
                if g == 0:
                    pe.wait_ge(masked, t + 1)
                if not (early(t, 1) and g == 0):
                    pe.wait_ge(copied, NG * t + g)
                for k in range(GROUP):
                    j = GROUP * g + k
                    mm = nc.tensor.transpose(turned[:, k, :], s[b][:, P * j:P * j + P], m.ident[:])
                mm.then_inc(turn_done, 1)

            def aggregate(t, b, g):
                if g == 0 and not early(t, 2):
                    pe.wait_ge(post.normalised, t - 1)
                pe.wait_ge(copied, NG * t + g + 1)
                for k in range(GROUP):
                    j = GROUP * g + k
                    mm = nc.tensor.matmul(agg[b], eT[g % 2][:, k, :], v_rows[:, j, :],
                                          start=(j == 0), stop=(j == T - 1))
                mm.then_inc(used, 1)

            for c in range(NG):
                scores(0, 0, 0, c)

            def tile(t, b, q):
                more = not late(t, 1)
                q_next = q if b == 0 else q + 1
                if more:
                    scores(t + 1, 1 - b, q_next, 0)
                    scores(t + 1, 1 - b, q_next, 1)
                turn(t, b, 0)
                if more:
                    scores(t + 1, 1 - b, q_next, 2)
                turn(t, b, 1)
                if more:
                    scores(t + 1, 1 - b, q_next, 3)
                aggregate(t, b, 0)
                turn(t, b, 2)
                aggregate(t, b, 1)
                turn(t, b, 3)
                aggregate(t, b, 2)
                aggregate(t, b, 3)
            pairs(pe, tile)


PARAMS = ["enc_bn_gamma", "enc_bn_beta", "enc_mlp_b", "enc_mlp_bn_gamma", "enc_mlp_bn_beta",
          "dec_mlp_b", "dec_mlp_bn_gamma", "dec_mlp_bn_beta", "bq", "bk"]


def program(nc, x, adj, adjT_blocks, w1, b1, wbd, wbdT, vbd, params, w_enc, w_dec, wq, wk, wv, wdec_head,
            bv, ptr, out):
    def scratch(name, *shape):
        return nc.dram_tensor(name, shape, F32).ap()
    x2_dram = scratch("x2_scratch", T, P, D)
    xc_dram = scratch("xc_scratch", T, P, D)
    x3_dram = scratch("x3_scratch", T, P, D)
    q_dram = scratch("q_scratch", T, P, KC, P)
    with ExitStack() as ctx:
        m = Memory(nc, ctx)
        m.h = m.at(8320, T, D)
        m.x1 = m.at(16512, T, D)
        m.feats = m.at(0, T, HEADS, DH + 1)
        m.values = m.at(0, T, D)
        m.f2 = m.at(32896, HEADS, N)
        m.f1 = m.small[:, 0:P].rearrange("p (t h) -> p t h", t=T)
        m.neg_top = m.small[:, P:2 * P].rearrange("p (t h) -> p t h", t=T)
        m.g_cols = m.small[:, 0:T]
        m.wext = m.weights[:, 0:KC * (P + 4)].rearrange("p (c n) -> p c n", c=KC)
        m.wv_rows = m.weights[:, KC * (P + 4):KC * (P + 4) + HEADS * P].rearrange("p (h n) -> p h n", h=HEADS)
        param = {k: m.params[:, KC * i:KC * (i + 1)] for i, k in enumerate(PARAMS)}
        rows = lambda start: m.at(start, T, D)
        cols = lambda start: m.at(start, KC, N)
        A, B, C, E = 8320, 16512, 24704, 32896

        constants(nc, m, params)
        layer0(nc, m, x, adjT_blocks, w1)
        layer2_weights(nc, m, wbd, wbdT, vbd)
        layer1(nc, m, adjT_blocks, b1, x2_dram)

        m.clear_semaphores()
        attention(nc, m, adj, xc_dram, "a1", True)
        turn_nodes(nc, m, "t1", rows(A), cols(B), False, load=(xc_dram, rows(A)))
        batch_norm(nc, m, "n1", cols(B), param["enc_bn_gamma"], param["enc_bn_beta"])
        dense(nc, m, "d1", cols(B), cols(C), w_enc, param["enc_mlp_b"], elu=True, residual=True, at=A)
        batch_norm(nc, m, "n2", cols(C), param["enc_mlp_bn_gamma"], param["enc_mlp_bn_beta"])
        turn_nodes(nc, m, "t2", cols(C), m.feats, True, by_head=True)

        m.clear_semaphores()
        attention(nc, m, adj, xc_dram, "a2", False)
        turn_nodes(nc, m, "t3", rows(A), cols(B), False, load=(xc_dram, rows(A)), extra=(x2_dram, rows(E)))
        dense(nc, m, "d2", cols(B), cols(C), wdec_head, None, elu=True, block_diagonal=True)
        dense(nc, m, "d3", cols(C), cols(B), w_dec, param["dec_mlp_b"], elu=True, residual=True)
        batch_norm(nc, m, "n4", cols(B), param["dec_mlp_bn_gamma"], param["dec_mlp_bn_beta"])
        turn_nodes(nc, m, "t4", cols(B), rows(A), True)
        layer_norm_rows(nc, m, rows(A), rows(E), x3_dram)

        turn_nodes(nc, m, "t5", rows(A), cols(B), False)
        values(nc, m, cols(B), wv, bv, m.values)
        dense(nc, m, "d4", cols(B), cols(C), wk, param["bk"])
        dense(nc, m, "d5", cols(B), cols(A), wq, param["bq"], scale=1.0 / 16)
        g_rows = m.at(45400, N)
        graph_ids(nc, m, ptr, cols(A), q_dram, g_rows, m.g_cols)
        m.clear_semaphores()
        layer3(nc, m, adj, q_dram, x3_dram, cols(C), m.values, g_rows, out)


def kernel(**inputs):
    import numpy as np
    import concourse.bacc as bacc
    from concourse import mybir as mb
    from concourse.bass_utils import run_bass_kernel_spmd as run

    g = {k: np.asarray(v) for k, v in inputs.items()}
    adj = g["adj"]

    def block_diagonal(a):
        n = a.shape[2]
        o = np.zeros((KC, P, 2 * n), a.dtype)
        for h in range(HEADS):
            o[h // 2, DH * (h % 2):DH * (h % 2) + DH, n * (h % 2):n * (h % 2) + n] = a[h]
        return o

    v = block_diagonal(g["L2_gnn_V"][..., 0].transpose(0, 2, 1))
    params = np.stack([g["L3_gnn_" + k if k in ("bq", "bk") else "L2_gnn_" + k] for k in PARAMS])
    head_out = np.zeros((KC, P, D), adj.dtype)
    wT = block_diagonal(g["L2_gnn_W"].transpose(0, 2, 1))
    for c in range(KC):
        head_out[c, :, P * c:P * c + P] = wT[c]
    arrays = {
        "x": g["x"],
        "adj": adj.reshape(T, P, N),
        "adjT_blocks": adj.reshape(T, P, T, P).transpose(0, 3, 2, 1).reshape(T, P, N),
        "w1": g["L1_gnn_W"].transpose(1, 0, 2).reshape(D, D),
        "b1": g["L1_gnn_b"].reshape(D),
        "wbd": block_diagonal(g["L2_gnn_W"]),
        "wbdT": wT,
        "vbd": v[:, :, [0, 2, 1, 3]],
        "params": params.reshape(-1, P).T,
        "w_enc": g["L2_gnn_enc_mlp_W"].T.reshape(KC, P, D),
        "w_dec": g["L2_gnn_dec_mlp_W"].T.reshape(KC, P, D),
        "wq": g["L3_gnn_Wq"].T.reshape(KC, P, D),
        "wk": g["L3_gnn_Wk"].T.reshape(KC, P, D),
        "wv": g["L3_gnn_Wv"].T.reshape(KC, P, D),
        "w_head_out": head_out,
        "bv": g["L3_gnn_bv"],
        "ptr": g["L3_gnn_ptr"],
    }
    nc = bacc.Bacc("TRN2", target_bir_lowering=False, num_devices=1)
    maps, args = {}, []
    for name, a in arrays.items():
        maps[f"in_{name}"] = np.ascontiguousarray(a)
        args.append(nc.dram_tensor(f"in_{name}", a.shape, mb.dt.from_np(a.dtype), kind="ExternalInput").ap())
    args.append(nc.dram_tensor("out_dram", (T, P, D), mb.dt.float32, kind="ExternalOutput").ap())
    program(nc, *args)
    return run(nc, [maps], core_ids=[0]).results[0]["out_dram"].reshape(N, D)
```

```python
from contextlib import ExitStack

import concourse.bass as bass
from concourse import mybir

F32 = mybir.dt.float32
BF16 = mybir.dt.bfloat16
I32 = mybir.dt.int32
ALU = mybir.AluOpType
ACT = mybir.ActivationFunctionType
AX_X = mybir.AxisListType.X

P = 128
N = 4096
T = N // P
D = 256
KC = D // P
HEADS = 4
DH = D // HEADS
NPTR = 33
LN_EPS = 1e-5
BN_EPS = 1e-6
NORM_EPS = 1e-12
MASKED = -1.0e38
TANH_ONE = 1.0 + 2.0 ** -23
OFF_GRAPH = -1000000.0
BANK = 512
GROUP = 8
NG = T // GROUP
GW = GROUP * P
CH = N // BANK


class Steps:

    def __init__(self, eng, sem, per):
        self.eng, self.sem, self.per, self.k = eng, sem, per, per

    def tile(self, t):
        assert self.k == self.per, (self.k, self.per)
        self.base, self.k = t * self.per, 0

    def __call__(self, ins):
        self.k += 1
        ins.then_inc(self.sem, 1)
        self.eng.wait_ge(self.sem, self.base + self.k)


def early(t, n):
    return isinstance(t, int) and t < n


def late(t, n):
    return isinstance(t, int) and t >= T - n


def pairs(eng, tile):
    for q in (0,):
        tile(2 * q, 0, q)
        tile(2 * q + 1, 1, q)
    with eng.Fori(1, T // 2 - 1) as q:
        tile(2 * q, 0, q)
        tile(2 * q + 1, 1, q)
    for q in (T // 2 - 1,):
        tile(2 * q, 0, q)
        tile(2 * q + 1, 1, q)


def singles(eng, tile):
    tile(0)
    with eng.Fori(1, T - 1) as t:
        tile(t)
    tile(T - 1)


def quads(eng, tile):
    for b in range(4):
        tile(b, b, 0)
    with eng.Fori(1, T // 4 - 1) as q:
        for b in range(4):
            tile(4 * q + b, b, q)
    for b in range(4):
        tile(T - 4 + b, b, T // 4 - 1)


class Memory:

    def __init__(self, nc, ctx):
        self.nc, self.taken = nc, []
        sb = lambda name, shape, dt=F32: ctx.enter_context(nc.sbuf_tensor(name, shape, dt))
        self.arena = sb("arena", [P, 51328])
        self.ident = sb("ident", [P, P])
        self.ones_bf = sb("ones_bf", [P, P], BF16)
        self.eps = sb("eps", [P, 3])
        self.weights = sb("weights", [P, 1040])
        self.small = sb("small", [P, 384])
        self.params = sb("params", [P, 2 * 10])
        self.banks = ctx.enter_context(nc.psum_tensor("banks", [P, 8, BANK], F32))

    def at(self, start, *shape):
        n = 1
        for s in shape:
            n *= s
        v = self.arena[:, start:start + n]
        if len(shape) == 2:
            v = v.rearrange("p (a b) -> p a b", a=shape[0])
        if len(shape) == 3:
            v = v.rearrange("p (a b c) -> p a b c", a=shape[0], b=shape[1])
        return v

    def sem(self, name):
        self.taken.append(self.nc.alloc_semaphore(name))
        return self.taken[-1]

    def clear_semaphores(self):
        self.nc.clear_and_free_semaphores(self.taken)
        self.nc.all_engine_barrier()
        self.taken = []

    def sems(self, name, n):
        return [self.sem(f"{name}{i}") for i in range(n)]


def constants(nc, m, params):
    s_loaded = m.sem("c_loaded")
    s_ones = m.sem("c_ones")
    s_built = m.sem("c_built")
    with nc.Block() as block:
        @block.sync
        def _(sp):
            sp.dma_start(m.params[:], params).then_inc(s_loaded, 16)
            sp.wait_ge(s_loaded, 16)

        @block.vector
        def _(dve):
            nc.vector.memset(m.ident[:], 1.0).then_inc(s_ones, 1)
            nc.vector.memset(m.ones_bf[:], 1.0).then_inc(s_ones, 1)
            nc.vector.memset(m.eps[:, 0:1], LN_EPS).then_inc(s_ones, 1)
            nc.vector.memset(m.eps[:, 1:2], BN_EPS).then_inc(s_ones, 1)
            nc.vector.memset(m.eps[:, 2:3], -0.5).then_inc(s_ones, 1)
            dve.wait_ge(s_ones, 5)

        @block.gpsimd
        def _(pool):
            pool.wait_ge(s_ones, 1)
            nc.gpsimd.affine_select(out=m.ident[:], in_=m.ident[:], compare_op=ALU.is_equal, fill=0.0,
                                    base=0, pattern=[[-1, P]], channel_multiplier=1).then_inc(s_built, 1)
            pool.wait_ge(s_built, 1)


class Post:

    def __init__(self, m, at, bank, name):
        self.m = m
        self.pre = m.at(at, D)
        self.xn = m.at(at + 256, D)
        self.xnT = m.at(at + 512, KC, P)
        self.stats = m.at(at + 768, 6)
        self.mv = m.at(at + 776, 2)
        self.rs = m.at(at + 784, 1)
        self.spare = m.at(at + 788, 1)
        self.turned_bank = bank.rearrange("p (c n) -> p c n", c=KC)
        self.var_built = m.sem(name + "_var_built")
        self.eps_added = m.sem(name + "_eps_added")
        self.rs_built = m.sem(name + "_rs_built")
        self.normalised = m.sem(name + "_normalised")
        self.turned = m.sem(name + "_turned")
        self.copied = m.sem(name + "_turned_copied")

    def normalise(self, nc, dve, steps, t, used=None):
        steps(nc.vector.bn_stats(self.stats, self.pre))
        if not early(t, 1):
            dve.wait_ge(self.rs_built, t)
        nc.vector.memset(self.spare, 0.0)
        nc.vector.bn_aggr(self.mv, self.stats).then_inc(self.var_built, 1)
        dve.wait_ge(self.var_built, t + 1)
        dve.wait_ge(self.rs_built, t + 1)
        if used is None and not early(t, 1):
            dve.wait_ge(self.turned, t)
        nc.vector.tensor_scalar(self.xn, self.pre, self.mv[:, 0:1], self.rs, ALU.subtract,
                                ALU.mult).then_inc(self.normalised, 1)

    def deviation(self, nc, pool, t):
        pool.wait_ge(self.var_built, t + 1)
        if not early(t, 1):
            pool.wait_ge(self.normalised, t)
        nc.gpsimd.tensor_tensor(self.rs, self.mv[:, 1:2], self.m.eps[:, 0:1], ALU.add).then_inc(
            self.eps_added, 1)
        pool.wait_ge(self.eps_added, t + 1)
        nc.gpsimd.tensor_tensor(self.rs, self.rs, self.m.eps[:, 2:3], ALU.pow).then_inc(self.rs_built, 1)

    def turn(self, nc, pe, t):
        pe.wait_ge(self.normalised, t + 1)
        if not early(t, 1):
            pe.wait_ge(self.copied, t)
        for c in range(KC):
            mm = nc.tensor.transpose(self.turned_bank[:, c, :], self.xn[:, c * P:(c + 1) * P], self.m.ident[:])
        mm.then_inc(self.turned, 1)

    def copy_turned(self, nc, act, t, used):
        act.wait_ge(self.turned, t + 1)
        if not early(t, 1):
            act.wait_ge(used, t)
        nc.scalar.copy(self.xnT, self.turned_bank).then_inc(self.copied, 1)


def layer0(nc, m, x, adjT_blocks, w1):
    x_in = m.at(0, T, D + 1)
    adj_in = [m.at(24704 + 4096 * b, T, P) for b in range(2)]
    inc = [m.at(32896 + 4096 * b, T, P) for b in range(2)]
    mask = m.arena[:, 41088:43136].bitcast(BF16).rearrange("p (t i) -> p t i", t=T)
    rnorm = m.at(43136, P)
    w = m.weights[:, 0:KC * D].rearrange("p (c n) -> p c n", c=KC)
    counts = m.banks[:, 0, 0:P]
    agg = [m.banks[:, 1 + b, 0:D + 1] for b in range(2)]
    proj = m.banks[:, 4, 0:D]
    post = Post(m, 43264, m.banks[:, 3, 0:D], "l0")
    rdeg = m.at(43264 + 1024, 1)

    adj_loaded = m.sems("l0_adj_loaded", 2)
    m.first_loaded = m.sems("l1_adj_loaded", 2)
    x_loaded = m.sem("l0_x_loaded")
    w_loaded = m.sem("l0_w_loaded")
    ones_set = m.sem("l0_ones_set")
    mask_built = m.sem("l0_mask_built")
    counted = m.sem("l0_counted")
    norm_built = m.sem("l0_norm_built")
    inc_built = m.sem("l0_inc_built")
    agg_done = m.sem("l0_agg_done")
    x1_kept = m.sem("l0_x1_kept")
    proj_done = m.sem("l0_proj_done")
    proj_copied = m.sem("l0_proj_copied")
    inc_step = m.sem("l0_inc_step")
    post_step = m.sem("l0_post_step")

    with nc.Block() as block:
        @block.sync
        def _(sp):
            def tile(t, b, q):
                if not early(t, 2):
                    sp.wait_ge(inc_built, t - 1)
                sp.dma_start(adj_in[b], adjT_blocks[t].rearrange("p (j i) -> p j i", j=T)).then_inc(
                    adj_loaded[b], 16)
                if early(t, 1):
                    sp.wait_ge(adj_loaded[0], 16)
                    sp.dma_start(x_in[:, :, 0:D], x.rearrange("(t p) d -> p t d", p=P)).then_inc(x_loaded, 16)
                    sp.dma_start(w, w1.rearrange("(c p) n -> p c n", p=P)).then_inc(w_loaded, 16)
            pairs(sp, tile)
            for b in range(2):
                sp.wait_ge(inc_built, T - 1 + b)
                sp.dma_start(adj_in[b], adjT_blocks[b].rearrange("p (j i) -> p j i", j=T)).then_inc(
                    m.first_loaded[b], 16)

        @block.vector
        def _(dve):
            inc_steps = Steps(dve, inc_step, 3)
            post_steps = Steps(dve, post_step, 3)

            def build_mask(t, b, q):
                dve.wait_ge(adj_loaded[b], 16 * (q + 1))
                if not early(t, 1):
                    dve.wait_ge(counted, t)
                nc.vector.tensor_scalar(mask, adj_in[b], 0.0, None, ALU.is_gt).then_inc(mask_built, 1)

            def build_inc(t, b):
                inc_steps.tile(t)
                dve.wait_ge(norm_built, t + 1)
                inc_steps(nc.vector.tensor_scalar(rnorm, rnorm, NORM_EPS, None, ALU.max))
                inc_steps(nc.vector.reciprocal(rnorm, rnorm))
                if not early(t, 2):
                    dve.wait_ge(agg_done, t - 1)
                rnorm_all = rnorm.unsqueeze(1).to_broadcast([P, T, P])
                inc_steps(nc.vector.scalar_tensor_tensor(inc[b], adj_in[b], 0.0, rnorm_all,
                                                         ALU.is_gt, ALU.mult))
                nc.vector.tensor_tensor(inc[b], inc[b], adj_in[b], ALU.add).then_inc(inc_built, 1)

            def finish(t, b):
                post_steps.tile(t)
                dve.wait_ge(agg_done, t + 1)
                post_steps(nc.vector.reciprocal(rdeg, agg[b][:, D:D + 1]))
                post_steps(nc.vector.scalar_tensor_tensor(post.pre, agg[b][:, 0:D], rdeg, x_in[:, t, 0:D],
                                                          ALU.mult, ALU.add))
                if not early(t, 1):
                    dve.wait_ge(x1_kept, t)
                post.normalise(nc, dve, post_steps, t)

            nc.vector.memset(x_in[:, :, D:D + 1], 1.0).then_inc(ones_set, 1)
            dve.wait_ge(x_loaded, 16)
            build_mask(0, 0, 0)
            build_inc(0, 0)
            build_mask(1, 1, 0)

            def tile(t, b, q):
                if not early(t, 1):
                    finish(t - 1, 1 - b)
                if not late(t, 1):
                    build_inc(t + 1, 1 - b)
                if not late(t, 2):
                    build_mask(t + 2, b, q + 1)
            pairs(dve, tile)
            finish(T - 1, 1)

        @block.scalar
        def _(act):
            def norm(t):
                act.wait_ge(counted, t + 1)
                if not early(t, 1):
                    act.wait_ge(inc_built, t)
                nc.scalar.activation(rnorm, counts, ACT.Sqrt).then_inc(norm_built, 1)

            def finish(t):
                post.copy_turned(nc, act, t, proj_done)
                act.wait_ge(proj_done, t + 1)
                nc.scalar.copy(m.h[:, t, :], proj).then_inc(proj_copied, 1)

            norm(0)

            def tile(t, b, q):
                if not late(t, 1):
                    norm(t + 1)
                if not early(t, 1):
                    finish(t - 1)
            pairs(act, tile)
            finish(T - 1)
            act.wait_ge(proj_copied, T)

        @block.gpsimd
        def _(pool):
            def tile(t, b, q):
                post.deviation(nc, pool, t)
                pool.wait_ge(post.normalised, t + 1)
                nc.gpsimd.tensor_copy(m.x1[:, t, :], post.xn).then_inc(x1_kept, 1)
            pairs(pool, tile)
            pool.wait_ge(x1_kept, T)

        @block.tensor
        def _(pe):
            def count(t):
                pe.wait_ge(mask_built, t + 1)
                if not early(t, 1):
                    pe.wait_ge(norm_built, t)
                for j in range(T):
                    mm = nc.tensor.matmul(counts, m.ones_bf[:], mask[:, j, :], start=(j == 0), stop=(j == T - 1))
                mm.then_inc(counted, 1)

            def aggregate(t, b):
                pe.wait_ge(inc_built, t + 1)
                if not early(t, 2):
                    pe.wait_ge(post.normalised, t - 1)
                for j in range(T):
                    mm = nc.tensor.matmul(agg[b], inc[b][:, j, :], x_in[:, j, :],
                                          start=(j == 0), stop=(j == T - 1))
                mm.then_inc(agg_done, 1)

            def project(t):
                post.turn(nc, pe, t)
                if not early(t, 1):
                    pe.wait_ge(proj_copied, t)
                pe.wait_ge(post.copied, t + 1)
                for c in range(KC):
                    mm = nc.tensor.matmul(proj, post.xnT[:, c, :], w[:, c, :], start=(c == 0), stop=(c == KC - 1))
                mm.then_inc(proj_done, 1)

            pe.wait_ge(ones_set, 1)
            pe.wait_ge(x_loaded, 16)
            pe.wait_ge(w_loaded, 16)
            count(0)

            def tile(t, b, q):
                if not late(t, 1):
                    count(t + 1)
                aggregate(t, b)
                if not early(t, 1):
                    project(t - 1)
            pairs(pe, tile)
            project(T - 1)


def layer2_weights(nc, m, wbd, wbdT, vbd):
    wT = m.at(43264, KC, P)
    v = m.at(43520, KC, 4)
    prod = m.banks[:, 0, 0:KC * 4].rearrange("p (c k) -> p c k", c=KC)
    loaded = m.sem("lw_loaded")
    multiplied = m.sem("lw_multiplied")
    spread = m.sem("lw_spread")
    with nc.Block() as block:
        @block.sync
        def _(sp):
            sp.dma_start(m.wext[:, :, 0:P], wbd.rearrange("c p n -> p c n")).then_inc(loaded, 16)
            sp.dma_start(wT, wbdT.rearrange("c p n -> p c n")).then_inc(loaded, 16)
            sp.dma_start(v, vbd.rearrange("c p n -> p c n")).then_inc(loaded, 16)
            sp.wait_ge(loaded, 48)

        @block.tensor
        def _(pe):
            pe.wait_ge(loaded, 48)
            for c in range(KC):
                mm = nc.tensor.matmul(prod[:, c, :], wT[:, c, :], v[:, c, :], start=True, stop=True)
            mm.then_inc(multiplied, 1)

        @block.vector
        def _(dve):
            dve.wait_ge(multiplied, 1)
            dve.wait_ge(loaded, 48)
            nc.vector.tensor_copy(m.wext[:, :, P:P + 4], prod).then_inc(spread, 1)
            for h in range(HEADS):
                col = prod[:, h // 2, 2 + h % 2:3 + h % 2]
                nc.vector.tensor_copy(m.wv_rows[:, h, :], col.to_broadcast([P, P])).then_inc(spread, 1)
            nc.vector.memset(m.feats[:, :, :, DH:DH + 1], 1.0).then_inc(spread, 1)
            dve.wait_ge(spread, 2 + HEADS)


def layer1(nc, m, adjT_blocks, b1, x2_dram):
    adj_in = [m.at(24704 + 4096 * b, T, P) for b in range(2)]
    bias = m.at(50400, D)
    agg = [m.banks[:, 1 + b, 0:D] for b in range(2)]
    proj = m.banks[:, 4, 0:KC * (P + 4)].rearrange("p (c k) -> p c k", c=KC)
    f2_rows = m.banks[:, 5, :].rearrange("p (h n) -> p h n", h=HEADS)
    post = Post(m, 49280, m.banks[:, 3, 0:D], "l1")

    adj_loaded = m.first_loaded
    bias_loaded = m.sem("l1_bias_loaded")
    agg_done = m.sem("l1_agg_done")
    x2_stored = m.sem("l1_x2_stored")
    proj_done = m.sem("l1_proj_done")
    proj_copied = m.sem("l1_proj_copied")
    post_step = m.sem("l1_post_step")

    with nc.Block() as block:
        @block.sync
        def _(sp):
            sp.dma_start(bias, b1.partition_broadcast(P)).then_inc(bias_loaded, 16)

            def tile(t, b, q):
                if early(t, 2):
                    return
                sp.wait_ge(agg_done, t - 1)
                sp.dma_start(adj_in[b], adjT_blocks[t].rearrange("p (j i) -> p j i", j=T)).then_inc(
                    adj_loaded[b], 16)
            pairs(sp, tile)

        @block.vector
        def _(dve):
            post_steps = Steps(dve, post_step, 3)
            dve.wait_ge(bias_loaded, 16)

            def tile(t, b, q):
                post_steps.tile(t)
                dve.wait_ge(agg_done, t + 1)
                if not early(t, 1):
                    dve.wait_ge(post.normalised, t)
                post_steps(nc.vector.tensor_tensor(post.pre, agg[b], bias, ALU.add))
                post_steps(nc.vector.tensor_tensor(post.pre, post.pre, m.x1[:, t, :], ALU.add))
                if not early(t, 1):
                    dve.wait_ge(x2_stored, 16 * t)
                post.normalise(nc, dve, post_steps, t)
            pairs(dve, tile)

        @block.scalar
        def _(act):
            def tile(t, b, q):
                act.wait_ge(post.normalised, t + 1)
                act.dma_start(x2_dram[t], post.xn).then_inc(x2_stored, 16)
                post.copy_turned(nc, act, t, proj_done)
                act.wait_ge(proj_done, t + 1)
                nc.scalar.copy(m.feats[:, t, :, 0:DH].rearrange("p (c k) n -> p c k n", c=KC),
                               proj[:, :, 0:P].rearrange("p c (k n) -> p c k n", k=2))
                nc.scalar.mul(m.f1[:, t, :].rearrange("p (c n) -> p c n", c=KC), proj[:, :, P:P + 2], 0.5)
                nc.scalar.copy(m.f2.rearrange("p h (t n) -> p h t n", t=T)[:, :, t, :], f2_rows).then_inc(
                    proj_copied, 1)
            pairs(act, tile)
            act.wait_ge(proj_copied, T)
            act.wait_ge(x2_stored, 16 * T)

        @block.gpsimd
        def _(pool):
            pairs(pool, lambda t, b, q: post.deviation(nc, pool, t))

        @block.tensor
        def _(pe):
            def aggregate(t, b, q):
                pe.wait_ge(adj_loaded[b], 16 * (q + 1))
                if not early(t, 2):
                    pe.wait_ge(post.normalised, t - 1)
                for j in range(T):
                    mm = nc.tensor.matmul(agg[b], adj_in[b][:, j, :], m.h[:, j, :],
                                          start=(j == 0), stop=(j == T - 1))
                mm.then_inc(agg_done, 1)

            def project(t):
                post.turn(nc, pe, t)
                if not early(t, 1):
                    pe.wait_ge(proj_copied, t)
                pe.wait_ge(post.copied, t + 1)
                for c in range(KC):
                    nc.tensor.matmul(proj[:, c, :], post.xnT[:, c, :], m.wext[:, c, :], start=True, stop=True)
                for h in range(HEADS):
                    mm = nc.tensor.matmul(f2_rows[:, h, :], m.wv_rows[:, h, :], post.xnT[:, h // 2, :],
                                          start=True, stop=True)
                mm.then_inc(proj_done, 1)

            def tile(t, b, q):
                aggregate(t, b, q)
                if not early(t, 1):
                    project(t - 1)
            pairs(pe, tile)
            project(T - 1)


def attention(nc, m, adj, out_dram, name, first):
    TC = HEADS * NG
    TANH_AHEAD, SCORE_AHEAD, EXP_AHEAD = 15, 10, 6
    e = [m.at(8320 + 4096 * h, N) for h in range(HEADS)]
    adj_in = m.at(24704, N)
    off_edge = m.at(28800, N)
    eT = [m.at(49280 + GW * i, GROUP, P) for i in range(2)]
    turned = [m.banks[:, 2 * i:2 * i + 2, :].rearrange("p a (b i) -> p (a b) i", i=P) for i in range(3)]
    slot = [n % 3 for n in range(TC - 1)] + [1]
    agg = [m.banks[:, 6 + h % 2, (DH + 1) * (h // 2):(DH + 1) * (h // 2 + 1)] for h in range(HEADS)]
    xc = m.weights[:, 0:D]
    den = m.weights[:, D:D + 1]
    top = m.weights[:, D + 2:D + 3]
    tops = m.weights[:, D + 4:D + 4 + NG]
    f1_now = [m.small[:, 2 * P + 8 * b:2 * P + 8 * b + HEADS] for b in range(2)]
    neg_top_now = [m.small[:, 2 * P + 8 * b + 4:2 * P + 8 * b + 8] for b in range(2)]
    on_vector = [] if first else [n for n in range(TC) if n % 2 == 0]
    on_scalar = [n for n in range(TC) if n not in on_vector]

    spare = m.weights[:, D + 8:D + 9]
    adj_loaded = m.sems(name + "_adj_loaded", NG)
    spare_set = m.sem(name + "_spare_set")
    off_edge_built = m.sem(name + "_off_edge_built")
    masked = m.sem(name + "_masked")
    tanh_done = m.sem(name + "_tanh_done")
    scored = m.sem(name + "_scored")
    top_found = m.sem(name + "_top_found")
    top_joined = m.sem(name + "_top_joined")
    neg_top_built = m.sem(name + "_neg_top_built")
    neg_top_kept = m.sem(name + "_neg_top_kept")
    f1_fetched = m.sem(name + "_f1_fetched")
    exp_done = m.sem(name + "_exp_done")
    turn_done = m.sem(name + "_turn_done")
    copied_by_vector = m.sem(name + "_copied_by_vector")
    copied_by_scalar = m.sem(name + "_copied_by_scalar")
    used = m.sem(name + "_used")
    agg_read = m.sem(name + "_agg_read")
    stored = m.sem(name + "_stored")
    finish_step = m.sem(name + "_finish_step")

    def ahead(t, n, k):
        return t + (n + k) // TC, (n + k) % TC

    def exists(t):
        return not (isinstance(t, int) and (t < 0 or t >= T))

    def wait_copied(eng, t, n):
        if n in on_vector:
            eng.wait_ge(copied_by_vector, len(on_vector) * t + on_vector.index(n) + 1)
        else:
            eng.wait_ge(copied_by_scalar, len(on_scalar) * t + on_scalar.index(n) + 1)

    def columns(n):
        return slice(GW * (n % NG), GW * (n % NG + 1))

    def copy_out(eng, copy, sem, t, n):
        if not exists(t):
            return
        eng.wait_ge(turn_done, TC * t + n + 1)
        if not (early(t, 1) and n < 2):
            eng.wait_ge(used, TC * t + n - 1)
        copy(eT[n % 2], turned[slot[n]]).then_inc(sem, 1)

    with nc.Block() as block:
        @block.sync
        def _(sp):
            def store(t):
                sp.wait_ge(agg_read, HEADS * (t + 1))
                sp.dma_start(out_dram[t], xc).then_inc(stored, 16)

            def tile(t, b, q):
                if not early(t, 2):
                    store(t - 2)
                for c in range(NG):
                    if not early(t, 1):
                        sp.wait_ge(scored, TC * t - NG + c + 1)
                        sp.wait_ge(adj_loaded[c], 16)
                    sp.dma_start(adj_in[:, columns(c)], adj[t][:, columns(c)]).then_inc(adj_loaded[c], 16)
            pairs(sp, tile)
            store(T - 2)
            store(T - 1)
            sp.wait_ge(stored, 16 * T)

        @block.vector
        def _(dve):
            finish_steps = Steps(dve, finish_step, 2)

            def find_off_edge(t, c):
                dve.wait_ge(adj_loaded[c], 16 * (t + 1))
                if not early(t, 1):
                    if first:
                        dve.wait_ge(top_found, TC * t - NG + c + 1)
                    else:
                        dve.wait_ge(masked, NG * (t - 1) + c + 1)
                        dve.wait_ge(scored, TC * t - NG + c + 1)
                nc.vector.tensor_scalar(off_edge[:, columns(c)], adj_in[:, columns(c)], 0.0, MASKED,
                                        ALU.is_equal, ALU.mult).then_inc(off_edge_built, 1)

            def mask(t, c):
                dve.wait_ge(off_edge_built, NG * t + c + 1)
                piece = adj_in[:, columns(c)]
                nc.vector.tensor_tensor(piece, piece, off_edge[:, columns(c)], ALU.add).then_inc(masked, 1)

            def score(t, n):
                dve.wait_ge(tanh_done, TC * t + n + 1)
                if first:
                    dve.wait_ge(adj_loaded[n % NG], 16 * (t + 1))
                else:
                    dve.wait_ge(masked, NG * t + n % NG + 1)
                c = columns(n)
                nc.vector.scalar_tensor_tensor(e[n // NG][:, c], e[n // NG][:, c], TANH_ONE, adj_in[:, c],
                                               ALU.add, ALU.mult).then_inc(scored, 1)

            def find_top(t, n):
                if n % NG == 0 and not (early(t, 1) and n == 0):
                    dve.wait_ge(top_joined, HEADS * t + n // NG)
                dve.wait_ge(off_edge_built, NG * t + n % NG + 1)
                dve.wait_ge(scored, TC * t + n + 1)
                if not (early(t, 1) and n == 0):
                    dve.wait_ge(spare_set, TC * t + n)
                nc.vector.memset(spare, 0.0).then_inc(spare_set, 1)
                chunk = e[n // NG][:, columns(n)]
                nc.vector.tensor_tensor_reduce(chunk, chunk, off_edge[:, columns(n)], 1.0, MASKED, ALU.add,
                                               ALU.max, tops[:, n % NG:n % NG + 1]).then_inc(top_found, 1)

            def join_tops(t, b, h):
                dve.wait_ge(top_found, TC * t + NG * (h + 1))
                if not (early(t, 1) and h == 0):
                    dve.wait_ge(neg_top_built, HEADS * t + h)
                nc.vector.tensor_reduce(top, tops, AX_X, ALU.max).then_inc(top_joined, 1)
                dve.wait_ge(top_joined, HEADS * t + h + 1)
                if h == 0 and not early(t, 2):
                    dve.wait_ge(exp_done, TC * (t - 1))
                    dve.wait_ge(neg_top_kept, t - 1)
                nc.vector.tensor_scalar(neg_top_now[b][:, h:h + 1], top, -0.5, -MASKED * 1e-8, ALU.mult,
                                        ALU.min).then_inc(neg_top_built, 1)
                if h == HEADS - 1:
                    dve.wait_ge(neg_top_built, HEADS * (t + 1))
                    nc.vector.tensor_copy(m.neg_top[:, t, :], neg_top_now[b]).then_inc(neg_top_kept, 1)

            def fetch_neg_top(t, b):
                if not early(t, 2):
                    dve.wait_ge(exp_done, TC * (t - 1))
                nc.vector.tensor_copy(neg_top_now[b], m.neg_top[:, t, :]).then_inc(neg_top_built, 1)

            def finish(t, h):
                finish_steps.tile(HEADS * t + h)
                dve.wait_ge(used, TC * t + NG * (h + 1))
                if not (early(t, 1) and h == 0):
                    dve.wait_ge(agg_read, HEADS * t + h)
                finish_steps(nc.vector.tensor_scalar(den, agg[h][:, DH:DH + 1], 1e-30, None, ALU.max))
                finish_steps(nc.vector.reciprocal(den, den))
                if h == 0 and not early(t, 1):
                    dve.wait_ge(stored, 16 * t)
                nc.vector.tensor_scalar(xc[:, DH * h:DH * h + DH], agg[h][:, 0:DH], den, None,
                                        ALU.mult).then_inc(agg_read, 1)

            def find_tops(t, b, n):
                if not first:
                    if n == 0:
                        fetch_neg_top(t, b)
                    return
                if n % NG > 0:
                    find_top(t, n - 1)
                if n % NG == NG - 1:
                    find_top(t, n)
                    join_tops(t, b, n // NG)

            def step(t, b, q, n):
                turn_t, turn_n = ahead(t, n, 2)
                if turn_n in on_vector:
                    copy_out(dve, nc.vector.tensor_copy, copied_by_vector, turn_t, turn_n)
                c = n - (TC - SCORE_AHEAD - 1)
                masks = 0 <= c < NG and exists(t + 1)
                if masks:
                    find_off_edge(t + 1, c)
                score_t, score_n = ahead(t, n, SCORE_AHEAD)
                score_b = b if score_n > n else 1 - b
                if exists(score_t):
                    score(score_t, score_n)
                if masks and not first:
                    mask(t + 1, c)
                if exists(score_t):
                    find_tops(score_t, score_b, score_n)
                if n % NG == 1:
                    done_t, done_n = ahead(t, n, -NG)
                    if exists(done_t):
                        finish(done_t, done_n // NG)

            for c in range(NG):
                find_off_edge(0, c)
                if not first:
                    mask(0, c)
            for n in range(SCORE_AHEAD):
                score(0, n)
                find_tops(0, 0, n)
            for n in range(2):
                if n in on_vector:
                    copy_out(dve, nc.vector.tensor_copy, copied_by_vector, 0, n)

            def tile(t, b, q):
                for n in range(TC):
                    step(t, b, q, n)
            pairs(dve, tile)
            finish(T - 1, HEADS - 1)

        @block.scalar
        def _(act):
            def fetch_f1(t, b):
                if not early(t, 2):
                    act.wait_ge(tanh_done, TC * (t - 1))
                nc.scalar.copy(f1_now[b], m.f1[:, t, :]).then_inc(f1_fetched, 1)

            def both(n):
                return slice(GW * (n % NG), GW * (n % NG + 2))

            def tanh(t, b, n):
                if n == 0:
                    act.wait_ge(f1_fetched, t + 1)
                if not early(t, 1):
                    act.wait_ge(turn_done, TC * (t - 1) + n + 2)
                h, c = n // NG, both(n)
                nc.scalar.activation(e[h][:, c], m.f2[:, h, c], ACT.Tanh, bias=f1_now[b][:, h:h + 1],
                                     scale=0.5).then_inc(tanh_done, 2)

            def exp(t, b, n):
                h, c = n // NG, both(n)
                if first:
                    act.wait_ge(neg_top_built, HEADS * t + h + 1)
                elif n == 0:
                    act.wait_ge(neg_top_built, t + 1)
                act.wait_ge(scored, TC * t + n + 2)
                nc.scalar.activation(e[h][:, c], e[h][:, c], ACT.Exp, bias=neg_top_now[b][:, h:h + 1],
                                     scale=0.5).then_inc(exp_done, 2)

            def copy(t, n):
                if n in on_scalar:
                    copy_out(act, nc.scalar.copy, copied_by_scalar, t, n)

            fetch_f1(0, 0)
            for n in range(0, TANH_AHEAD, 2):
                tanh(0, 0, n)
            for n in range(0, EXP_AHEAD, 2):
                exp(0, 0, n)
            copy(0, 0)
            copy(0, 1)

            def tile(t, b, q):
                for n in range(TC):
                    copy(*ahead(t, n, 2))
                    if n == 0 and exists(t + 1):
                        fetch_f1(t + 1, 1 - b)
                    if n % 2 == 0:
                        exp_t, exp_n = ahead(t, n, EXP_AHEAD)
                        if exists(exp_t):
                            exp(exp_t, b if exp_n > n else 1 - b, exp_n)
                    else:
                        tanh_t, tanh_n = ahead(t, n, TANH_AHEAD)
                        if exists(tanh_t):
                            tanh(tanh_t, 1 - b, tanh_n)
            pairs(act, tile)

        @block.tensor
        def _(pe):
            def turn(t, n):
                if not exists(t):
                    return
                pe.wait_ge(exp_done, TC * t + n + 1)
                before = [k for k in range(n) if slot[k] == slot[n]]
                if before:
                    wait_copied(pe, t, before[-1])
                elif not early(t, 1):
                    wait_copied(pe, t - 1, max(k for k in range(TC) if slot[k] == slot[n]))
                for k in range(GROUP):
                    at = GW * (n % NG) + P * k
                    mm = nc.tensor.transpose(turned[slot[n]][:, k, :], e[n // NG][:, at:at + P], m.ident[:])
                mm.then_inc(turn_done, 1)

            def aggregate(t, n):
                h = n // NG
                if n % NG == 0 and not (early(t, 1) and h < 2):
                    pe.wait_ge(agg_read, HEADS * t + h - 1)
                wait_copied(pe, t, n)
                for k in range(GROUP):
                    j = GROUP * (n % NG) + k
                    mm = nc.tensor.matmul(agg[h], eT[n % 2][:, k, :], m.feats[:, j, h, :],
                                          start=(j == 0), stop=(j == T - 1))
                mm.then_inc(used, 1)

            turn(0, 0)
            turn(0, 1)

            def tile(t, b, q):
                for n in range(TC):
                    turn(*ahead(t, n, 2))
                    aggregate(t, n)
            pairs(pe, tile)

def turn_nodes(nc, m, name, src, dst, to_rows, load=None, extra=None, by_head=False):
    PER = BANK // P
    STEPS = KC * T // PER
    bank = [m.banks[:, i, :].rearrange("p (k i) -> p k i", k=PER) for i in range(8)]
    loaded = m.sems(name + "_loaded", 4)
    extra_loaded = m.sem(name + "_extra_loaded")
    turned = m.sem(name + "_turned")
    copied = m.sems(name + "_copied", 2)
    QT = T // 4

    def contents(k):
        if by_head:
            return m.banks[:, k % 8, :].rearrange("p (t h n) -> p t h n", h=HEADS, n=DH)
        return bank[k % 8]

    def blocks(k):
        if to_rows:
            t = k * PER // KC
            to = dst[:, t:t + PER // KC]
            to = to[:, :, :, 0:DH] if by_head else to.rearrange("p t (c i) -> p (t c) i", c=KC)
            return [(t + i // KC, i % KC) for i in range(PER)], to
        t, c = PER * (k // KC), k % KC
        return [(t + i, c) for i in range(PER)], dst[:, c, P * t:P * (t + PER)].rearrange(
            "p (k i) -> p k i", k=PER)

    with nc.Block() as block:
        @block.sync
        def _(sp):
            if load is not None:
                for i in range(4):
                    sp.dma_start(load[1][:, QT * i:QT * (i + 1), :],
                                 load[0][QT * i:QT * (i + 1)].rearrange("t p d -> p t d")).then_inc(loaded[i], 16)
            if extra is not None:
                sp.dma_start(extra[1], extra[0].rearrange("t p d -> p t d")).then_inc(extra_loaded, 16)
                sp.wait_ge(extra_loaded, 16)

        @block.tensor
        def _(pe):
            for k in range(STEPS):
                where, _ = blocks(k)
                if load is not None and k % (STEPS // 4) == 0:
                    pe.wait_ge(loaded[k // (STEPS // 4)], 16)
                if k >= 8:
                    pe.wait_ge(copied[k % 2], (k - 8) // 2 + 1)
                for i, (t, c) in enumerate(where):
                    block_in = src[:, c, P * t:P * t + P] if to_rows else src[:, t, P * c:P * c + P]
                    mm = nc.tensor.transpose(bank[k % 8][:, i, :], block_in, m.ident[:])
                mm.then_inc(turned, 1)

        @block.vector
        def _(dve):
            for k in range(0, STEPS, 2):
                dve.wait_ge(turned, k + 1)
                nc.vector.tensor_copy(blocks(k)[1], contents(k)).then_inc(copied[0], 1)
            dve.wait_ge(copied[0], STEPS // 2)

        @block.scalar
        def _(act):
            for k in range(1, STEPS, 2):
                act.wait_ge(turned, k + 1)
                nc.scalar.copy(blocks(k)[1], contents(k)).then_inc(copied[1], 1)
            act.wait_ge(copied[1], STEPS // 2)


def batch_norm(nc, m, name, data, gamma, beta):
    stats = m.weights[:, 0:KC * CH * 6].rearrange("p (c n k) -> p c n k", c=KC, n=CH)
    mv = m.weights[:, 100:100 + 2 * KC].rearrange("p (c k) -> p c k", c=KC)
    sd = m.weights[:, 110:110 + KC]
    scale = m.weights[:, 112:112 + KC]
    shift = m.weights[:, 114:114 + KC]
    measured = m.sem(name + "_measured")
    var_built = m.sem(name + "_var_built")
    sd_built = m.sem(name + "_sd_built")
    affine = m.sem(name + "_affine")
    applied = m.sem(name + "_applied")
    with nc.Block() as block:
        @block.vector
        def _(dve):
            for c in range(KC):
                for n in range(CH):
                    nc.vector.bn_stats(stats[:, c, n, :], data[:, c, BANK * n:BANK * (n + 1)]).then_inc(measured, 1)
            dve.wait_ge(measured, KC * CH)
            for c in range(KC):
                nc.vector.bn_aggr(mv[:, c, :], stats[:, c, :, :].rearrange("p n k -> p (n k)")).then_inc(
                    var_built, 1)
            dve.wait_ge(sd_built, 1)
            nc.vector.reciprocal(sd, sd).then_inc(affine, 1)
            dve.wait_ge(affine, 1)
            nc.vector.tensor_tensor(scale, sd, gamma, ALU.mult).then_inc(affine, 1)
            dve.wait_ge(affine, 2)
            dve.wait_ge(var_built, KC)
            nc.vector.tensor_tensor(shift, mv[:, :, 0], scale, ALU.mult).then_inc(affine, 1)
            dve.wait_ge(affine, 3)
            nc.vector.tensor_tensor(shift, beta, shift, ALU.subtract).then_inc(affine, 1)
            dve.wait_ge(affine, 4)
            nc.vector.tensor_scalar(data[:, 0, :], data[:, 0, :], scale[:, 0:1], shift[:, 0:1], ALU.mult,
                                    ALU.add).then_inc(applied, 1)

        @block.scalar
        def _(act):
            act.wait_ge(var_built, KC)
            nc.scalar.activation(sd, mv[:, :, 1], ACT.Sqrt, bias=m.eps[:, 1:2]).then_inc(sd_built, 1)
            act.wait_ge(affine, 4)
            nc.scalar.activation(data[:, 1, :], data[:, 1, :], ACT.Identity, bias=shift[:, 1:2],
                                 scale=scale[:, 1:2]).then_inc(applied, 1)
            act.wait_ge(applied, 2)


def dense(nc, m, name, src, dst, w_dram, bias, elu=False, residual=False, block_diagonal=False,
          scale=None, at=41088):
    w = m.weights[:, 0:KC * D].rearrange("p (c n) -> p c n", c=KC)
    low = [m.at(at + BANK * i, BANK) for i in range(2)]
    high = [m.at(at + 1024 + BANK * i, BANK) for i in range(2)]
    loaded = m.sem(name + "_loaded")
    multiplied = m.sem(name + "_multiplied")
    low_built = m.sem(name + "_low_built")
    low_exp = m.sem(name + "_low_exp")
    high_built = m.sem(name + "_high_built")
    joined = m.sem(name + "_joined")
    done = m.sem(name + "_done")
    steps = [(k // CH, slice(BANK * (k % CH), BANK * (k % CH + 1))) for k in range(KC * CH)]

    with nc.Block() as block:
        @block.sync
        def _(sp):
            sp.dma_start(w, w_dram.rearrange("c p n -> p c n")).then_inc(loaded, 16)

        @block.tensor
        def _(pe):
            pe.wait_ge(loaded, 16)
            for k, (o, nodes) in enumerate(steps):
                if k >= 4:
                    pe.wait_ge(high_built if elu else done, k - 3)
                chunks = [o] if block_diagonal else list(range(KC))
                for c in chunks:
                    mm = nc.tensor.matmul(m.banks[:, k % 4, :], w[:, c, P * o:P * o + P], src[:, c, nodes],
                                          start=(c == chunks[0]), stop=(c == chunks[-1]))
                mm.then_inc(multiplied, 1)

        @block.vector
        def _(dve):
            if elu:
                def join(k):
                    o, nodes = steps[k]
                    dve.wait_ge(low_exp, k + 1)
                    dve.wait_ge(high_built, k + 1)
                    to = high[k % 2] if residual else dst[:, o, nodes]
                    nc.vector.scalar_tensor_tensor(to, low[k % 2], -1.0, high[k % 2], ALU.add,
                                                   ALU.add).then_inc(joined, 1)
                    if residual:
                        dve.wait_ge(joined, k + 1)
                        nc.vector.tensor_tensor(dst[:, o, nodes], high[k % 2], src[:, o, nodes],
                                                ALU.add).then_inc(done, 1)

                for k, (o, nodes) in enumerate(steps):
                    dve.wait_ge(multiplied, k + 1)
                    if k >= 2:
                        dve.wait_ge(joined, k - 1)
                    b = 0.0 if bias is None else bias[:, o:o + 1]
                    nc.vector.tensor_scalar(low[k % 2], m.banks[:, k % 4, :], b, 0.0, ALU.add,
                                            ALU.min).then_inc(low_built, 1)
                    if k >= 1:
                        join(k - 1)
                join(len(steps) - 1)
                dve.wait_ge(done if residual else joined, len(steps))
            else:
                for k, (o, nodes) in enumerate(steps):
                    dve.wait_ge(multiplied, k + 1)
                    nc.vector.tensor_scalar(dst[:, o, nodes], m.banks[:, k % 4, :], bias[:, o:o + 1],
                                            1.0 if scale is None else scale, ALU.add, ALU.mult).then_inc(done, 1)
                dve.wait_ge(done, len(steps))

        @block.scalar
        def _(act):
            if elu:
                for k, (o, nodes) in enumerate(steps):
                    act.wait_ge(low_built, k + 1)
                    if k >= 2:
                        act.wait_ge(done if residual else joined, k - 1)
                    b = 0.0 if bias is None else bias[:, o:o + 1]
                    nc.scalar.activation(high[k % 2], m.banks[:, k % 4, :], ACT.Relu, bias=b).then_inc(
                        high_built, 1)
                    nc.scalar.activation(low[k % 2], low[k % 2], ACT.Exp).then_inc(low_exp, 1)
                act.wait_ge(low_exp, len(steps))


def layer_norm_rows(nc, m, rows, residual, x3_dram):
    stats = m.at(0, T, 6)
    mv = m.at(256, T, 2)
    sd = m.at(384, T)
    measured = m.sem("n3_measured")
    added = m.sem("n3_added")
    var_built = m.sem("n3_var_built")
    sd_built = m.sem("n3_sd_built")
    rs_built = m.sem("n3_rs_built")
    normalised = m.sem("n3_normalised")
    m.x3_stored = m.sem("n3_x3_stored")
    with nc.Block() as block:
        @block.vector
        def _(dve):
            nc.vector.tensor_tensor(rows, rows, residual, ALU.add).then_inc(added, 1)
            dve.wait_ge(added, 1)
            for t in range(T):
                nc.vector.bn_stats(stats[:, t, :], rows[:, t, :]).then_inc(measured, 1)
            dve.wait_ge(measured, T)
            for t in range(T):
                nc.vector.bn_aggr(mv[:, t, :], stats[:, t, :]).then_inc(var_built, 1)
            dve.wait_ge(sd_built, 1)
            nc.vector.reciprocal(sd, sd).then_inc(rs_built, 1)
            dve.wait_ge(rs_built, 1)
            dve.wait_ge(var_built, T)
            for t in range(T):
                nc.vector.tensor_scalar(rows[:, t, :], rows[:, t, :], mv[:, t, 0:1], sd[:, t:t + 1],
                                        ALU.subtract, ALU.mult).then_inc(normalised, 1)

        @block.scalar
        def _(act):
            act.wait_ge(var_built, T)
            nc.scalar.activation(sd, mv[:, :, 1], ACT.Sqrt, bias=m.eps[:, 0:1]).then_inc(sd_built, 1)

        @block.sync
        def _(sp):
            sp.wait_ge(normalised, T)
            sp.dma_start(x3_dram.rearrange("t p d -> p t d"), rows).then_inc(m.x3_stored, 16)


def values(nc, m, xT, w_dram, bv, v_rows):
    w = m.weights[:, 0:KC * D].rearrange("p (c n) -> p c n", c=KC)
    bias = m.at(41088, D)
    loaded = m.sem("v_loaded")
    multiplied = m.sem("v_multiplied")
    done = m.sem("v_done")
    with nc.Block() as block:
        @block.sync
        def _(sp):
            sp.dma_start(w, w_dram.rearrange("c p n -> p c n")).then_inc(loaded, 16)
            sp.dma_start(bias, bv.partition_broadcast(P)).then_inc(loaded, 16)
            sp.wait_ge(m.x3_stored, 16)

        @block.tensor
        def _(pe):
            pe.wait_ge(loaded, 32)
            for t in range(T):
                if t >= 8:
                    pe.wait_ge(done, t - 7)
                for c in range(KC):
                    mm = nc.tensor.matmul(m.banks[:, t % 8, 0:D], xT[:, c, P * t:P * t + P], w[:, c, :],
                                          start=(c == 0), stop=(c == KC - 1))
                mm.then_inc(multiplied, 1)

        @block.vector
        def _(dve):
            dve.wait_ge(loaded, 32)
            for t in range(T):
                dve.wait_ge(multiplied, t + 1)
                nc.vector.tensor_tensor(v_rows[:, t, :], m.banks[:, t % 8, 0:D], bias, ALU.add).then_inc(done, 1)
            dve.wait_ge(done, T)


def graph_ids(nc, m, ptr, q, q_dram, g_rows, g_cols):
    ptr_in = m.at(33000, NPTR).bitcast(I32)
    ptr_f = m.at(33100, NPTR)
    node = m.at(33200, T)
    at_most = m.at(33300, T, NPTR)
    spread = m.at(34400, T * P // 2).bitcast(BF16).rearrange("p (t i) -> p t i", t=T)
    loaded = m.sem("g_loaded")
    numbered = m.sem("g_numbered")
    step = m.sem("g_step")
    broadcast = m.sem("g_broadcast")
    copied = m.sem("g_copied")
    stored = m.sem("g_q_stored")
    with nc.Block() as block:
        @block.sync
        def _(sp):
            sp.dma_start(ptr_in, ptr.partition_broadcast(P)).then_inc(loaded, 16)
            for c in range(KC):
                sp.dma_start(q_dram.rearrange("t p c n -> c p t n")[c],
                             q[:, c, :].rearrange("p (t n) -> p t n", t=T)).then_inc(stored, 16)
            sp.wait_ge(stored, 16 * KC)

        @block.gpsimd
        def _(pool):
            nc.gpsimd.iota(node, pattern=[[P, T]], base=0, channel_multiplier=1,
                           allow_small_or_imprecise_dtypes=True).then_inc(numbered, 1)

        @block.vector
        def _(dve):
            dve.wait_ge(loaded, 16)
            nc.vector.tensor_copy(ptr_f, ptr_in).then_inc(step, 1)
            dve.wait_ge(step, 1)
            dve.wait_ge(numbered, 1)
            nc.vector.tensor_tensor(at_most, node.unsqueeze(2).to_broadcast([P, T, NPTR]),
                                    ptr_f.unsqueeze(1).to_broadcast([P, T, NPTR]), ALU.is_ge).then_inc(step, 1)
            dve.wait_ge(step, 2)
            nc.vector.tensor_reduce(g_cols, at_most, AX_X, ALU.add).then_inc(step, 1)
            dve.wait_ge(step, 3)
            nc.vector.tensor_tensor(spread, m.ident[:].unsqueeze(1).to_broadcast([P, T, P]),
                                    g_cols.unsqueeze(2).to_broadcast([P, T, P]), ALU.mult).then_inc(step, 1)
            for n in range(CH):
                dve.wait_ge(broadcast, n + 1)
                nc.vector.tensor_copy(g_rows[:, BANK * n:BANK * (n + 1)], m.banks[:, n, :]).then_inc(copied, 1)
            dve.wait_ge(copied, CH)

        @block.tensor
        def _(pe):
            pe.wait_ge(step, 4)
            for n in range(CH):
                nc.tensor.matmul(m.banks[:, n, :], m.ones_bf[:], spread[:, 4 * n:4 * n + 4, :],
                                 start=True, stop=True).then_inc(broadcast, 1)


def needed_groups(nc, m, g_rows):
    first = m.at(36600, T, NG)
    last = m.at(36800, T, NG)
    step = m.sem("need_step")
    tile_first, tile_last = (g_rows.rearrange("p (t i) -> p t i", t=T)[:, :, i:i + 1].to_broadcast([P, T, NG])
                             for i in (0, P - 1))
    group_first, group_last = (g_rows.rearrange("p (c i) -> p i c", c=NG)[:, i:i + 1, :].to_broadcast([P, T, NG])
                               for i in (0, GW - 1))
    with nc.Block() as block:
        @block.vector
        def _(dve):
            nc.vector.tensor_tensor(first, group_last, tile_first, ALU.is_ge).then_inc(step, 1)
            nc.vector.tensor_tensor(last, tile_last, group_first, ALU.is_ge).then_inc(step, 1)
            nc.vector.memset(m.zeros, 0.0).then_inc(step, 1)
            nc.vector.memset(m.off_graph, 2.0 * OFF_GRAPH).then_inc(step, 1)
            dve.wait_ge(step, 4)
            nc.vector.tensor_tensor(first, first, last, ALU.mult).then_inc(step, 1)
            dve.wait_ge(step, 5)
            nc.vector.tensor_copy(m.need, first).then_inc(step, 1)
            dve.wait_ge(step, 6)


def layer3(nc, m, adj, q_dram, x3_dram, kT, v_rows, g_rows, out):
    s = [m.at(start, N) for start in (16512, 16512 + N, 32896, 32896 + N)]
    factor = m.at(12416, GW)
    off_graph = m.off_graph.to_broadcast([P, GW])
    eT = [m.at(41088 + GW * i, GROUP, P) for i in range(2)]
    q_in = [m.at(43136 + D * b, KC, P) for b in range(2)]
    x3_in = [m.at(43648 + D * b, D) for b in range(2)]
    top = m.at(44160, 1)
    tops = m.at(44164, NG)
    rden = m.at(44168, 1)
    neg_top = [m.at(44172 + b, 1) for b in range(2)]
    post = Post(m, 44200, m.banks[:, 7, 0:D], "l3")
    in_graph_qk = m.at(49500, GW)
    row_sums = m.small[:, P:2 * P].rearrange("p (t c) -> p t c", t=T)
    qk = [m.banks[:, 2 * i:2 * i + 2, :].rearrange("p a n -> p (a n)") for i in range(2)]
    turned = m.banks[:, 4:6, :].rearrange("p a (b i) -> p (a b) i", i=P)
    agg = [m.banks[:, 6 + b, 0:D] for b in range(2)]

    adj_loaded = m.sems("l3_adj_loaded", 4)
    q_loaded = m.sems("l3_q_loaded", 2)
    x3_loaded = m.sems("l3_x3_loaded", 2)
    plain_step = m.sem("l3_plain_step")
    qk_done = m.sem("l3_qk_done")
    qk_read = m.sem("l3_qk_read")
    top_found = m.sem("l3_top_found")
    top_joined = m.sem("l3_top_joined")
    neg_top_built = m.sem("l3_neg_top_built")
    exp_done = m.sem("l3_exp_done")
    masked = m.sem("l3_masked")
    turn_done = m.sem("l3_turn_done")
    copied = m.sem("l3_copied")
    used = m.sem("l3_used")
    agg_opened = m.sem("l3_agg_opened")
    agg_closed = m.sem("l3_agg_closed")
    post_step = m.sem("l3_post_step")
    stored = m.sem("l3_stored")

    def nodes(c):
        return slice(GW * c, GW * (c + 1))

    def exists(t):
        return not (isinstance(t, int) and (t < 0 or t >= T))

    def fetch_need(eng, regs, t):
        eng.reg_load(regs, m.need[0:1, t, :])

    def pass_by(eng, sem, t, c):
        if not (early(t, 1) and c == 0):
            eng.wait_ge(sem, NG * t + c)
        eng.sem_inc(sem, 1)

    with nc.Block() as block:
        @block.sync
        def _(sp):
            def load_adj(t, b, q):
                if not early(t, 4):
                    sp.wait_ge(turn_done, NG * (t - 3))
                sp.dma_start(s[b], adj[t]).then_inc(adj_loaded[b], 16)

            def load_q(t, b):
                if not early(t, 2):
                    sp.wait_ge(qk_done, NG * (t - 1))
                sp.dma_start(q_in[b % 2], q_dram[t]).then_inc(q_loaded[b % 2], 16)

            def load_x3(t, b):
                if not early(t, 2):
                    sp.wait_ge(post.normalised, t - 1)
                sp.dma_start(x3_in[b % 2], x3_dram[t]).then_inc(x3_loaded[b % 2], 16)

            load_adj(0, 0, 0)
            load_q(0, 0)
            load_adj(1, 1, 0)
            load_q(1, 1)
            load_adj(2, 2, 0)

            def tile(t, b, q):
                if exists(t + 2):
                    load_q(t + 2, b + 2)
                if exists(t + 3):
                    load_adj(t + 3, (b + 3) % 4, q + (b + 3) // 4)
                load_x3(t, b)
            quads(sp, tile)

        @block.vector
        def _(dve):
            post_steps = Steps(dve, post_step, 4)
            need = [[dve.alloc_register(f"l3_vector_need{b}_{c}") for c in range(NG)] for b in range(2)]

            def score(t, b, q, groups):
                if groups[0] == 0:
                    fetch_need(dve, need[b % 2], t)
                g = m.g_cols.unsqueeze(2)[:, t, :]
                for c in groups:
                    piece, ids = s[b][:, nodes(c)], g_rows[:, nodes(c)]

                    def wait_for_inputs():
                        dve.wait_ge(adj_loaded[b], 16 * (q + 1))
                        if not early(t, 1):
                            dve.wait_ge(top_joined, t)
                        if not (early(t, 1) and c == 0):
                            dve.wait_ge(top_found, NG * t + c)
                    with dve.If_ne(need[b % 2][c], 0):
                        wait_for_inputs()
                        nc.vector.tensor_scalar(factor, ids, g, 2.0 - 2.0 * OFF_GRAPH, ALU.is_equal,
                                                ALU.mult).then_inc(plain_step, 1)
                        dve.wait_ge(plain_step, 2 * (NG * t + c) + 1)
                        nc.vector.scalar_tensor_tensor(piece, factor, 2.0 * OFF_GRAPH, piece, ALU.add,
                                                       ALU.mult).then_inc(plain_step, 1)
                        dve.wait_ge(qk_done, NG * t + c + 1)
                        nc.vector.scalar_tensor_tensor(in_graph_qk, ids, g, qk[c % 2], ALU.is_equal,
                                                       ALU.mult).then_inc(qk_read, 1)
                        dve.wait_ge(plain_step, 2 * (NG * t + c) + 2)
                        dve.wait_ge(qk_read, NG * t + c + 1)
                        nc.vector.memset(post.spare, 0.0)
                        nc.vector.tensor_tensor_reduce(piece, piece, in_graph_qk, 1.0, -3.0e38, ALU.add,
                                                       ALU.max, tops[:, c:c + 1]).then_inc(top_found, 1)
                    with dve.Else():
                        wait_for_inputs()
                        nc.vector.memset(post.spare, 0.0)
                        nc.vector.tensor_tensor_reduce(piece, piece, off_graph, 1.0, -3.0e38, ALU.mult,
                                                       ALU.max, tops[:, c:c + 1]).then_inc(top_found, 1)
                        pass_by(dve, qk_read, t, c)
                        if not (early(t, 1) and c == 0):
                            dve.wait_ge(plain_step, 2 * (NG * t + c))
                        dve.sem_inc(plain_step, 2)
                if groups[-1] == NG - 1:
                    join_tops(t, b)

            def join_tops(t, b):
                dve.wait_ge(top_found, NG * (t + 1))
                if not early(t, 1):
                    dve.wait_ge(neg_top_built, t)
                nc.vector.tensor_reduce(top, tops, AX_X, ALU.max).then_inc(top_joined, 1)
                dve.wait_ge(top_joined, t + 1)
                if not early(t, 2):
                    dve.wait_ge(exp_done, NG * (t - 1))
                nc.vector.tensor_scalar(neg_top[b % 2], top, -1.0, None, ALU.mult).then_inc(neg_top_built, 1)

            def mask(t, b, groups):
                g = m.g_cols.unsqueeze(2)[:, t, :]
                for c in groups:
                    with dve.If_ne(need[b % 2][c], 0):
                        dve.wait_ge(exp_done, NG * t + c + 1)
                        nc.vector.scalar_tensor_tensor(s[b][:, nodes(c)], g_rows[:, nodes(c)], g,
                                                       s[b][:, nodes(c)], ALU.is_equal,
                                                       ALU.mult).then_inc(masked, 1)
                    with dve.Else():
                        pass_by(dve, masked, t, c)

            def finish(t, b, pair):
                post_steps.tile(t)
                dve.wait_ge(agg_closed, t + 1)
                dve.wait_ge(x3_loaded[b % 2], 16 * (pair + 1))
                if not early(t, 1):
                    dve.wait_ge(post.normalised, t)
                post_steps(nc.vector.tensor_reduce(rden, row_sums[:, t, :], AX_X, ALU.add))
                post_steps(nc.vector.reciprocal(rden, rden))
                post_steps(nc.vector.scalar_tensor_tensor(post.pre, agg[b % 2], rden, x3_in[b % 2], ALU.mult,
                                                          ALU.add))
                if not early(t, 1):
                    dve.wait_ge(stored, 16 * t)
                post.normalise(nc, dve, post_steps, t, used=stored)

            score(0, 0, 0, range(NG))
            score(1, 1, 0, range(NG))
            mask(0, 0, range(NG))

            def tile(t, b, q):
                for c in range(NG):
                    if exists(t + 1):
                        mask(t + 1, (b + 1) % 4, [c])
                    if exists(t + 2):
                        score(t + 2, (b + 2) % 4, q + (b + 2) // 4, [c])
                    if c == 1 and not early(t, 1):
                        finish(t - 1, (b + 3) % 4, 2 * q + (b - 1) // 2)
            quads(dve, tile)
            finish(T - 1, 3, T // 2 - 1)

        @block.scalar
        def _(act):
            need = [act.alloc_register(f"l3_scalar_need{c}") for c in range(NG)]

            def exp(t, b, c):
                act.wait_ge(neg_top_built, t + 1)
                nc.scalar.activation(s[b][:, nodes(c)], s[b][:, nodes(c)], ACT.Exp, bias=neg_top[b % 2],
                                     accum_out=row_sums[:, t, c:c + 1]).then_inc(exp_done, 1)

            def store(t):
                act.wait_ge(post.normalised, t + 1)
                act.dma_start(out[t], post.xn).then_inc(stored, 16)

            for c in range(NG):
                exp(0, 0, c)

            def tile(t, b, q):
                fetch_need(act, need, t)
                for c in range(NG):
                    with act.If_ne(need[c], 0):
                        act.wait_ge(turn_done, NG * t + c + 1)
                        if not (early(t, 1) and c < 2):
                            act.wait_ge(used, NG * t + c - 1)
                        nc.scalar.copy(eT[c % 2], turned).then_inc(copied, 1)
                    with act.Else():
                        pass_by(act, copied, t, c)
                    if exists(t + 1):
                        exp(t + 1, (b + 1) % 4, c)
                if not early(t, 1):
                    store(t - 1)
            quads(act, tile)
            store(T - 1)
            act.wait_ge(stored, 16 * T)

        @block.gpsimd
        def _(pool):
            pairs(pool, lambda t, b, q: post.deviation(nc, pool, t))

        @block.tensor
        def _(pe):
            need = [[pe.alloc_register(f"l3_tensor_need{b}_{c}") for c in range(NG)] for b in range(4)]

            def scores(t, b, pair, c):
                with pe.If_ne(need[b][c], 0):
                    pe.wait_ge(q_loaded[b % 2], 16 * (pair + 1))
                    if not (early(t, 1) and c < 2):
                        pe.wait_ge(qk_read, NG * t + c - 1)
                    for half in range(2):
                        for k in range(KC):
                            n = GW * c + BANK * half
                            mm = nc.tensor.matmul(qk[c % 2][:, BANK * half:BANK * (half + 1)],
                                                  q_in[b % 2][:, k, :], kT[:, k, n:n + BANK],
                                                  start=(k == 0), stop=(k == KC - 1))
                    mm.then_inc(qk_done, 1)
                with pe.Else():
                    pass_by(pe, qk_done, t, c)

            def turn(t, b, c):
                pe.wait_ge(masked, NG * t + c + 1)
                if not (early(t, 1) and c == 0):
                    pe.wait_ge(copied, NG * t + c)
                for k in range(GROUP):
                    j = GROUP * c + k
                    mm = nc.tensor.transpose(turned[:, k, :], s[b][:, P * j:P * j + P], m.ident[:])
                mm.then_inc(turn_done, 1)

            def aggregate(t, b, c):
                pe.wait_ge(copied, NG * t + c + 1)
                for k in range(GROUP):
                    mm = nc.tensor.matmul(agg[b % 2], eT[c % 2][:, k, :], v_rows[:, GROUP * c + k, :],
                                          start=False, stop=False)
                mm.then_inc(used, 1)

            for t in range(2):
                fetch_need(pe, need[t], t)
                for c in range(NG):
                    scores(t, t, 0, c)

            def tile(t, b, q):
                if exists(t + 2):
                    fetch_need(pe, need[(b + 2) % 4], t + 2)
                def scores_ahead(c):
                    if exists(t + 2):
                        scores(t + 2, (b + 2) % 4, 2 * q + (b + 2) // 2, c)

                if not early(t, 2):
                    pe.wait_ge(post_step, 4 * (t - 2) + 3)
                nc.tensor.matmul(agg[b % 2], m.zeros[:, 0:P], m.zeros, start=True, stop=False).then_inc(
                    agg_opened, 1)
                for c in range(NG):
                    with pe.If_ne(need[b][c], 0):
                        turn(t, b, c)
                        scores_ahead(c)
                        aggregate(t, b, c)
                    with pe.Else():
                        pass_by(pe, turn_done, t, c)
                        pass_by(pe, used, t, c)
                        scores_ahead(c)
                nc.tensor.matmul(agg[b % 2], m.zeros[:, 0:P], m.zeros, start=False, stop=True).then_inc(
                    agg_closed, 1)
            quads(pe, tile)

PARAMS = ["enc_bn_gamma", "enc_bn_beta", "enc_mlp_b", "enc_mlp_bn_gamma", "enc_mlp_bn_beta",
          "dec_mlp_b", "dec_mlp_bn_gamma", "dec_mlp_bn_beta", "bq", "bk"]


def program(nc, x, adj, adjT_blocks, w1, b1, wbd, wbdT, vbd, params, w_enc, w_dec, wq, wk, wv, wdec_head,
            bv, ptr, out):
    def scratch(name, *shape):
        return nc.dram_tensor(name, shape, F32).ap()
    x2_dram = scratch("x2_scratch", T, P, D)
    xc_dram = scratch("xc_scratch", T, P, D)
    x3_dram = scratch("x3_scratch", T, P, D)
    q_dram = scratch("q_scratch", T, P, KC, P)
    with ExitStack() as ctx:
        m = Memory(nc, ctx)
        m.h = m.at(8320, T, D)
        m.x1 = m.at(16512, T, D)
        m.feats = m.at(0, T, HEADS, DH + 1)
        m.values = m.at(0, T, D)
        m.f2 = m.at(32896, HEADS, N)
        m.f1 = m.small[:, 0:P].rearrange("p (t h) -> p t h", t=T)
        m.neg_top = m.small[:, P:2 * P].rearrange("p (t h) -> p t h", t=T)
        m.g_cols = m.small[:, 0:T]
        m.need = m.small[:, 2 * P:3 * P].bitcast(I32).rearrange("p (t c) -> p t c", t=T)
        m.zeros = m.weights[:, 0:D]
        m.off_graph = m.weights[:, D:D + 1]
        m.wext = m.weights[:, 0:KC * (P + 4)].rearrange("p (c n) -> p c n", c=KC)
        m.wv_rows = m.weights[:, KC * (P + 4):KC * (P + 4) + HEADS * P].rearrange("p (h n) -> p h n", h=HEADS)
        param = {k: m.params[:, KC * i:KC * (i + 1)] for i, k in enumerate(PARAMS)}
        rows = lambda start: m.at(start, T, D)
        cols = lambda start: m.at(start, KC, N)
        A, B, C, E = 8320, 16512, 24704, 32896

        constants(nc, m, params)
        layer0(nc, m, x, adjT_blocks, w1)
        layer2_weights(nc, m, wbd, wbdT, vbd)
        layer1(nc, m, adjT_blocks, b1, x2_dram)

        m.clear_semaphores()
        attention(nc, m, adj, xc_dram, "a1", True)
        turn_nodes(nc, m, "t1", rows(A), cols(B), False, load=(xc_dram, rows(A)))
        batch_norm(nc, m, "n1", cols(B), param["enc_bn_gamma"], param["enc_bn_beta"])
        dense(nc, m, "d1", cols(B), cols(C), w_enc, param["enc_mlp_b"], elu=True, residual=True, at=A)
        batch_norm(nc, m, "n2", cols(C), param["enc_mlp_bn_gamma"], param["enc_mlp_bn_beta"])
        turn_nodes(nc, m, "t2", cols(C), m.feats, True, by_head=True)

        m.clear_semaphores()
        attention(nc, m, adj, xc_dram, "a2", False)
        turn_nodes(nc, m, "t3", rows(A), cols(B), False, load=(xc_dram, rows(A)), extra=(x2_dram, rows(E)))
        dense(nc, m, "d2", cols(B), cols(C), wdec_head, None, elu=True, block_diagonal=True)
        dense(nc, m, "d3", cols(C), cols(B), w_dec, param["dec_mlp_b"], elu=True, residual=True)
        batch_norm(nc, m, "n4", cols(B), param["dec_mlp_bn_gamma"], param["dec_mlp_bn_beta"])
        turn_nodes(nc, m, "t4", cols(B), rows(A), True)
        layer_norm_rows(nc, m, rows(A), rows(E), x3_dram)

        turn_nodes(nc, m, "t5", rows(A), cols(B), False)
        values(nc, m, cols(B), wv, bv, m.values)
        dense(nc, m, "d4", cols(B), cols(C), wk, param["bk"])
        dense(nc, m, "d5", cols(B), cols(A), wq, param["bq"], scale=1.0 / 16)
        g_rows = m.at(45400, N)
        graph_ids(nc, m, ptr, cols(A), q_dram, g_rows, m.g_cols)
        needed_groups(nc, m, g_rows)
        m.clear_semaphores()
        layer3(nc, m, adj, q_dram, x3_dram, cols(C), m.values, g_rows, out)


def kernel(**inputs):
    import numpy as np
    import concourse.bacc as bacc
    from concourse import mybir as mb
    from concourse.bass_utils import run_bass_kernel_spmd as run

    g = {k: np.asarray(v) for k, v in inputs.items()}
    adj = g["adj"]

    def block_diagonal(a):
        n = a.shape[2]
        o = np.zeros((KC, P, 2 * n), a.dtype)
        for h in range(HEADS):
            o[h // 2, DH * (h % 2):DH * (h % 2) + DH, n * (h % 2):n * (h % 2) + n] = a[h]
        return o

    v = block_diagonal(g["L2_gnn_V"][..., 0].transpose(0, 2, 1))
    params = np.stack([g["L3_gnn_" + k if k in ("bq", "bk") else "L2_gnn_" + k] for k in PARAMS])
    head_out = np.zeros((KC, P, D), adj.dtype)
    wT = block_diagonal(g["L2_gnn_W"].transpose(0, 2, 1))
    for c in range(KC):
        head_out[c, :, P * c:P * c + P] = wT[c]
    arrays = {
        "x": g["x"],
        "adj": adj.reshape(T, P, N),
        "adjT_blocks": adj.reshape(T, P, T, P).transpose(0, 3, 2, 1).reshape(T, P, N),
        "w1": g["L1_gnn_W"].transpose(1, 0, 2).reshape(D, D),
        "b1": g["L1_gnn_b"].reshape(D),
        "wbd": block_diagonal(g["L2_gnn_W"]),
        "wbdT": wT,
        "vbd": v[:, :, [0, 2, 1, 3]],
        "params": params.reshape(-1, P).T,
        "w_enc": g["L2_gnn_enc_mlp_W"].T.reshape(KC, P, D),
        "w_dec": g["L2_gnn_dec_mlp_W"].T.reshape(KC, P, D),
        "wq": g["L3_gnn_Wq"].T.reshape(KC, P, D),
        "wk": g["L3_gnn_Wk"].T.reshape(KC, P, D),
        "wv": g["L3_gnn_Wv"].T.reshape(KC, P, D),
        "w_head_out": head_out,
        "bv": g["L3_gnn_bv"],
        "ptr": g["L3_gnn_ptr"],
    }
    nc = bacc.Bacc("TRN2", target_bir_lowering=False, num_devices=1)
    maps, args = {}, []
    for name, a in arrays.items():
        maps[f"in_{name}"] = np.ascontiguousarray(a)
        args.append(nc.dram_tensor(f"in_{name}", a.shape, mb.dt.from_np(a.dtype), kind="ExternalInput").ap())
    args.append(nc.dram_tensor("out_dram", (T, P, D), mb.dt.float32, kind="ExternalOutput").ap())
    program(nc, *args)
    return run(nc, [maps], core_ids=[0]).results[0]["out_dram"].reshape(N, D)
```
